# Optimizing a Trainium2 kernel written in Bass

```python
import numpy as np
import jax
import jax.numpy as jnp

def _softmax(x, axis=-1):
    return jax.nn.softmax(x, axis=axis)

def _gelu(x):
    return jax.nn.gelu(x, approximate=True)

def _silu(x):
    return jax.nn.silu(x)

def _sigmoid(x):
    return jax.nn.sigmoid(x)

def _layernorm(x, axis=-1, eps=1e-05):
    m = jnp.mean(x, axis=axis, keepdims=True)
    v = jnp.var(x, axis=axis, keepdims=True)
    return (x - m) / jnp.sqrt(v + eps)

def _scatter_add(tgt, idx, src, axis=0):
    return tgt.at[idx].add(src)

def _segment_sum(src, seg, n):
    return jax.ops.segment_sum(src, seg, n)
kernel_name = 'mk_decoder_preln_d2_seqx_r4_7cac3d'

def setup_inputs(seed: int=0):
    np.random.seed(seed)
    _w = jnp.asarray

    def _rec_inputs():
        import jax
        import jax.numpy as jnp
        _rk = jax.random.key(seed)
        x = 7.22e-05 + 1 * jax.random.normal(jax.random.fold_in(_rk, 1), (2, 1024, 256), jnp.float32)
        _lenS = 1024 - jax.random.randint(jax.random.fold_in(_rk, 7), (2,), 0, max(1, 1024 // 4) + 1, jnp.int32)
        _lenS2 = 77 - jax.random.randint(jax.random.fold_in(_rk, 8), (2,), 0, max(1, 77 // 4) + 1, jnp.int32)
        _ctx_1024P = jax.random.normal(jax.random.fold_in(_rk, 11), (2, 16, 256), jnp.float32)
        _ctx_1024c = jax.random.dirichlet(jax.random.fold_in(_rk, 511), 0.3 * jnp.ones((16,), jnp.float32), (2, 77))
        _ctx_1024t = jnp.einsum('bsk,bkd->bsd', _ctx_1024c, _ctx_1024P)
        _ctx_1024t = _ctx_1024t * jax.lax.rsqrt(jnp.mean(jnp.square(_ctx_1024t)) + 1e-12) * 0.953939
        ctx_1024 = 4.13588e-05 + 0.999923 * (_ctx_1024t + 0.3 * jax.random.normal(jax.random.fold_in(_rk, 611), (2, 77, 256), jnp.float32))
        fside_BxSxS2_0 = jax.random.uniform(jax.random.fold_in(_rk, 12), (2, 1024, 77), jnp.float32, 0.0, 10)
        return (x, ctx_1024, fside_BxSxS2_0)
    x, ctx_1024, fside_BxSxS2_0 = _rec_inputs()

    def _L0_attn_setup():
        import jax, jax.numpy as jnp
        from jax import lax
        import numpy as np
        BATCH, SEQ = (2, 512)
        D_MODEL, D_STATE, D_CONV = (256, 16, 4)
        D_INNER = 2 * D_MODEL
        DT_RANK = D_MODEL // 16
        DT_MIN, DT_MAX = (0.001, 0.1)

        def _mamba_fwd(hidden_states, in_proj_w, conv_w, conv_b, x_proj_w, dt_proj_w, dt_proj_b, A_log, D, out_proj_w):
            silu = jax.nn.silu
            b, l, _ = hidden_states.shape
            xz = hidden_states @ in_proj_w.T
            x, z = jnp.split(xz, 2, axis=-1)
            xc = jnp.transpose(x, (0, 2, 1))
            xc = lax.conv_general_dilated(xc, conv_w, window_strides=(1,), padding=[(D_CONV - 1, 0)], feature_group_count=D_INNER, dimension_numbers=('NCH', 'OIH', 'NCH')) + conv_b[None, :, None]
            x = silu(jnp.transpose(xc, (0, 2, 1)))
            A = -jnp.exp(A_log)
            xp = x @ x_proj_w.T
            dt, Bm, C = jnp.split(xp, [DT_RANK, DT_RANK + D_STATE], axis=-1)
            dt = jax.nn.softplus(dt @ dt_proj_w.T + dt_proj_b)

            def step(h, ins):
                dt_t, B_t, C_t, x_t = ins
                dA = jnp.exp(dt_t[:, :, None] * A)
                h = dA * h + dt_t[:, :, None] * B_t[:, None, :] * x_t[:, :, None]
                y = jnp.einsum('bdn,bn->bd', h, C_t)
                return (h, y)
            h0 = jnp.zeros((b, D_INNER, D_STATE), hidden_states.dtype)
            xs = (jnp.transpose(dt, (1, 0, 2)), jnp.transpose(Bm, (1, 0, 2)), jnp.transpose(C, (1, 0, 2)), jnp.transpose(x, (1, 0, 2)))
            _, ys = lax.scan(step, h0, xs)
            y = jnp.transpose(ys, (1, 0, 2)) + x * D
            return y * silu(z) @ out_proj_w.T
        key = jax.random.key(seed)
        ks = jax.random.split(key, 8)
        s = 0.02
        dt = jnp.exp(jax.random.uniform(ks[0], (D_INNER,)) * (np.log(DT_MAX) - np.log(DT_MIN)) + np.log(DT_MIN))
        dt = jnp.clip(dt, 0.0001, None)
        inv_dt = dt + jnp.log(-jnp.expm1(-dt))
        dt_std = DT_RANK ** (-0.5)
        return {'hidden_states': jax.random.normal(ks[1], (BATCH, SEQ, D_MODEL), jnp.float32), 'in_proj_w': jax.random.normal(ks[2], (2 * D_INNER, D_MODEL), jnp.float32) * s, 'conv_w': jax.random.normal(ks[3], (D_INNER, 1, D_CONV), jnp.float32) * s, 'conv_b': jnp.zeros((D_INNER,), jnp.float32), 'x_proj_w': jax.random.normal(ks[4], (DT_RANK + 2 * D_STATE, D_INNER), jnp.float32) * s, 'dt_proj_w': jax.random.uniform(ks[5], (D_INNER, DT_RANK), jnp.float32, -dt_std, dt_std), 'dt_proj_b': inv_dt, 'A_log': jnp.log(jnp.tile(jnp.arange(1, D_STATE + 1, dtype=jnp.float32), (D_INNER, 1))), 'D': jnp.ones((D_INNER,), jnp.float32), 'out_proj_w': jax.random.normal(ks[6], (D_MODEL, D_INNER), jnp.float32) * s}
    _L0_attn_all = _L0_attn_setup()
    _L0_attn_in = {k: v for k, v in _L0_attn_all.items() if k in ('in_proj_w', 'conv_w', 'conv_b', 'x_proj_w', 'dt_proj_w', 'dt_proj_b', 'A_log', 'D', 'out_proj_w')}
    del _L0_attn_all

    def _L0_xattn_setup():
        import jax, jax.numpy as jnp
        import numpy as np
        EMBED_DIM = 256
        NUM_HEADS = 16
        HEAD_DIM = EMBED_DIM // NUM_HEADS
        B, SQ, SK = (4, 512, 512)

        def _xavier(key, shape):
            fan_in, fan_out = (shape[1], shape[0])
            limit = float(np.sqrt(6.0 / (fan_in + fan_out)))
            return jax.random.uniform(key, shape, jnp.float32, -limit, limit)
        key = jax.random.key(seed)
        ks = jax.random.split(key, 9)
        return {'query': jax.random.normal(ks[0], (B, SQ, EMBED_DIM), jnp.float32), 'key_': jax.random.normal(ks[1], (B, SK, EMBED_DIM), jnp.float32), 'value': jax.random.normal(ks[2], (B, SK, EMBED_DIM), jnp.float32), 'distances': jax.random.uniform(ks[3], (B, SQ, SK), jnp.float32, 0.01, 10.0), 'Wq': _xavier(ks[4], (EMBED_DIM, EMBED_DIM)), 'bq': jnp.zeros((EMBED_DIM,), jnp.float32), 'Wk': _xavier(ks[5], (EMBED_DIM, EMBED_DIM)), 'bk': jnp.zeros((EMBED_DIM,), jnp.float32), 'Wv': _xavier(ks[6], (EMBED_DIM, EMBED_DIM)), 'bv': jnp.zeros((EMBED_DIM,), jnp.float32), 'Wo': _xavier(ks[7], (EMBED_DIM, EMBED_DIM)), 'bo': jnp.zeros((EMBED_DIM,), jnp.float32), 'distance_scaling': jnp.asarray(1.0, jnp.float32)}
    _L0_xattn_all = _L0_xattn_setup()
    _L0_xattn_in = {k: v for k, v in _L0_xattn_all.items() if k in ('Wq', 'bq', 'Wk', 'bk', 'Wv', 'bv', 'Wo', 'bo', 'distance_scaling')}
    del _L0_xattn_all

    def _L0_ffn_setup():
        import jax, jax.numpy as jnp
        import numpy as np
        CAPACITY_FACTOR = 1.0

        def _top1_gate(x2d, wg):
            S, _ = x2d.shape
            E = wg.shape[1]
            C = int(CAPACITY_FACTOR * S / E)
            logits = x2d @ wg
            gates = jax.nn.softmax(logits, axis=-1)
            idx = jnp.argmax(gates, axis=-1)
            mask = jax.nn.one_hot(idx, E, dtype=jnp.int32)
            loc = jnp.cumsum(mask, axis=0) - 1
            me = jnp.mean(gates, axis=0)
            ce = jnp.mean(mask.astype(gates.dtype), axis=0)
            l_aux = E * jnp.sum(me * ce)
            mask = mask * (loc < C).astype(jnp.int32)
            gate_s = jnp.sum(gates * mask, axis=-1)
            loc_s = jnp.sum(loc * mask, axis=-1)
            loc_oh = jax.nn.one_hot(loc_s, C, dtype=gates.dtype)
            combine = (gate_s[:, None] * mask.astype(gates.dtype))[:, :, None] * loc_oh[:, None, :]
            dispatch = (combine > 0).astype(gates.dtype)
            return (l_aux, combine, dispatch)
        key = jax.random.key(seed)
        k1, k2, k3, k4 = jax.random.split(key, 4)
        s, b, m, E, ffn = (512, 4, 256, 8, 1024)
        x = jax.random.normal(k1, (s, b, m), dtype=jnp.float32)
        wg = jax.random.normal(k2, (m, E), dtype=jnp.float32) * 0.02
        w1 = jax.random.normal(k3, (E, m, ffn), dtype=jnp.float32) * 0.02
        w2 = jax.random.normal(k4, (E, ffn, m), dtype=jnp.float32) * 0.02
        return {'x': x, 'wg': wg, 'w1': w1, 'w2': w2}
    _L0_ffn_all = _L0_ffn_setup()
    _L0_ffn_in = {k: v for k, v in _L0_ffn_all.items() if k in ('wg', 'w1', 'w2')}
    del _L0_ffn_all

    def _L1_attn_setup():
        import jax, jax.numpy as jnp
        import numpy as np
        B, N, D = (4, 512, 256)
        H, HD = (8, 64)
        FF = 1024
        ETA = 0.1
        DT = 0.01
        GAMMA_FLOOR = 0.1
        EPS = 1e-05

        def layernorm(x, g, b):
            m = jnp.mean(x, -1, keepdims=True)
            v = jnp.var(x, -1, keepdims=True)
            return (x - m) * jax.lax.rsqrt(v + EPS) * g + b

        def _cf_scan(d):
            dT = jnp.swapaxes(d, 0, 1)

            def step(c, di):
                a = di - 1.0 / c
                return (a, a)
            _, rest = jax.lax.scan(step, dT[0], dT[1:])
            return jnp.swapaxes(jnp.concatenate([dT[:1], rest], 0), 0, 1)

        def bk_core_diag(V, gamma):
            d = jax.lax.complex(V + 2.0, -gamma)
            a = _cf_scan(d)
            b = _cf_scan(d[:, ::-1])[:, ::-1]
            G = 1.0 / (a + b - d)
            return jnp.stack([G.real, G.imag], axis=-1)

        def hebbian_scan(q, k, v, gamma):
            qT = jnp.transpose(q, (1, 0, 2, 3))
            kT = jnp.transpose(k, (1, 0, 2, 3))
            vT = jnp.transpose(v, (1, 0, 2, 3))
            gT = jnp.swapaxes(gamma, 0, 1)
            W0 = jnp.zeros((q.shape[0], H, HD, HD), dtype=q.dtype)

            def step(W, inp):
                q_t, k_t, v_t, g_t = inp
                decay = jnp.exp(-g_t * DT)[:, None, None, None]
                W = decay * W + ETA * (k_t[..., :, None] * v_t[..., None, :])
                o = jnp.einsum('bhd,bhde->bhe', q_t, W)
                return (W, o)
            _, outs = jax.lax.scan(step, W0, (qT, kT, vT, gT))
            return jnp.transpose(outs, (1, 0, 2, 3)).reshape(q.shape[0], q.shape[1], H * HD)
        key = jax.random.key(seed)
        ks = jax.random.split(key, 12)
        s = lambda fan: 1.0 / np.sqrt(fan)
        return {'x': jax.random.normal(ks[0], (B, N, D), jnp.float32), 'ln1_g': jnp.ones((D,), jnp.float32), 'ln1_b': jnp.zeros((D,), jnp.float32), 'ln2_g': jnp.ones((D,), jnp.float32), 'ln2_b': jnp.zeros((D,), jnp.float32), 'ln3_g': jnp.ones((D,), jnp.float32), 'ln3_b': jnp.zeros((D,), jnp.float32), 'w_pot': jax.random.normal(ks[1], (D, 2), jnp.float32) * s(D), 'b_pot': jnp.zeros((2,), jnp.float32), 'w_bk': jax.random.normal(ks[2], (2, D), jnp.float32) * s(2), 'b_bk': jnp.zeros((D,), jnp.float32), 'w_qkv': jax.random.normal(ks[3], (D, 3 * H * HD), jnp.float32) * s(D), 'b_qkv': jnp.zeros((3 * H * HD,), jnp.float32), 'w_out': jax.random.normal(ks[4], (H * HD, D), jnp.float32) * s(H * HD), 'b_out': jnp.zeros((D,), jnp.float32), 'w_ff1': jax.random.normal(ks[5], (D, FF), jnp.float32) * s(D), 'b_ff1': jnp.zeros((FF,), jnp.float32), 'w_ff2': jax.random.normal(ks[6], (FF, D), jnp.float32) * s(FF), 'b_ff2': jnp.zeros((D,), jnp.float32)}
    _L1_attn_all = _L1_attn_setup()
    _L1_attn_in = {k: v for k, v in _L1_attn_all.items() if k in ('ln1_g', 'ln1_b', 'ln2_g', 'ln2_b', 'ln3_g', 'ln3_b', 'w_pot', 'b_pot', 'w_bk', 'b_bk', 'w_qkv', 'b_qkv', 'w_out', 'b_out', 'w_ff1', 'b_ff1', 'w_ff2', 'b_ff2')}
    del _L1_attn_all

    def _L1_xattn_setup():
        import jax, jax.numpy as jnp
        import numpy as np
        D_MODEL = 256
        N_HEADS = 16
        HEAD_DIM = D_MODEL // N_HEADS

        def sparsemax(x):
            x = x - jnp.max(x, axis=-1, keepdims=True)
            zs = -jnp.sort(-x, axis=-1)
            L = x.shape[-1]
            rho = jnp.arange(1, L + 1, dtype=x.dtype)
            cssv = jnp.cumsum(zs, axis=-1) - 1.0
            support = zs > cssv / rho
            k = jnp.maximum(jnp.sum(support, axis=-1, keepdims=True), 1)
            tau = jnp.take_along_axis(cssv, k - 1, axis=-1) / k.astype(x.dtype)
            return jnp.clip(x - tau, 0.0)

        def _split_heads(x):
            B, L, _ = x.shape
            return x.reshape(B, L, N_HEADS, HEAD_DIM).transpose(0, 2, 1, 3)
        key = jax.random.key(seed)
        ks = jax.random.split(key, 11)
        B, L = (2, 512)
        s = 0.02
        inp = {'q': jax.random.normal(ks[0], (B, L, D_MODEL), jnp.float32), 'k': jax.random.normal(ks[1], (B, L, D_MODEL), jnp.float32), 'v': jax.random.normal(ks[2], (B, L, D_MODEL), jnp.float32), 'Wq': jax.random.normal(ks[3], (D_MODEL, D_MODEL), jnp.float32) * s, 'bq': jnp.zeros((D_MODEL,), jnp.float32), 'Wk': jax.random.normal(ks[4], (D_MODEL, D_MODEL), jnp.float32) * s, 'bk': jnp.zeros((D_MODEL,), jnp.float32), 'Wv': jax.random.normal(ks[5], (D_MODEL, D_MODEL), jnp.float32) * s, 'bv': jnp.zeros((D_MODEL,), jnp.float32), 'Wo': jax.random.normal(ks[6], (D_MODEL, D_MODEL), jnp.float32) * s, 'bo': jnp.zeros((D_MODEL,), jnp.float32)}
        return inp
    _L1_xattn_all = _L1_xattn_setup()
    _L1_xattn_in = {k: v for k, v in _L1_xattn_all.items() if k in ('Wq', 'bq', 'Wk', 'bk', 'Wv', 'bv', 'Wo', 'bo')}
    del _L1_xattn_all

    def _L1_ffn_setup():
        import jax, jax.numpy as jnp
        import numpy as np
        JITTER_EPS = 0.01

        def phi_routing(logits, jitter_eps=JITTER_EPS):
            m, sel = jax.lax.top_k(logits, 2)
            T, E = logits.shape
            m1 = m[:, :1]
            factor1 = jnp.maximum(jnp.abs(logits), m1)
            mask1 = (m1 - logits) / factor1 > 2.0 * jitter_eps
            p1 = jax.nn.softmax(jnp.where(mask1, -jnp.inf, logits), axis=-1)
            mult1 = jnp.take_along_axis(p1, sel[:, :1], axis=-1)
            m2 = m[:, 1:2]
            factor2 = jnp.maximum(jnp.abs(logits), m2)
            mask2 = (m2 - logits) / factor2 > 2.0 * jitter_eps
            drop_top1 = jnp.arange(E)[None, :] == sel[:, :1]
            p2 = jax.nn.softmax(jnp.where(mask2 | drop_top1, -jnp.inf, logits), axis=-1)
            mult2 = jnp.take_along_axis(p2, sel[:, 1:2], axis=-1)
            return (jnp.concatenate([mult1, mult2], axis=-1), sel)
        key = jax.random.key(seed)
        k = jax.random.split(key, 5)
        B, S, H, F, E = (1, 128, 256, 1024, 8)
        return {'hidden_states': jax.random.normal(k[0], (B, S, H), jnp.float32), 'gate_w': jax.random.normal(k[1], (E, H), jnp.float32) * 0.02, 'w1': jax.random.normal(k[2], (E, F, H), jnp.float32) * 0.02, 'w2': jax.random.normal(k[3], (E, H, F), jnp.float32) * 0.02, 'w3': jax.random.normal(k[4], (E, F, H), jnp.float32) * 0.02}
    _L1_ffn_all = _L1_ffn_setup()
    _L1_ffn_in = {k: v for k, v in _L1_ffn_all.items() if k in ('gate_w', 'w1', 'w2', 'w3')}
    del _L1_ffn_all
    return {'x': x, 'ctx_1024': ctx_1024, 'fside_BxSxS2_0': fside_BxSxS2_0, 'L0_attn_in_proj_w': _L0_attn_in['in_proj_w'], 'L0_attn_conv_w': _L0_attn_in['conv_w'], 'L0_attn_conv_b': _L0_attn_in['conv_b'], 'L0_attn_x_proj_w': _L0_attn_in['x_proj_w'], 'L0_attn_dt_proj_w': _L0_attn_in['dt_proj_w'], 'L0_attn_dt_proj_b': _L0_attn_in['dt_proj_b'], 'L0_attn_A_log': _L0_attn_in['A_log'], 'L0_attn_D': _L0_attn_in['D'], 'L0_attn_out_proj_w': _L0_attn_in['out_proj_w'], 'L0_xattn_Wq': _L0_xattn_in['Wq'], 'L0_xattn_bq': _L0_xattn_in['bq'], 'L0_xattn_Wk': _L0_xattn_in['Wk'], 'L0_xattn_bk': _L0_xattn_in['bk'], 'L0_xattn_Wv': _L0_xattn_in['Wv'], 'L0_xattn_bv': _L0_xattn_in['bv'], 'L0_xattn_Wo': _L0_xattn_in['Wo'], 'L0_xattn_bo': _L0_xattn_in['bo'], 'L0_xattn_distance_scaling': _L0_xattn_in['distance_scaling'], 'L0_ffn_wg': _L0_ffn_in['wg'], 'L0_ffn_w1': _L0_ffn_in['w1'], 'L0_ffn_w2': _L0_ffn_in['w2'], 'L1_attn_ln1_g': _L1_attn_in['ln1_g'], 'L1_attn_ln1_b': _L1_attn_in['ln1_b'], 'L1_attn_ln2_g': _L1_attn_in['ln2_g'], 'L1_attn_ln2_b': _L1_attn_in['ln2_b'], 'L1_attn_ln3_g': _L1_attn_in['ln3_g'], 'L1_attn_ln3_b': _L1_attn_in['ln3_b'], 'L1_attn_w_pot': _L1_attn_in['w_pot'], 'L1_attn_b_pot': _L1_attn_in['b_pot'], 'L1_attn_w_bk': _L1_attn_in['w_bk'], 'L1_attn_b_bk': _L1_attn_in['b_bk'], 'L1_attn_w_qkv': _L1_attn_in['w_qkv'], 'L1_attn_b_qkv': _L1_attn_in['b_qkv'], 'L1_attn_w_out': _L1_attn_in['w_out'], 'L1_attn_b_out': _L1_attn_in['b_out'], 'L1_attn_w_ff1': _L1_attn_in['w_ff1'], 'L1_attn_b_ff1': _L1_attn_in['b_ff1'], 'L1_attn_w_ff2': _L1_attn_in['w_ff2'], 'L1_attn_b_ff2': _L1_attn_in['b_ff2'], 'L1_xattn_Wq': _L1_xattn_in['Wq'], 'L1_xattn_bq': _L1_xattn_in['bq'], 'L1_xattn_Wk': _L1_xattn_in['Wk'], 'L1_xattn_bk': _L1_xattn_in['bk'], 'L1_xattn_Wv': _L1_xattn_in['Wv'], 'L1_xattn_bv': _L1_xattn_in['bv'], 'L1_xattn_Wo': _L1_xattn_in['Wo'], 'L1_xattn_bo': _L1_xattn_in['bo'], 'L1_ffn_gate_w': _L1_ffn_in['gate_w'], 'L1_ffn_w1': _L1_ffn_in['w1'], 'L1_ffn_w2': _L1_ffn_in['w2'], 'L1_ffn_w3': _L1_ffn_in['w3']}

def reference(x, ctx_1024, fside_BxSxS2_0, L0_attn_in_proj_w, L0_attn_conv_w, L0_attn_conv_b, L0_attn_x_proj_w, L0_attn_dt_proj_w, L0_attn_dt_proj_b, L0_attn_A_log, L0_attn_D, L0_attn_out_proj_w, L0_xattn_Wq, L0_xattn_bq, L0_xattn_Wk, L0_xattn_bk, L0_xattn_Wv, L0_xattn_bv, L0_xattn_Wo, L0_xattn_bo, L0_xattn_distance_scaling, L0_ffn_wg, L0_ffn_w1, L0_ffn_w2, L1_attn_ln1_g, L1_attn_ln1_b, L1_attn_ln2_g, L1_attn_ln2_b, L1_attn_ln3_g, L1_attn_ln3_b, L1_attn_w_pot, L1_attn_b_pot, L1_attn_w_bk, L1_attn_b_bk, L1_attn_w_qkv, L1_attn_b_qkv, L1_attn_w_out, L1_attn_b_out, L1_attn_w_ff1, L1_attn_b_ff1, L1_attn_w_ff2, L1_attn_b_ff2, L1_xattn_Wq, L1_xattn_bq, L1_xattn_Wk, L1_xattn_bk, L1_xattn_Wv, L1_xattn_bv, L1_xattn_Wo, L1_xattn_bo, L1_ffn_gate_w, L1_ffn_w1, L1_ffn_w2, L1_ffn_w3):
    import jax
    import jax.numpy as jnp

    def _L0_attn_ref(hidden_states, in_proj_w, conv_w, conv_b, x_proj_w, dt_proj_w, dt_proj_b, A_log, D, out_proj_w):
        import jax, jax.numpy as jnp
        from jax import lax
        import numpy as np
        BATCH, SEQ = (2, 512)
        D_MODEL, D_STATE, D_CONV = (256, 16, 4)
        D_INNER = 2 * D_MODEL
        DT_RANK = D_MODEL // 16
        DT_MIN, DT_MAX = (0.001, 0.1)

        def _mamba_fwd(hidden_states, in_proj_w, conv_w, conv_b, x_proj_w, dt_proj_w, dt_proj_b, A_log, D, out_proj_w):
            silu = jax.nn.silu
            b, l, _ = hidden_states.shape
            xz = hidden_states @ in_proj_w.T
            x, z = jnp.split(xz, 2, axis=-1)
            xc = jnp.transpose(x, (0, 2, 1))
            xc = lax.conv_general_dilated(xc, conv_w, window_strides=(1,), padding=[(D_CONV - 1, 0)], feature_group_count=D_INNER, dimension_numbers=('NCH', 'OIH', 'NCH')) + conv_b[None, :, None]
            x = silu(jnp.transpose(xc, (0, 2, 1)))
            A = -jnp.exp(A_log)
            xp = x @ x_proj_w.T
            dt, Bm, C = jnp.split(xp, [DT_RANK, DT_RANK + D_STATE], axis=-1)
            dt = jax.nn.softplus(dt @ dt_proj_w.T + dt_proj_b)

            def step(h, ins):
                dt_t, B_t, C_t, x_t = ins
                dA = jnp.exp(dt_t[:, :, None] * A)
                h = dA * h + dt_t[:, :, None] * B_t[:, None, :] * x_t[:, :, None]
                y = jnp.einsum('bdn,bn->bd', h, C_t)
                return (h, y)
            h0 = jnp.zeros((b, D_INNER, D_STATE), hidden_states.dtype)
            xs = (jnp.transpose(dt, (1, 0, 2)), jnp.transpose(Bm, (1, 0, 2)), jnp.transpose(C, (1, 0, 2)), jnp.transpose(x, (1, 0, 2)))
            _, ys = lax.scan(step, h0, xs)
            y = jnp.transpose(ys, (1, 0, 2)) + x * D
            return y * silu(z) @ out_proj_w.T
        return _mamba_fwd(hidden_states, in_proj_w, conv_w, conv_b, x_proj_w, dt_proj_w, dt_proj_b, A_log, D, out_proj_w)

    def _L0_xattn_ref(query, key_, value, distances, Wq, bq, Wk, bk, Wv, bv, Wo, bo, distance_scaling):
        import jax, jax.numpy as jnp
        import numpy as np
        EMBED_DIM = 256
        NUM_HEADS = 16
        HEAD_DIM = EMBED_DIM // NUM_HEADS
        B, SQ, SK = (4, 512, 512)

        def _xavier(key, shape):
            fan_in, fan_out = (shape[1], shape[0])
            limit = float(np.sqrt(6.0 / (fan_in + fan_out)))
            return jax.random.uniform(key, shape, jnp.float32, -limit, limit)
        b, sq, e = query.shape
        sk = key_.shape[1]
        h, d = (NUM_HEADS, HEAD_DIM)
        q = (query @ Wq.T + bq) * d ** (-0.5)
        k = key_ @ Wk.T + bk
        v = value @ Wv.T + bv
        q = q.reshape(b, sq, h, d).transpose(0, 2, 1, 3)
        k = k.reshape(b, sk, h, d).transpose(0, 2, 1, 3)
        v = v.reshape(b, sk, h, d).transpose(0, 2, 1, 3)
        scores = jnp.einsum('bhqd,bhkd->bhqk', q, k)
        distance_bias = -jnp.log(distances + 1e-09) * jnp.abs(distance_scaling)
        scores = scores + distance_bias[:, None, :, :]
        attn = jax.nn.softmax(scores, axis=-1)
        out = jnp.einsum('bhqk,bhkd->bhqd', attn, v)
        out = out.transpose(0, 2, 1, 3).reshape(b, sq, e)
        return out @ Wo.T + bo

    def _L0_ffn_ref(x, wg, w1, w2):
        import jax, jax.numpy as jnp
        import numpy as np
        CAPACITY_FACTOR = 1.0

        def _top1_gate(x2d, wg):
            S, _ = x2d.shape
            E = wg.shape[1]
            C = int(CAPACITY_FACTOR * S / E)
            logits = x2d @ wg
            gates = jax.nn.softmax(logits, axis=-1)
            idx = jnp.argmax(gates, axis=-1)
            mask = jax.nn.one_hot(idx, E, dtype=jnp.int32)
            loc = jnp.cumsum(mask, axis=0) - 1
            me = jnp.mean(gates, axis=0)
            ce = jnp.mean(mask.astype(gates.dtype), axis=0)
            l_aux = E * jnp.sum(me * ce)
            mask = mask * (loc < C).astype(jnp.int32)
            gate_s = jnp.sum(gates * mask, axis=-1)
            loc_s = jnp.sum(loc * mask, axis=-1)
            loc_oh = jax.nn.one_hot(loc_s, C, dtype=gates.dtype)
            combine = (gate_s[:, None] * mask.astype(gates.dtype))[:, :, None] * loc_oh[:, None, :]
            dispatch = (combine > 0).astype(gates.dtype)
            return (l_aux, combine, dispatch)
        s, b, m = x.shape
        x2d = x.reshape(-1, m)
        l_aux, combine, dispatch = _top1_gate(x2d, wg)
        combine = combine[:, None]
        dispatch = dispatch[:, None]
        xr = x2d[:, None, :]
        dispatched = jnp.einsum('szfc,szm->zfcm', dispatch, xr)
        E = w1.shape[0]
        di = dispatched.reshape(E, -1, m)
        h = jax.nn.relu(jnp.einsum('ecm,emh->ech', di, w1))
        eo = jnp.einsum('ech,ehm->ecm', h, w2)
        eo = eo[None]
        out = jnp.einsum('szfc,zfcm->sm', combine, eo)
        return out.reshape(s, b, m)

    def _L1_attn_ref(x, ln1_g, ln1_b, ln2_g, ln2_b, ln3_g, ln3_b, w_pot, b_pot, w_bk, b_bk, w_qkv, b_qkv, w_out, b_out, w_ff1, b_ff1, w_ff2, b_ff2):
        import jax, jax.numpy as jnp
        import numpy as np
        B, N, D = (4, 512, 256)
        H, HD = (8, 64)
        FF = 1024
        ETA = 0.1
        DT = 0.01
        GAMMA_FLOOR = 0.1
        EPS = 1e-05

        def layernorm(x, g, b):
            m = jnp.mean(x, -1, keepdims=True)
            v = jnp.var(x, -1, keepdims=True)
            return (x - m) * jax.lax.rsqrt(v + EPS) * g + b

        def _cf_scan(d):
            dT = jnp.swapaxes(d, 0, 1)

            def step(c, di):
                a = di - 1.0 / c
                return (a, a)
            _, rest = jax.lax.scan(step, dT[0], dT[1:])
            return jnp.swapaxes(jnp.concatenate([dT[:1], rest], 0), 0, 1)

        def bk_core_diag(V, gamma):
            d = jax.lax.complex(V + 2.0, -gamma)
            a = _cf_scan(d)
            b = _cf_scan(d[:, ::-1])[:, ::-1]
            G = 1.0 / (a + b - d)
            return jnp.stack([G.real, G.imag], axis=-1)

        def hebbian_scan(q, k, v, gamma):
            qT = jnp.transpose(q, (1, 0, 2, 3))
            kT = jnp.transpose(k, (1, 0, 2, 3))
            vT = jnp.transpose(v, (1, 0, 2, 3))
            gT = jnp.swapaxes(gamma, 0, 1)
            W0 = jnp.zeros((q.shape[0], H, HD, HD), dtype=q.dtype)

            def step(W, inp):
                q_t, k_t, v_t, g_t = inp
                decay = jnp.exp(-g_t * DT)[:, None, None, None]
                W = decay * W + ETA * (k_t[..., :, None] * v_t[..., None, :])
                o = jnp.einsum('bhd,bhde->bhe', q_t, W)
                return (W, o)
            _, outs = jax.lax.scan(step, W0, (qT, kT, vT, gT))
            return jnp.transpose(outs, (1, 0, 2, 3)).reshape(q.shape[0], q.shape[1], H * HD)
        b, n, d = x.shape
        xn1 = layernorm(x, ln1_g, ln1_b)
        pot = xn1 @ w_pot + b_pot
        V = pot[..., 0]
        gamma = jax.nn.softplus(pot[..., 1]) + GAMMA_FLOOR
        bk_features = bk_core_diag(V, gamma)
        x = x + bk_features @ w_bk + b_bk
        xn2 = layernorm(x, ln2_g, ln2_b)
        qkv = (xn2 @ w_qkv + b_qkv).reshape(b, n, 3, H, HD)
        q, k, v = (qkv[:, :, 0], qkv[:, :, 1], qkv[:, :, 2])
        heb = hebbian_scan(q, k, v, gamma)
        x = x + heb @ w_out + b_out
        xn3 = layernorm(x, ln3_g, ln3_b)
        x = x + jax.nn.gelu(xn3 @ w_ff1 + b_ff1) @ w_ff2 + b_ff2
        return x

    def _L1_xattn_ref(q, k, v, Wq, bq, Wk, bk, Wv, bv, Wo, bo):
        import jax, jax.numpy as jnp
        import numpy as np
        D_MODEL = 256
        N_HEADS = 16
        HEAD_DIM = D_MODEL // N_HEADS

        def sparsemax(x):
            x = x - jnp.max(x, axis=-1, keepdims=True)
            zs = -jnp.sort(-x, axis=-1)
            L = x.shape[-1]
            rho = jnp.arange(1, L + 1, dtype=x.dtype)
            cssv = jnp.cumsum(zs, axis=-1) - 1.0
            support = zs > cssv / rho
            k = jnp.maximum(jnp.sum(support, axis=-1, keepdims=True), 1)
            tau = jnp.take_along_axis(cssv, k - 1, axis=-1) / k.astype(x.dtype)
            return jnp.clip(x - tau, 0.0)

        def _split_heads(x):
            B, L, _ = x.shape
            return x.reshape(B, L, N_HEADS, HEAD_DIM).transpose(0, 2, 1, 3)
        qh = _split_heads(q @ Wq + bq)
        kh = _split_heads(k @ Wk + bk)
        vh = _split_heads(v @ Wv + bv)
        scale = HEAD_DIM ** (-0.5)
        scores = jnp.einsum('bhqd,bhkd->bhqk', qh, kh) * scale
        attn = sparsemax(scores)
        out = jnp.einsum('bhqk,bhkd->bhqd', attn, vh)
        B, L = (q.shape[0], q.shape[1])
        out = out.transpose(0, 2, 1, 3).reshape(B, L, D_MODEL)
        return out @ Wo + bo

    def _L1_ffn_ref(hidden_states, gate_w, w1, w2, w3):
        import jax, jax.numpy as jnp
        import numpy as np
        JITTER_EPS = 0.01

        def phi_routing(logits, jitter_eps=JITTER_EPS):
            m, sel = jax.lax.top_k(logits, 2)
            T, E = logits.shape
            m1 = m[:, :1]
            factor1 = jnp.maximum(jnp.abs(logits), m1)
            mask1 = (m1 - logits) / factor1 > 2.0 * jitter_eps
            p1 = jax.nn.softmax(jnp.where(mask1, -jnp.inf, logits), axis=-1)
            mult1 = jnp.take_along_axis(p1, sel[:, :1], axis=-1)
            m2 = m[:, 1:2]
            factor2 = jnp.maximum(jnp.abs(logits), m2)
            mask2 = (m2 - logits) / factor2 > 2.0 * jitter_eps
            drop_top1 = jnp.arange(E)[None, :] == sel[:, :1]
            p2 = jax.nn.softmax(jnp.where(mask2 | drop_top1, -jnp.inf, logits), axis=-1)
            mult2 = jnp.take_along_axis(p2, sel[:, 1:2], axis=-1)
            return (jnp.concatenate([mult1, mult2], axis=-1), sel)
        B, S, H = hidden_states.shape
        E = w1.shape[0]
        x = hidden_states.reshape(-1, H)
        logits = x @ gate_w.T
        routing_weights, selected = phi_routing(logits)
        T = x.shape[0]
        wte = jnp.zeros((T, E), x.dtype).at[jnp.arange(T)[:, None], selected].add(routing_weights)
        out = jnp.zeros_like(x)
        for e in range(E):
            h = jax.nn.silu(x @ w1[e].T) * (x @ w3[e].T)
            out = out + wte[:, e:e + 1] * (h @ w2[e].T)
        return out.reshape(B, S, H)
    x = x + _L0_attn_ref(_layernorm(x, axis=-1), L0_attn_in_proj_w, L0_attn_conv_w, L0_attn_conv_b, L0_attn_x_proj_w, L0_attn_dt_proj_w, L0_attn_dt_proj_b, L0_attn_A_log, L0_attn_D, L0_attn_out_proj_w)
    x = x + _L0_xattn_ref(_layernorm(x, axis=-1), ctx_1024, ctx_1024, fside_BxSxS2_0, L0_xattn_Wq, L0_xattn_bq, L0_xattn_Wk, L0_xattn_bk, L0_xattn_Wv, L0_xattn_bv, L0_xattn_Wo, L0_xattn_bo, L0_xattn_distance_scaling)
    x = x + _L0_ffn_ref(_layernorm(x, axis=-1), L0_ffn_wg, L0_ffn_w1, L0_ffn_w2)
    x = x + _L1_attn_ref(_layernorm(x, axis=-1), L1_attn_ln1_g, L1_attn_ln1_b, L1_attn_ln2_g, L1_attn_ln2_b, L1_attn_ln3_g, L1_attn_ln3_b, L1_attn_w_pot, L1_attn_b_pot, L1_attn_w_bk, L1_attn_b_bk, L1_attn_w_qkv, L1_attn_b_qkv, L1_attn_w_out, L1_attn_b_out, L1_attn_w_ff1, L1_attn_b_ff1, L1_attn_w_ff2, L1_attn_b_ff2)
    x = x + _L1_xattn_ref(_layernorm(x, axis=-1), ctx_1024, ctx_1024, L1_xattn_Wq, L1_xattn_bq, L1_xattn_Wk, L1_xattn_bk, L1_xattn_Wv, L1_xattn_bv, L1_xattn_Wo, L1_xattn_bo)
    x = x + _L1_ffn_ref(_layernorm(x, axis=-1), L1_ffn_gate_w, L1_ffn_w1, L1_ffn_w2, L1_ffn_w3)
    return x

_drawn_inputs = setup_inputs


def setup_inputs(seed=0):
    import zlib

    import numpy as np

    out = dict(_drawn_inputs(seed))
    spreads = {'L0_attn_conv_b': (0.0, 0.8),
     'L0_attn_D': (1.0, 0.6),
     'L0_xattn_bq': (0.0, 0.8),
     'L0_xattn_bk': (0.0, 2.0),
     'L0_xattn_bv': (0.0, 0.519),
     'L0_xattn_bo': (0.0, 0.513),
     'L1_attn_ln1_g': (1.0, 0.2),
     'L1_attn_ln1_b': (0.0, 0.1),
     'L1_attn_ln2_g': (1.0, 0.2),
     'L1_attn_ln2_b': (0.0, 0.1),
     'L1_attn_ln3_g': (1.0, 0.6),
     'L1_attn_ln3_b': (0.0, 0.8),
     'L1_attn_b_pot': (0.0, 0.346),
     'L1_attn_b_bk': (0.0, 0.1),
     'L1_attn_b_qkv': (0.0, 0.1),
     'L1_attn_b_out': (0.0, 0.8),
     'L1_attn_b_ff1': (0.0, 0.8),
     'L1_attn_b_ff2': (0.0, 2.0),
     'L1_xattn_bq': (0.0, 0.8),
     'L1_xattn_bk': (0.0, 2.0),
     'L1_xattn_bv': (0.0, 0.8),
     'L1_xattn_bo': (0.0, 2.0)}
    factors = {'L0_attn_in_proj_w': 8.0,
     'L0_attn_conv_w': 8.0,
     'L0_attn_x_proj_w': 8.0,
     'L0_attn_dt_proj_w': 8.0,
     'L0_attn_dt_proj_b': 8.0,
     'L0_attn_A_log': 8.0,
     'L0_attn_out_proj_w': 8.0,
     'L0_ffn_wg': 11.305,
     'L0_ffn_w1': 13.429,
     'L1_attn_w_ff1': 3.024,
     'L1_attn_w_ff2': 2.784,
     'L1_xattn_Wq': 8.0,
     'L1_xattn_Wk': 8.0,
     'L1_xattn_Wv': 8.0,
     'L1_xattn_Wo': 8.0,
     'L1_ffn_gate_w': 8.0,
     'L1_ffn_w1': 8.0,
     'L1_ffn_w2': 8.0,
     'L1_ffn_w3': 8.0,
     'fside_BxSxS2_0': 2.926,
     'L0_xattn_Wq': 3.36,
     'L0_xattn_Wk': 3.283,
     'L0_ffn_w2': 4.46}
    for name, (base, spread) in spreads.items():
        noise = np.random.default_rng([zlib.crc32(name.encode()), seed]).standard_normal(out[name].shape)
        drawn = base * np.exp(spread * noise) if base else spread * noise
        out[name] = jnp.asarray(drawn.astype(out[name].dtype))
    for name, factor in factors.items():
        out[name] = (out[name] * factor).astype(out[name].dtype)
    return out
```

```python
from contextlib import ExitStack

import concourse.bass as bass
from concourse import mybir
from concourse.bass import ds

ALU = mybir.AluOpType
ACT = mybir.ActivationFunctionType
F32 = mybir.dt.float32
BF16 = mybir.dt.bfloat16
F32R = mybir.dt.float32r
U32 = mybir.dt.uint32
AX_X = mybir.AxisListType.X

P = 128
B, S, D = 2, 1024, 256
T = B * S
NT = T // P
TB = S // P
KD = D // P
EPS = 1e-5


class Chain:

    def __init__(self, eng, sem):
        self.eng, self.sem, self.n, self.base, self.k = eng, sem, 0, None, 0

    def add(self, ins):
        ins.then_inc(self.sem, 1)
        if self.base is None:
            self.n += 1
        else:
            self.k += 1

    def sync(self):
        if self.base is None:
            self.eng.wait_ge(self.sem, self.n)
        else:
            self.eng.wait_ge(self.sem, self.base + self.k)

    def __call__(self, ins):
        self.add(ins)
        self.sync()

    def enter(self, i, per):
        self.base, self.k, self.per = i * per + self.n, 0, per

    def leave(self, trips):
        assert self.k == self.per, (self.k, self.per)
        self.base, self.n = None, self.n + trips * self.per


class LayerNorm:

    def __init__(self, g, ctx, name, src, dst, dstT, banks, gain=None, bias=None):
        nc = g.nc
        self.g, self.src, self.dst, self.dstT, self.banks = g, src, dst, dstT, banks
        self.gain, self.bias = gain, bias
        sem = g.semaphores(name + "_")
        self.chain, self.var_ready, self.std_ready = sem("chain"), sem("var_ready"), sem("std_ready")
        self.xn_ready, self.tp_ready, self.xt_ready = sem("xn_ready"), sem("tp_ready"), sem("xt_ready")
        sb = lambda n, s: ctx.enter_context(nc.sbuf_tensor(f"{name}_{n}", s, F32))
        self.stats = sb("stats", [P, NT, 6])
        self.mv = sb("mv", [P, NT, 2])
        self.std = sb("std", [P, NT])
        self.rstd = sb("rstd", [P, NT])

    def dve(self, dve):
        ch = Chain(dve, self.chain)
        for t in range(NT):
            ch.add(dve.bn_stats(self.stats[:, t, :], self.src[:, t, :]))
        for t in range(NT):
            dve.wait_ge(self.chain, t + 1)
            ins = dve.bn_aggr(self.mv[:, t, :], self.stats[:, t, :])
        ins.then_inc(self.var_ready, 1)
        dve.wait_ge(self.std_ready, 1)
        ch(dve.reciprocal(self.rstd[:, :], self.std[:, :]))
        for t in range(NT):
            dve.tensor_scalar(self.dst[:, t, :], self.src[:, t, :], self.mv[:, t, 0:1], self.rstd[:, t:t + 1],
                              ALU.subtract, ALU.mult).then_inc(self.xn_ready, 1)

    def act(self, act):
        act.wait_ge(self.var_ready, 1)
        act.activation(self.std[:, :], self.mv[:, :, 1], ACT.Sqrt, bias=self.g.eps[:, 0:1]).then_inc(self.std_ready, 1)
        if self.dstT is None:
            return
        for t in range(NT):
            act.wait_ge(self.tp_ready, t + 1)
            bank = self.banks[t % len(self.banks)]
            if self.gain is None:
                act.activation(self.dstT[:, :, t * P:(t + 1) * P],
                               bank[:, 0:D].rearrange("p (k n) -> p k n", k=KD), ACT.Copy).then_inc(self.xt_ready, 1)
            else:
                for k in range(KD):
                    ins = act.activation(self.dstT[:, k, t * P:(t + 1) * P], bank[:, k * P:(k + 1) * P], ACT.Identity,
                                         bias=self.bias[:, k:k + 1], scale=self.gain[:, k:k + 1])
                ins.then_inc(self.xt_ready, 1)

    def pe(self, pe):
        for t in range(NT):
            pe.wait_ge(self.xn_ready, t + 1)
            if t >= len(self.banks):
                pe.wait_ge(self.xt_ready, t + 1 - len(self.banks))
            bank = self.banks[t % len(self.banks)]
            for k in range(KD):
                ins = pe.transpose(bank[:, k * P:(k + 1) * P], self.dst[:, t, k * P:(k + 1) * P], self.g.ident[:, :])
            ins.then_inc(self.tp_ready, 1)


class G:

    def __init__(self, nc):
        self.nc, self.made = nc, []

    def semaphores(self, prefix):
        def make_one(name):
            self.made.append(self.nc.alloc_semaphore(name=prefix + name))
            return self.made[-1]
        return make_one

    def end_stage(self):
        self.nc.clear_and_free_semaphores(self.made)
        self.nc.all_engine_barrier()
        self.made = []


def setup(g, ctx, a):
    nc = g.nc
    sb = lambda n, s, dt=F32: ctx.enter_context(nc.sbuf_tensor(n, s, dt))
    g.X = sb("X", [P, NT, D])
    g.XT = sb("XT", [P, KD, T])
    g.ident = sb("ident", [P, P])
    g.upper = sb("upper", [P, P])
    g.ones = sb("ones", [P, P])
    g.eps = sb("eps", [P, 2])
    g.ps = ctx.enter_context(nc.psum_tensor("ps", [P, 8, 512], F32))
    g.PS = [g.ps[:, i, :] for i in range(8)]
    sem = g.semaphores("s_")
    x_loaded, const_chain = sem("x_loaded"), sem("const_chain")
    with nc.Block() as block:
        @block.sync
        def _(sp):
            sp.dma_start(g.X[:, :, :], a["x"]).then_inc(x_loaded, 16)
            sp.wait_ge(x_loaded, 16)

        @block.gpsimd
        def _(pool):
            ch = Chain(pool, const_chain)
            ch.add(pool.memset(g.ident[:, :], 0.0))
            ch.add(pool.memset(g.ones[:, :], 1.0))
            ch.add(pool.memset(g.eps[:, 0:1], EPS))
            ch.add(pool.memset(g.eps[:, 1:2], 1e-9))
            ch.sync()
            ch.add(pool.affine_select(out=g.ident[:, :], in_=g.ident[:, :], compare_op=ALU.not_equal, fill=1.0,
                                      base=0, pattern=[[-1, P]], channel_multiplier=1))
            ch(pool.affine_select(out=g.upper[:, :], in_=g.ones[:, :], compare_op=ALU.is_ge, fill=0.0,
                                  base=0, pattern=[[1, P]], channel_multiplier=-1))


DI, NS, DC, R = 512, 16, 4, 16
CI = DI // P
HB = S // 512
RING = 3


def mamba(g, a):
    nc = g.nc
    PS = g.PS
    with ExitStack() as ctx:
        sb = lambda n, s, dt=F32: ctx.enter_context(nc.sbuf_tensor(n, s, dt))
        sem = g.semaphores("m_")
        w_in = sb("w_in", [P, KD, 2 * DI])
        w_x = sb("w_x", [P, CI, 3 * 2 * NS + R])
        w_dt = sb("w_dt", [P, DI])
        w_out = sb("m_w_out", [P, CI, D])
        conv_w, conv_b = sb("conv_w", [P, CI, DC]), sb("conv_b", [P, CI])
        dt_b, skip = sb("dt_b", [P, CI]), sb("skip", [P, CI])
        nA = sb("nA", [P, CI, NS])
        sel = sb("sel", [P, 2 * NS, P], BF16)
        XC = sb("XC", [P, CI, DC - 1 + S])
        Z = sb("Z", [P, CI, S])
        XS = sb("XS", [P, CI, S])
        DT = sb("DT", [P, CI, S])
        DTX = XC
        GY = sb("GY", [P, CI, S])
        XN = GY[:, :, :].rearrange("p c (t d) -> p (c t) d", d=D)
        dA = sb("dA", [P, RING, S])
        U = sb("U", [P, RING, S])
        H = sb("H", [P, RING, S])
        HC = sb("HC", [P, RING, S])
        BC = sb("BC", [P, 2, 2, S])
        XP = dA[:, 0, :]
        R1, R2 = dA[:, 1, :], dA[:, 2, :]
        parts = sb("parts", [P, S], BF16)
        part_f = sb("part_f", [P, 2, 512], BF16)
        EA = lambda k: GY[:, k % CI, k // CI * 512:(k // CI + 1) * 512]
        LN = lambda k: [U, H, HC][k // 3][:, k % 3, 0:512]
        W1 = lambda k: [U, H, HC][k // 3][:, k % 3, 512:1024]

        loaded, cc = sem("loaded"), sem("const_chain")
        ln = LayerNorm(g, ctx, "m_ln", g.X, XN, g.XT, PS[0:4])
        neg_a = sem("neg_a")
        chain, act_chain = sem("chain"), sem("act_chain")
        in_ready, in_used = sem("in_ready"), sem("in_used")
        conv_ready, xs_ready = sem("conv_ready"), sem("xs_ready")
        xp_ready, xp_used, parts_ready = sem("xp_ready"), sem("xp_used"), sem("parts_ready")
        dtp_ready, dtp_used, abs_used, log_ready = sem("dtp_ready"), sem("dtp_used"), sem("abs_used"), sem("log_ready")
        exp_ready = sem("exp_ready")
        dtx_ready = sem("dtx_ready")
        bc_ready, bc_copied, bc_used = sem("bc_ready"), sem("bc_copied"), sem("bc_used")
        da_ready, u_ready, h_ready, hc_ready, hc_used = (sem("da_ready"), sem("u_ready"), sem("h_ready"),
                                                         sem("hc_ready"), sem("hc_used"))
        y_ready, y_used, gy_ready = sem("y_ready"), sem("y_used"), sem("gy_ready")
        o_ready, o_used = sem("o_ready"), sem("o_used")

        names = [(w_in[:, :, :], "w_in"), (w_x[:, :, :], "w_x"), (w_dt[96:96 + R, :], "w_dt"), (w_out[:, :, :], "w_out"),
                 (conv_w[:, :, :], "conv_w"), (conv_b[:, :], "conv_b"), (dt_b[:, :], "dt_b"), (skip[:, :], "skip"),
                 (nA[:, :, :], "A_log")]
        ALL = 16 * len(names)
        CPB = 2
        ITS = NS * CPB
        NBLK = CI // CPB

        with nc.Block() as block:
            @block.sync
            def _(sp):
                for dst, name in names:
                    sp.dma_start(dst, a["m_" + name]).then_inc(loaded, 16)

            @block.gpsimd
            def _(pool):
                ch = Chain(pool, cc)
                ch.add(pool.memset(XC[:, :, 0:DC - 1], 0.0))
                ch.add(pool.memset(sel[0:96, :, :], 0.0))
                ch.sync()
                for q in range(3):
                    ch(pool.affine_select(out=sel[0:96, :, :], in_=sel[0:96, :, :], compare_op=ALU.not_equal, fill=1.0,
                                          base=-32 * q, pattern=[[-1, 2 * NS], [0, P]], channel_multiplier=1))
                for b in range(B):
                    for blk in range(NBLK):
                        for it in range(ITS):
                            n, c = it // CPB, CPB * blk + it % CPB
                            step = blk * ITS + it
                            if it == 0:
                                pool.wait_ge(dtx_ready, (b + 1) * CI * HB)
                            if it % CPB == 0:
                                pool.wait_ge(bc_copied, b * (NBLK * NS * 4) + 4 * (blk * NS + n) + 2)
                            if step >= RING:
                                pool.wait_ge(h_ready, b * (NBLK * ITS) + step - RING + 1)
                            pool.tensor_tensor(U[:, step % RING, :], DTX[:, c, 0:S], BC[:, 0, n % 2, :],
                                               ALU.mult).then_inc(u_ready, 1)

            @block.tensor
            def _(pe):
                pe.wait_ge(cc, 5)
                ln.pe(pe)
                pe.wait_ge(loaded, ALL)
                for b in range(B):
                    pe.wait_ge(ln.xt_ready, NT)
                    if b:
                        pe.wait_ge(o_used, b * TB)
                    k = 0
                    for f in range(2 * CI):
                        for h in range(HB):
                            if k >= 4:
                                pe.wait_ge(in_used, b * 16 + k - 3)
                            for kd in range(KD):
                                ins = pe.matmul(PS[k % 4][:, :], w_in[:, kd, f * P:(f + 1) * P],
                                                g.XT[:, kd, b * S + h * 512:b * S + (h + 1) * 512], start=(kd == 0), stop=(kd == KD - 1))
                            ins.then_inc(in_ready, 1)
                            k += 1
                    for h in range(HB):
                        pe.wait_ge(xs_ready, b * 8 + 4 * (h + 1))
                        for c in range(CI):
                            ins = pe.matmul(PS[4 + h][0:112, :], w_x[:, c, :], XS[:, c, h * 512:(h + 1) * 512],
                                            start=(c == 0), stop=(c == CI - 1))
                        ins.then_inc(xp_ready, 1)
                    k = 0
                    for h in range(HB):
                        pe.wait_ge(xp_used, b * 2 + h + 1)
                        for c in range(CI):
                            if k == 0:
                                pe.wait_ge(in_used, (b + 1) * 16)
                            if k >= 4:
                                pe.wait_ge(dtp_used, b * 8 + k - 3)
                                pe.wait_ge(abs_used, b * 8 + k - 3)
                            pe.matmul(PS[k % 4][:, :], w_dt[96:96 + R, c * P:(c + 1) * P],
                                      XP[96:96 + R, h * 512:(h + 1) * 512], start=True, stop=True).then_inc(dtp_ready, 1)
                            k += 1
                    def broadcast(blk, n):
                        m = blk * NS + n
                        for w in range(2):
                            for h in range(HB):
                                q = 4 * m + 2 * w + h
                                if m == 0 and w == 0 and h == 0:
                                    pe.wait_ge(parts_ready, b + 1)
                                if m >= 1:
                                    pe.wait_ge(bc_copied, b * (NBLK * NS * 4) + q - 3)
                                pe.matmul(PS[4 + 2 * w + h][:, :], sel[0:96, NS * w + n, :],
                                          parts[0:96, h * 512:(h + 1) * 512], start=True, stop=True).then_inc(bc_ready, 1)

                    for blk in range(NBLK):
                        if blk == 0:
                            broadcast(0, 0)
                        for it in range(ITS):
                            n, c = it // CPB, it % CPB
                            step = blk * ITS + it
                            if c == 0 and blk * NS + n + 1 < NBLK * NS:
                                broadcast((blk * NS + n + 1) // NS, (n + 1) % NS)
                            if it < CPB:
                                if blk == 0:
                                    pe.wait_ge(dtp_used, (b + 1) * 8)
                                    pe.wait_ge(abs_used, (b + 1) * 8)
                                else:
                                    pe.wait_ge(y_used, b * (NBLK * 4) + 4 * blk)
                            pe.wait_ge(hc_ready, b * (NBLK * ITS) + step + 1)
                            for h in range(HB):
                                ins = pe.matmul(PS[2 * c + h][:, :], g.ident[:, :], HC[:, step % RING, h * 512:(h + 1) * 512],
                                                start=(n == 0), stop=(n == NS - 1))
                            ins.then_inc(hc_used, 1)
                    for t in range(TB):
                        if t == 0:
                            pe.wait_ge(gy_ready, (b + 1) * CI * HB)
                        if t >= 2:
                            pe.wait_ge(o_used, b * TB + t - 1)
                        for c in range(CI):
                            ins = pe.matmul(PS[t % 2][:, 0:D], GY[:, c, t * P:(t + 1) * P], w_out[:, c, :],
                                            start=(c == 0), stop=(c == CI - 1))
                        ins.then_inc(o_ready, 1)

            @block.scalar
            def _(act):
                act.wait_ge(loaded, ALL)
                ch = Chain(act, act_chain)
                ln.act(act)
                ch(act.activation(nA[:, :, :], nA[:, :, :], ACT.Exp))
                act.wait_ge(act_chain, 1)
                ch(act.mul(nA[:, :, :], nA[:, :, :], -1.0))
                for b in range(B):
                    k = 0
                    if b:
                        act.wait_ge(dtx_ready, b * 8)
                    if b:
                        act.wait_ge(u_ready, b * (NBLK * ITS))
                    if b:
                        act.wait_ge(gy_ready, b * 8)
                    for f in range(2 * CI):
                        for h in range(HB):
                            act.wait_ge(in_ready, b * 16 + k + 1)
                            if f < CI:
                                dst, fn = XC[:, f, DC - 1 + h * 512:DC - 1 + (h + 1) * 512], ACT.Copy
                            else:
                                dst, fn = Z[:, f - CI, h * 512:(h + 1) * 512], ACT.Silu
                            act.activation(dst, PS[k % 4][:, :], fn).then_inc(in_used, 1)
                            k += 1
                    for h in range(HB):
                        for c in range(CI):
                            act.wait_ge(conv_ready, b * 8 + 4 * h + c + 1)
                            act.activation(XS[:, c, h * 512:(h + 1) * 512], GY[:, c, h * 512:(h + 1) * 512],
                                           ACT.Silu).then_inc(xs_ready, 1)
                    for h in range(HB):
                        act.wait_ge(xp_ready, b * 2 + h + 1)
                        act.activation(XP[0:112, h * 512:(h + 1) * 512], PS[4 + h][0:112, :], ACT.Copy).then_inc(xp_used, 1)
                    for k in range(CI * HB):
                        act.wait_ge(dtp_ready, b * 8 + k + 1)
                        act.activation(EA(k), PS[k % 4][:, :], ACT.Abs, bias=dt_b[:, k % CI:k % CI + 1]).then_inc(abs_used, 1)
                    for k in range(CI * HB):
                        act.wait_ge(abs_used, b * 8 + k + 1)
                        act.activation(EA(k), EA(k), ACT.Exp, scale=-1.0).then_inc(exp_ready, 1)
                    for k in range(CI * HB):
                        act.wait_ge(exp_ready, b * 8 + k + 1)
                        act.activation(LN(k), EA(k), ACT.Ln, bias=1.0).then_inc(log_ready, 1)
                    for blk in range(NBLK):
                        def copy_bc(n):
                            m = blk * NS + n
                            for w in range(2):
                                for h in range(HB):
                                    q = 4 * m + 2 * w + h
                                    act.wait_ge(bc_ready, b * (NBLK * NS * 4) + q + 1)
                                    if m >= 2 and h == 0 and w == 0:
                                        act.wait_ge(hc_ready, b * (NBLK * ITS) + CPB * (m - 1))
                                    act.activation(BC[:, w, n % 2, h * 512:(h + 1) * 512], PS[4 + 2 * w + h][:, :],
                                                   ACT.Copy).then_inc(bc_copied, 1)
                        for it in range(ITS):
                            n, c = it // CPB, CPB * blk + it % CPB
                            step = blk * ITS + it
                            if it % CPB == 0:
                                copy_bc(n)
                            if step == 0:
                                act.wait_ge(dtx_ready, (b + 1) * 8)
                            if step >= RING:
                                act.wait_ge(h_ready, b * (NBLK * ITS) + step - RING + 1)
                            act.activation(dA[:, step % RING, :], DT[:, c, :], ACT.Exp,
                                           scale=nA[:, c, n:n + 1]).then_inc(da_ready, 1)

            @block.vector
            def _(dve):
                ln.dve(dve)
                dve.wait_ge(loaded, ALL)
                dve.wait_ge(ln.tp_ready, NT)
                ch = Chain(dve, chain)
                for b in range(B):
                    if b:
                        dve.wait_ge(o_ready, b * TB)
                    for h in range(HB):
                        for c in range(CI):
                            o = GY[:, c, h * 512:(h + 1) * 512]
                            dve.wait_ge(in_used, b * 16 + 2 * c + h + 1)
                            ch(dve.tensor_scalar(o, XC[:, c, h * 512:h * 512 + 512], conv_w[:, c, 0:1], conv_b[:, c:c + 1],
                                                 ALU.mult, ALU.add))
                            for j in range(1, DC):
                                ins = dve.scalar_tensor_tensor(o, XC[:, c, h * 512 + j:h * 512 + j + 512],
                                                               conv_w[:, c, j:j + 1], o, ALU.mult, ALU.add)
                                if j < DC - 1:
                                    ch(ins)
                            ins.then_inc(conv_ready, 1)
                    for h in range(HB):
                        dve.wait_ge(xp_used, b * 2 + h + 1)
                        s = slice(h * 512, (h + 1) * 512)
                        ch(dve.tensor_copy(part_f[0:96, 0, :], XP[0:96, s]))
                        ch(dve.tensor_tensor(R1[0:96, s], XP[0:96, s], part_f[0:96, 0, :], ALU.subtract))
                        ch(dve.tensor_copy(part_f[0:96, 1, :], R1[0:96, s]))
                        ch(dve.tensor_tensor(R2[0:96, s], R1[0:96, s], part_f[0:96, 1, :], ALU.subtract))
                        if h == 0:
                            if b:
                                dve.wait_ge(bc_ready, b * (NBLK * NS * 4))
                        dve.tensor_copy(parts[0:32, s], part_f[0:32, 0, :])
                        dve.tensor_copy(parts[32:64, s], part_f[32:64, 1, :])
                        ins = dve.tensor_copy(parts[64:96, s], R2[64:96, s])
                        ch(ins)
                    dve.sem_inc(parts_ready, 1)
                    for k in range(CI * HB):
                        c, s = k % CI, slice(k // CI * 512, (k // CI + 1) * 512)
                        dve.wait_ge(abs_used, b * 8 + k + 1)
                        dve.tensor_scalar(DT[:, c, s], PS[k % 4][:, :], dt_b[:, c:c + 1], 0.0, ALU.add,
                                          ALU.max).then_inc(dtp_used, 1)
                    dve.wait_ge(in_used, (b + 1) * 16)
                    for k in range(CI * HB):
                        c, s = k % CI, slice(k // CI * 512, (k // CI + 1) * 512)
                        dve.wait_ge(exp_ready, b * 8 + k + 1)
                        ch(dve.tensor_scalar(W1(k), EA(k), 1.0, None, ALU.add))
                        ch(dve.scalar_tensor_tensor(W1(k), W1(k), 1.0, EA(k), ALU.subtract, ALU.subtract))
                        ch(dve.tensor_tensor(DT[:, c, s], DT[:, c, s], W1(k), ALU.subtract))
                        dve.wait_ge(log_ready, b * 8 + k + 1)
                        ch(dve.tensor_tensor(DT[:, c, s], DT[:, c, s], LN(k), ALU.add))
                        dve.tensor_tensor(DTX[:, c, s], DT[:, c, s], XS[:, c, s], ALU.mult).then_inc(dtx_ready, 1)
                    for blk in range(NBLK):
                        for it in range(ITS):
                            n, c = it // CPB, it % CPB
                            step = blk * ITS + it
                            r = step % RING
                            dve.wait_ge(da_ready, b * (NBLK * ITS) + step + 1)
                            dve.wait_ge(u_ready, b * (NBLK * ITS) + step + 1)
                            dve.tensor_tensor_scan(H[:, r, :], dA[:, r, :], U[:, r, :], 0.0, ALU.mult,
                                                   ALU.add).then_inc(h_ready, 1)
                            dve.wait_ge(h_ready, b * (NBLK * ITS) + step + 1)
                            if c == 0:
                                dve.wait_ge(bc_copied, b * (NBLK * NS * 4) + 4 * (blk * NS + n) + 4)
                            if step >= RING:
                                dve.wait_ge(hc_used, b * (NBLK * ITS) + step - RING + 1)
                            dve.tensor_tensor(HC[:, r, :], H[:, r, :], BC[:, 1, n % 2, :], ALU.mult).then_inc(hc_ready, 1)
                        dve.wait_ge(hc_used, b * (NBLK * ITS) + (blk + 1) * ITS)
                        for c in range(CPB):
                            for h in range(HB):
                                cc_, s = CPB * blk + c, slice(h * 512, (h + 1) * 512)
                                dve.scalar_tensor_tensor(GY[:, cc_, s], XS[:, cc_, s], skip[:, cc_:cc_ + 1],
                                                         PS[2 * c + h][:, :], ALU.mult, ALU.add).then_inc(y_used, 1)
                                dve.wait_ge(y_used, b * 8 + 4 * blk + 2 * c + h + 1)
                                dve.tensor_tensor(GY[:, cc_, s], GY[:, cc_, s], Z[:, cc_, s], ALU.mult).then_inc(gy_ready, 1)
                    for t in range(TB):
                        dve.wait_ge(o_ready, b * TB + t + 1)
                        row = g.X[:, b * TB + t, :]
                        dve.tensor_tensor(row, row, PS[t % 2][:, 0:D], ALU.add).then_inc(o_used, 1)

NH, HD, SK = 16, 16, 77
HALF = NH // 2
HW = HALF * SK
NCH = -(-HW // P)
LASTW = HW - (NCH - 1) * P
NEWTON = 24
OUT = 384


def attention(g, a, pre, sparse):
    nc = g.nc
    ps, PS = g.ps, g.PS
    with ExitStack() as ctx:
        sb = lambda n, s, dt=F32: ctx.enter_context(nc.sbuf_tensor(pre + n, s, dt))
        sem = g.semaphores(pre)
        wq, wk, wv, wo = (sb(n, [P, KD, D]) for n in ("wq", "wk", "wv", "wo"))
        bq, bk = sb("bq", [P, KD]), sb("bk", [P, KD])
        bv, bo = sb("bv", [P, D]), sb("bo", [P, D])
        ctxT = sb("ctxT", [P, KD, B * SK])
        KT = sb("KT", [P, KD, B * SK])
        hmask = sb("hmask", [P, HALF])
        KBD = sb("KBD", [P, 2, B, HALF, SK])
        VS = sb("VS", [P, B, D])
        VBD = sb("VBD", [P, B, 2, NCH, P])
        QT = sb("QT", [P, KD, T])
        PN = sb("PN", [P, 2, NH, SK])
        PT = sb("PT", [P, 2, 2, NCH, P])
        OT = sb("OT", [P, 2, D])
        zeros = sb("zeros", [P, NCH * P])
        if sparse:
            SC = sb("SC", [P, NT, NH, SK])
            Z8 = sb("Z8", [P, NT * NH, 8])
            reset = sb("reset", [P, NT * NH, 8])
            W8, CS = (QT[:, k, :].rearrange("p (r e) -> p r e", e=8) for k in range(2))
            T8 = g.XT[:, 0, :].rearrange("p (r e) -> p r e", e=8)
            rank = sb("rank", [P, 8])
            cnt, rcnt, th = sb("cnt", [P, NT * NH]), sb("rcnt", [P, NT * NH]), sb("th", [P, NT * NH])
            top = sb("top", [P, 2])
            topi = sb("topi", [1, 1], mybir.dt.int32)
            nt_d, nt_g = PN[:, 0, :, :], PN[:, 1, :, :]
            nt_f, nt_c = sb("nt_f", [P, NH]), sb("nt_c", [P, NH])
            XN = SC[:, 0:4, :, :].rearrange("p a h s -> p (a h s)")[:, 0:NT * D].rearrange("p (t d) -> p t d", d=D)
        else:
            LB = sb("LB", [P, NT, SK])
            scaling = sb("scaling", [P, 2])
            SC = sb("SC", [P, 2, NH, SK])
            mx, sm, rs = sb("mx", [P, 2, NH]), sb("sm", [P, 2, NH]), sb("rs", [P, 2, NH])
            xn_room = sb("xn", [P, NT, D])
            XN = xn_room[:, :, :]
        VD = nc.dram_tensor(pre + "values", (B, 2, NCH * P * P), F32).ap()

        loaded, hm, vz = sem("loaded"), sem("hm"), sem("vz")
        ln = LayerNorm(g, ctx, pre + "ln", g.X, XN, g.XT, PS[0:4])
        bo_added = sem("bo_added")
        k_ready, kt_ready, kbd_ready = sem("k_ready"), sem("kt_ready"), sem("kbd_ready")
        v_ready, vs_ready, v_stored, vbd_ready = sem("v_ready"), sem("vs_ready"), sem("v_stored"), sem("vbd_ready")
        q_ready, q_used, bq_scaled = sem("q_ready"), sem("q_used"), sem("bq_scaled")
        sc_ready, sc_used, sc_copied = sem("sc_ready"), sem("sc_used"), sem("sc_copied")
        chain, act_chain = sem("chain"), sem("act_chain")
        sub_ready, e_ready, rs_ready, pn_ready = sem("sub_ready"), sem("e_ready"), sem("rs_ready"), sem("pn_ready")
        tpa_ready, pta_ready, ot_ready, otc_ready, o_ready, x_ready = (
            sem("tpa_ready"), sem("pta_ready"), sem("ot_ready"), sem("otc_ready"), sem("o_ready"), sem("x_ready"))
        top_ready, topt_ready, lb_ready = sem("top_ready"), sem("topt_ready"), sem("lb_ready")

        names = [(wq[:, :, :], pre + "wq"), (wk[:, :, :], pre + "wk"), (wv[:, :, :], pre + "wv"), (wo[:, :, :], pre + "wo"),
                 (bq[:, :], pre + "bq"), (bk[:, :], pre + "bk"), (ctxT[:, :, :], "ctxT"),
                 (bv[:, :], pre + "bv"), (bo[:, :], pre + "bo")]
        if not sparse:
            names += [(LB[:, :, :], "dist"), (scaling[:, 0:1], "scaling")]
        ALL = 16 * len(names)

        def score_view(bank0):
            return ps[:, bank0:bank0 + 4, 0:HW // 2]

        with nc.Block() as block:
            @block.sync
            def _(sp):
                for dst, name in names:
                    src = a[name]
                    if dst.shape[0] == P and src.shape[0] == 1:
                        src = src.to_broadcast([P, src.shape[1]])
                    sp.dma_start(dst, src).then_inc(loaded, 16)
                sp.wait_ge(hm, 1)
                for b in range(B):
                    for h in range(2):
                        sp.dma_start(VD[b, h].rearrange("(q w) -> q w", w=NCH * P), zeros[:, :]).then_inc(vz, 16)
                sp.wait_ge(vz, 16 * 2 * B)
                sp.wait_ge(vs_ready, B)
                step = SK * P + HD
                for b in range(B):
                    for h in range(2):
                        dst = VD[b, h, 0:HALF * step].rearrange("(h x) -> h x", x=step)[:, 0:SK * P]
                        dst = dst.rearrange("h (s c) -> s h c", c=P)[:, :, 0:HD]
                        sp.dma_start(dst, VS[0:SK, b, h * P:(h + 1) * P].rearrange("s (h d) -> s h d", d=HD)).then_inc(v_stored, 16)
                sp.wait_ge(v_stored, 16 * 2 * B)
                for b in range(B):
                    for h in range(2):
                        sp.dma_start(VBD[:, b, h, :, :], VD[b, h].rearrange("(m p c) -> p m c", p=P, c=P)).then_inc(vbd_ready, 16)

            @block.gpsimd
            def _(pool):
                pool.memset(zeros[:, :], 0.0).then_inc(hm, 1)
                pool.memset(hmask[:, :], 1.0).then_inc(hm, 1)
                pool.wait_ge(hm, 2)
                pool.affine_select(out=hmask[:, :], in_=hmask[:, :], compare_op=ALU.is_ge, fill=0.0,
                                   base=0, pattern=[[-HD, HALF]], channel_multiplier=1).then_inc(hm, 1)
                pool.wait_ge(hm, 3)
                pool.affine_select(out=hmask[:, :], in_=hmask[:, :], compare_op=ALU.is_ge, fill=0.0,
                                   base=HD - 1, pattern=[[HD, HALF]], channel_multiplier=-1).then_inc(hm, 1)
                if sparse:
                    pool.memset(reset[:, :, :], 1.0).then_inc(hm, 1)
                    pool.iota(rank[:, :], pattern=[[1, 8]], base=1, channel_multiplier=0,
                              allow_small_or_imprecise_dtypes=True).then_inc(hm, 1)
                    pool.wait_ge(hm, 6)
                    pool.memset(reset[:, :, 0:1], 0.0).then_inc(hm, 1)
                pool.wait_ge(loaded, ALL)
                with pool.Fori(0, NT) as i:
                    pool.wait_ge(ln.xn_ready, i + 1)
                    row = g.X[:, ds(i, 1), :].rearrange("p a d -> p (a d)")
                    pool.tensor_tensor(row, row, bo[:, :], ALU.add).then_inc(bo_added, 1)
                if not sparse:
                    with pool.Fori(0, NT // 2) as j:
                        for u in range(2):
                            pool.wait_ge(rs_ready, 2 * j + u + 1)
                            pool.tensor_tensor(PN[:, u, :, :], PN[:, u, :, :],
                                               rs[:, u, :].unsqueeze(2).to_broadcast([P, NH, SK]),
                                               ALU.mult).then_inc(pn_ready, 1)

            @block.tensor
            def _(pe):
                pe.wait_ge(loaded, ALL)
                for k in range(KD):
                    for kd in range(KD):
                        ins = pe.matmul(PS[4 + k][:, 0:B * SK], wk[:, kd, k * P:(k + 1) * P], ctxT[:, kd, :],
                                        start=(kd == 0), stop=(kd == KD - 1))
                    ins.then_inc(k_ready, 1)
                for b in range(B):
                    for kd in range(KD):
                        ins = pe.matmul(PS[6 + b][0:SK, 0:D], ctxT[:, kd, b * SK:(b + 1) * SK], wv[:, kd, :],
                                        start=(kd == 0), stop=(kd == KD - 1))
                    ins.then_inc(v_ready, 1)
                ln.pe(pe)
                k = 0
                pe.wait_ge(kt_ready, KD)
                for j in range(T // 512):
                    pe.wait_ge(ln.xt_ready, 4 * (j + 1))
                    for f in range(KD):
                        if k >= 2:
                            pe.wait_ge(q_used, k - 1)
                        for kd in range(KD):
                            ins = pe.matmul(PS[4 + k % 2][:, :], wq[:, kd, f * P:(f + 1) * P], g.XT[:, kd, j * 512:(j + 1) * 512],
                                            start=(kd == 0), stop=(kd == KD - 1))
                        ins.then_inc(q_ready, 1)
                        k += 1

                def scores(i):
                    for q in range(4):
                        half, hh = q // 2, q % 2
                        ins = pe.matmul(PS[q + (4 * (i % 2) if sparse else 0)][:, 0:HW // 2], QT[:, half, i * P:(i + 1) * P],
                                        KBD[:, half, i // TB, 4 * hh:4 * hh + 4, :].rearrange("p h s -> p (h s)"),
                                        start=True, stop=True)
                    return ins

                def project(i):
                    pe.wait_ge(otc_ready, i + 1)
                    for c in range(2):
                        for h in range(2):
                            ins = pe.matmul(PS[2 + c][:, OUT:OUT + P], OT[:, i % 2, h * P:(h + 1) * P], wo[:, h, c * P:(c + 1) * P],
                                            start=(h == 0), stop=(h == 1))
                    return ins

                def round_(n):
                    if n >= 1:
                        pe.wait_ge(sc_used, n)
                    if n < NT:
                        ins = scores(n)
                    if n >= 4:
                        ins = project(n - 4)
                    ins.then_inc(sc_ready, 1)

                def transpose_weights(i):
                    pe.wait_ge(pn_ready, i + 1)
                    weights = PN[:, i % 2, :, :].rearrange("p h s -> p (h s)")
                    for h in range(2):
                        if i >= 1:
                            pe.wait_ge(pta_ready, 3 * (i - 1) + h + 1)
                        for m in range(NCH - 1):
                            ins = pe.transpose(PS[4 + h][:, m * P:(m + 1) * P], weights[:, h * HW + m * P:h * HW + (m + 1) * P],
                                               g.ident[:, :])
                        ins.then_inc(tpa_ready, 1)
                    if i >= 1:
                        pe.wait_ge(pta_ready, 3 * i)
                    for h in range(2):
                        ins = pe.transpose(PS[6][0:LASTW, h * P:(h + 1) * P], weights[:, (h + 1) * HW - LASTW:(h + 1) * HW],
                                           g.ident[:, :])
                    ins.then_inc(tpa_ready, 1)

                def weigh_values(i):
                    if i == 0:
                        pe.wait_ge(vbd_ready, 16 * 2 * B)
                    if i >= 1:
                        pe.wait_ge(otc_ready, i)
                    pe.wait_ge(pta_ready, 3 * (i + 1))
                    for h in range(2):
                        for m in range(NCH):
                            w = P if m < NCH - 1 else LASTW
                            ins = pe.matmul(PS[7][:, h * P:(h + 1) * P], VBD[0:w, i // TB, h, m, :], PT[0:w, i % 2, h, m, :],
                                            start=(m == 0), stop=(m == NCH - 1))
                    ins.then_inc(ot_ready, 1)

                pe.wait_ge(kbd_ready, 2 * B)
                pe.wait_ge(q_used, 2 * (T // 512))
                pe.wait_ge(ln.xt_ready, NT)
                pe.wait_ge(vs_ready, B)
                if sparse:
                    for i in range(NT):
                        if i >= 2:
                            pe.wait_ge(sc_copied, i - 1)
                        scores(i).then_inc(sc_ready, 1)
                    pe.wait_ge(top_ready, 1)
                    pe.transpose(PS[4][0:2, 0:P], top[:, :], g.ident[:, :]).then_inc(topt_ready, 1)
                else:
                    round_(0)
                    round_(1)
                for i in range(NT + 2):
                    if not sparse:
                        round_(i + 2)
                    elif i >= 2:
                        if i >= 3:
                            pe.wait_ge(x_ready, i - 2)
                        project(i - 2).then_inc(o_ready, 1)
                    if 1 <= i <= NT:
                        weigh_values(i - 1)
                    if i < NT:
                        transpose_weights(i)

            @block.scalar
            def _(act):
                act.wait_ge(loaded, ALL)
                ch = Chain(act, act_chain)
                if not sparse:
                    ch.add(act.activation(LB[:, :, :], LB[:, :, :], ACT.Ln, bias=g.eps[:, 1:2]))
                    ch.add(act.activation(scaling[:, 1:2], scaling[:, 0:1], ACT.Abs))
                    ch.sync()
                    ch(act.mul(scaling[:, 1:2], scaling[:, 1:2], -1.0))
                    act.activation(LB[:, :, :], LB[:, :, :], ACT.Copy, scale=scaling[:, 1:2]).then_inc(lb_ready, 1)
                act.activation(bq[:, :], bq[:, :], ACT.Copy, scale=HD ** -0.5).then_inc(bq_scaled, 1)
                for k in range(KD):
                    act.wait_ge(k_ready, k + 1)
                    act.activation(KT[:, k, :], PS[4 + k][:, 0:B * SK], ACT.Identity, bias=bk[:, k:k + 1]).then_inc(kt_ready, 1)
                ln.act(act)
                act.wait_ge(bq_scaled, 1)
                k = 0
                for j in range(T // 512):
                    for f in range(KD):
                        act.wait_ge(q_ready, k + 1)
                        act.activation(QT[:, f, j * 512:(j + 1) * 512], PS[4 + k % 2][:, :], ACT.Identity,
                                       bias=bq[:, f:f + 1], scale=HD ** -0.5).then_inc(q_used, 1)
                        k += 1

                def out_steps(i, u):
                    fn = ACT.Relu if sparse else ACT.Copy
                    for h in range(2):
                        act.wait_ge(tpa_ready, 3 * i + h + 1)
                        act.activation(PT[:, u, h, 0:NCH - 1, :], PS[4 + h][:, :].rearrange("p (m n) -> p m n", n=P),
                                       fn).then_inc(pta_ready, 1)
                    act.wait_ge(tpa_ready, 3 * i + 3)
                    act.activation(PT[0:LASTW, u, :, NCH - 1, :], PS[6][0:LASTW, 0:2 * P].rearrange("p (h n) -> p h n", h=2),
                                   fn).then_inc(pta_ready, 1)

                if sparse:
                    with act.Fori(0, NT // 2) as j:
                        for u in range(2):
                            act.wait_ge(sc_ready, 2 * j + u + 1)
                            act.activation(SC[:, ds(2 * j + u, 1), :, :].rearrange("p a (q h) s -> p (a q) (h s)", q=4),
                                           score_view(4 * u), ACT.Copy).then_inc(sc_copied, 1)

                def exponentials(i, u):
                    act.wait_ge(sub_ready, i + 1)
                    act.activation(PN[:, u, :, :], SC[:, u, :, :], ACT.Exp).then_inc(e_ready, 1)

                def outputs(i, u):
                    act.wait_ge(ot_ready, i + 1)
                    act.activation(OT[:, u, :], PS[7][:, 0:D], ACT.Copy).then_inc(otc_ready, 1)

                if not sparse:
                    exponentials(0, 0)
                    exponentials(1, 1)
                out_steps(0, 0)
                with act.Fori(0, NT // 2 - 1) as j:
                    for u in range(2):
                        i = 2 * j + u
                        if not sparse:
                            exponentials(i + 2, u)
                        outputs(i, u)
                        out_steps(i + 1, 1 - u)
                outputs(NT - 2, 0)
                out_steps(NT - 1, 1)
                outputs(NT - 1, 1)

            @block.vector
            def _(dve):
                ch = Chain(dve, chain)
                ln.dve(dve)
                dve.wait_ge(loaded, ALL)
                dve.wait_ge(hm, 4)
                for b in range(B):
                    dve.wait_ge(v_ready, b + 1)
                    dve.tensor_tensor(VS[0:SK, b, :], PS[6 + b][0:SK, 0:D], bv[0:SK, :], ALU.add).then_inc(vs_ready, 1)
                for h in range(2):
                    for b in range(B):
                        dve.wait_ge(kt_ready, h + 1)
                        dve.tensor_tensor(KBD[:, h, b, :, :], KT[:, h, b * SK:(b + 1) * SK].unsqueeze(1).to_broadcast([P, HALF, SK]),
                                          hmask[:, :].unsqueeze(2).to_broadcast([P, HALF, SK]), ALU.mult).then_inc(kbd_ready, 1)
                if sparse:
                    for i in range(NT):
                        dve.wait_ge(sc_copied, i + 1)
                        for h in range(NH):
                            ins = dve.max(Z8[:, i * NH + h, :], SC[:, i, h, :])
                        ins.then_inc(sc_used, 1)
                    dve.wait_ge(sc_used, NT)
                    dve.wait_ge(hm, 7)
                    flat = lambda x: x[:, :, :].rearrange("p r e -> p (r e)")
                    first = Z8[:, :, 0:1].to_broadcast([P, NT * NH, 8])
                    ch(dve.tensor_tensor(W8[:, :, :], Z8[:, :, :], first, ALU.subtract))
                    ch.add(dve.tensor_tensor_scan(flat(CS), flat(reset), flat(W8), 0.0, ALU.mult, ALU.add))
                    ch.add(dve.tensor_tensor(T8[:, :, :], W8[:, :, :], rank[:, :].unsqueeze(1).to_broadcast([P, NT * NH, 8]), ALU.mult))
                    ch.sync()
                    ch(dve.scalar_tensor_tensor(flat(T8), flat(T8), 1.0, flat(CS), ALU.add, ALU.subtract))
                    ch(dve.tensor_scalar(flat(T8), flat(T8), 0.0, None, ALU.is_gt))
                    ch.add(dve.tensor_reduce(cnt[:, :], T8[:, :, :], AX_X, ALU.add))
                    ch.add(dve.tensor_tensor(W8[:, :, :], W8[:, :, :], T8[:, :, :], ALU.mult))
                    ch.sync()
                    ch.add(dve.tensor_reduce(th[:, :], W8[:, :, :], AX_X, ALU.add))
                    ch.add(dve.reciprocal(rcnt[:, :], cnt[:, :]))
                    ch.add(dve.memset(top[:, :], 0.0))
                    ch.sync()
                    dve.tensor_reduce(top[:, 0:1], cnt[:, :], AX_X, ALU.max).then_inc(top_ready, 1)
                    ch(dve.scalar_tensor_tensor(th[:, :], th[:, :], -1.0, rcnt[:, :], ALU.add, ALU.mult))
                    ch(dve.tensor_tensor(th[:, :], th[:, :], Z8[:, :, 0], ALU.add))
                    dve.wait_ge(topt_ready, 1)
                    ch(dve.tensor_reduce(top[0:1, 1:2], PS[4][0:1, 0:P], AX_X, ALU.max))
                    ch(dve.tensor_copy(topi[0:1, 0:1], top[0:1, 1:2]))
                    dve.wait_ge(sc_copied, NT)
                    widest = dve.value_load(topi[0:1, 0:1], min_val=0, max_val=8)
                    with dve.If(widest >= 8):
                        with dve.Fori(0, NEWTON) as it:
                            with dve.Fori(0, NT) as i:
                                thv = th[:, ds(i * NH, NH)]
                                dve.tensor_tensor(nt_d, SC[:, ds(i, 1), :, :].rearrange("p a h s -> p (a h) s"),
                                                  thv.unsqueeze(2).to_broadcast([P, NH, SK]), ALU.subtract)
                                dve.drain()
                                dve.tensor_scalar(nt_g, nt_d, 0.0, None, ALU.is_gt)
                                dve.tensor_scalar(nt_d, nt_d, 0.0, None, ALU.max)
                                dve.drain()
                                dve.tensor_reduce(nt_c[:, :], nt_g, AX_X, ALU.add)
                                dve.tensor_reduce(nt_f[:, :], nt_d, AX_X, ALU.add)
                                dve.drain()
                                dve.reciprocal(nt_c[:, :], nt_c[:, :])
                                dve.drain()
                                dve.scalar_tensor_tensor(nt_f[:, :], nt_f[:, :], -1.0, nt_c[:, :], ALU.add, ALU.mult)
                                dve.drain()
                                dve.tensor_tensor(thv, thv, nt_f[:, :], ALU.add)
                                dve.drain()

                def add_out(i):
                    row = g.X[:, ds(i, 1), :].rearrange("p a (c n) -> p (a c) n", n=P)
                    return dve.tensor_tensor(row, row, ps[:, 2:4, OUT:OUT + P], ALU.add)

                dve.wait_ge(bo_added, NT)
                if sparse:
                    def weights(i, u):
                        thv = th[:, ds(i * NH, NH)]
                        dve.tensor_tensor(PN[:, u, :, :], SC[:, ds(i, 1), :, :].rearrange("p a h s -> p (a h) s"),
                                          thv.unsqueeze(2).to_broadcast([P, NH, SK]), ALU.subtract).then_inc(pn_ready, 1)

                    def output(i):
                        dve.wait_ge(o_ready, i + 1)
                        add_out(i).then_inc(x_ready, 1)
                    weights(0, 0)
                    weights(1, 1)
                    with dve.Fori(0, NT // 2 - 1) as j:
                        for u in range(2):
                            i = 2 * j + u
                            dve.wait_ge(tpa_ready, 3 * i + 3)
                            weights(i + 2, u)
                            output(i)
                    output(NT - 2)
                    output(NT - 1)
                else:
                    dve.wait_ge(lb_ready, 1)

                    def round_(n, u, scores=True, output=True):
                        dve.wait_ge(sc_ready, n + 1)
                        if scores:
                            for q in range(4):
                                ins = dve.tensor_tensor(SC[:, u, 4 * q:4 * q + 4, :], PS[q][:, 0:HW // 2].rearrange("p (h s) -> p h s", s=SK),
                                                        LB[:, ds(n, 1), :].to_broadcast([P, 4, SK]), ALU.add)
                        if output:
                            ins = add_out(n - 4)
                        ins.then_inc(sc_used, 1)
                        if scores:
                            dve.wait_ge(sc_used, n + 1)
                            ch(dve.tensor_reduce(mx[:, u, :], SC[:, u, :, :], AX_X, ALU.max))
                            dve.tensor_tensor(SC[:, u, :, :], SC[:, u, :, :], mx[:, u, :].unsqueeze(2).to_broadcast([P, NH, SK]),
                                              ALU.subtract).then_inc(sub_ready, 1)

                    def sums(i, u):
                        dve.wait_ge(e_ready, i + 1)
                        ch(dve.tensor_reduce(sm[:, u, :], PN[:, u, :, :], AX_X, ALU.add))
                        dve.reciprocal(rs[:, u, :], sm[:, u, :]).then_inc(rs_ready, 1)

                    round_(0, 0, output=False)
                    round_(1, 1, output=False)
                    for i in range(2):
                        sums(i, i)
                        round_(i + 2, i, output=False)
                    with dve.Fori(0, NT // 2 - 2) as j:
                        ch.enter(j, 4)
                        for u in range(2):
                            sums(2 * j + u + 2, u)
                            round_(2 * j + u + 4, u)
                    ch.leave(NT // 2 - 2)
                    for i in range(2):
                        sums(NT - 2 + i, i)
                        round_(NT + i, i, scores=False)
                    round_(NT + 2, 0, scores=False)
                    round_(NT + 3, 1, scores=False)


def xattn0(g, a):
    attention(g, a, "a0_", False)


def xattn1(g, a):
    attention(g, a, "a1_", True)


E = 8
F = 1024
FC = F // P
CAP = T // E
CB = CAP // P
NTE = NT * E
BIG = float(1 << 20)


class Router:

    def __init__(self, g, ctx, pre):
        nc = g.nc
        self.g = g
        sb = lambda n, s, dt=F32: ctx.enter_context(nc.sbuf_tensor(pre + "r_" + n, s, dt))
        sem = g.semaphores(pre + "r_")
        self.sb = sb
        self.wg = sb("wg", [P, KD, E])
        self.L, self.EX, self.A1, self.A2 = (sb(n, [P, NT, E]) for n in ("L", "EX", "A1", "A2"))
        self.TOT, self.CUM, self.first = (sb(n, [P, E, NT]) for n in ("TOT", "CUM", "first"))
        self.OH = sb("OH", [P, NT, E])
        self.PL = sb("PL", [P, NT, E])
        self.e8 = sb("e8", [P, E])
        self.logits_ready, self.exp_in, self.exp_out = sem("logits_ready"), sem("exp_in"), sem("exp_out")
        self.oh_ready, self.count_ready, self.const = sem("oh_ready"), sem("count_ready"), sem("const")

    def pool(self, pool):
        pool.iota(self.e8[:, :], pattern=[[1, E]], base=-E, channel_multiplier=0,
                  allow_small_or_imprecise_dtypes=True).then_inc(self.const, 1)
        pool.memset(self.first[:, :, :], 1.0).then_inc(self.const, 1)
        pool.wait_ge(self.const, 2)
        pool.memset(self.first[:, :, 0:1], 0.0).then_inc(self.const, 1)

    def pe_logits(self, pe, ln):
        for t in range(NT):
            pe.wait_ge(ln.xt_ready, t + 1)
            for kd in range(KD):
                ins = pe.matmul(self.g.PS[4][:, t * E:(t + 1) * E], self.g.XT[:, kd, t * P:(t + 1) * P], self.wg[:, kd, :],
                                start=(kd == 0), stop=(kd == KD - 1))
        ins.then_inc(self.logits_ready, 1)

    def pe_counts(self, pe):
        pe.wait_ge(self.oh_ready, 1)
        oh = self.OH[:, :, :].rearrange("p t e -> p (t e)")
        pe.matmul(self.g.PS[5][:, 0:NTE], self.g.upper[:, :], oh, start=True, stop=True)
        pe.matmul(self.g.PS[6][:, 0:NTE], self.g.ones[:, :], oh, start=True, stop=True).then_inc(self.count_ready, 1)

    def wide(self, x):
        return x.unsqueeze(2).to_broadcast([P, NT, E])

    def row(self, x):
        return x.unsqueeze(1).to_broadcast([P, NT, E])

    def dve_first(self, dve, ch, best, onehot, low):
        ch(dve.tensor_tensor(self.A1[:, :, :], best, self.row(self.e8[:, :]), ALU.mult))
        ch(dve.tensor_reduce(low, self.A1[:, :, :], AX_X, ALU.min))
        ch(dve.tensor_tensor(onehot, self.row(self.e8[:, :]), self.wide(low), ALU.is_equal))

    def dve_places(self, dve, ch):
        dve.sem_inc(self.oh_ready, 1)
        dve.wait_ge(self.count_ready, 1)
        dve.wait_ge(self.const, 3)
        flat = lambda x: x[:, :, :].rearrange("p e t -> p (e t)")
        ch(dve.tensor_copy(self.TOT[:, :, :], self.g.PS[6][:, 0:NTE].rearrange("p (t e) -> p e t", e=E)))
        ch(dve.tensor_tensor_scan(flat(self.CUM), flat(self.first), flat(self.TOT), 0.0, ALU.mult, ALU.add))
        ch(dve.tensor_tensor(self.TOT[:, :, :], self.CUM[:, :, :], self.TOT[:, :, :], ALU.subtract))
        ch(dve.tensor_tensor(self.PL[:, :, :], self.g.PS[5][:, 0:NTE].rearrange("p (t e) -> p t e", e=E),
                             self.TOT[:, :, :].rearrange("p e t -> p t e"), ALU.add))
        ch(dve.tensor_scalar(self.PL[:, :, :], self.PL[:, :, :], 1.0, None, ALU.subtract))


def ffn0(g, a):
    nc, PS = g.nc, g.PS
    with ExitStack() as ctx:
        sb = lambda n, s, dt=F32: ctx.enter_context(nc.sbuf_tensor("f0_" + n, s, dt))
        sem = g.semaphores("f0_")
        WR = 3
        w1, w2 = sb("w1", [P, WR, KD, F]), sb("w2", [P, WR, FC, D])
        XN = sb("XN", [P, NT, D])
        rt = Router(g, ctx, "f0_")
        gate, low, loc, slot, keep, gk, t1 = (sb(n, [P, NT]) for n in ("gate", "low", "loc", "slot", "keep", "gk", "t1"))
        put, get = sb("put", [P, NT], U32), sb("get", [P, NT], U32)
        zeros = sb("zeros", [P, 2 * D])
        DI = sb("DI", [P, 2, CB, D])
        DIT = sb("DIT", [P, 2, KD, CAP])
        HT = sb("HT", [P, 2, FC, CAP])
        EO = sb("EO", [P, 2, CB, D])
        rows_in = nc.dram_tensor("f0_rows_in", (E * CAP, D), F32).ap()
        rows_out = nc.dram_tensor("f0_rows_out", (E * CAP, D), F32).ap()

        ln = LayerNorm(g, ctx, "f0_ln", g.X, XN, g.XT, PS[0:4])
        chain, wg_loaded = sem("chain"), sem("wg_loaded")
        w_loaded = [sem(f"w_loaded{i}") for i in range(WR)]
        zeroed, cleared = sem("zeroed"), sem("cleared")
        slots_ready, scattered = sem("slots_ready"), sem("scattered")
        di_loaded = [sem(f"di_loaded{i}") for i in range(2)]
        dtp_ready, dit_ready = sem("dtp_ready"), sem("dit_ready")
        h_ready, ht_ready, eo_ready, eo_copied = sem("h_ready"), sem("ht_ready"), sem("eo_ready"), sem("eo_copied")
        stored = [sem(f"stored{i}") for i in range(2)]
        gathered = sem("gathered")

        with nc.Block() as block:
            @block.sync
            def _(sp):
                sp.dma_start(rt.wg[:, :, :], a["f0_wg"]).then_inc(wg_loaded, 16)

                def load_weights(e):
                    if e >= WR:
                        sp.wait_ge(eo_ready, CB * (e - WR + 1))
                    sp.dma_start(w1[:, e % WR, :, :], a["f0_w1"][e]).then_inc(w_loaded[e % WR], 16)
                    sp.dma_start(w2[:, e % WR, :, :], a["f0_w2"][e]).then_inc(w_loaded[e % WR], 16)
                sp.wait_ge(zeroed, 1)
                for q in range(E * CAP * D // (P * 2 * D)):
                    sp.dma_start(rows_in[q * 2 * P:(q + 1) * 2 * P, :].rearrange("(p r) d -> p (r d)", r=2),
                                 zeros[:, :]).then_inc(cleared, 16)
                for e in range(WR):
                    load_weights(e)
                sp.wait_ge(scattered, 16 * NT)
                for e in range(E):
                    if e >= 2:
                        sp.wait_ge(dtp_ready, CB * (e - 1))
                    sp.dma_start(DI[:, e % 2, :, :], rows_in[e * CAP:(e + 1) * CAP, :].rearrange("(s p) d -> p s d", p=P)).then_inc(
                        di_loaded[e % 2], 16)
                    if e >= 1:
                        if e - 1 + WR < E:
                            load_weights(e - 1 + WR)
                        sp.wait_ge(eo_copied, CB * e)
                        sp.dma_start(rows_out[(e - 1) * CAP:e * CAP, :].rearrange("(s p) d -> p s d", p=P),
                                     EO[:, (e - 1) % 2, :, :]).then_inc(stored[(e - 1) % 2], 16)
                sp.wait_ge(eo_copied, CB * E)
                sp.dma_start(rows_out[(E - 1) * CAP:E * CAP, :].rearrange("(s p) d -> p s d", p=P),
                             EO[:, (E - 1) % 2, :, :]).then_inc(stored[(E - 1) % 2], 16)
                for s in stored:
                    sp.wait_ge(s, 16 * E // 2)

            @block.gpsimd
            def _(pool):
                pool.memset(zeros[:, :], 0.0).then_inc(zeroed, 1)
                rt.pool(pool)
                pool.wait_ge(slots_ready, 1)
                pool.wait_ge(cleared, 16 * (E * CAP // (2 * P)))
                for t in range(NT):
                    pool.indirect_dma_start(out=rows_in, out_offset=bass.IndirectOffsetOnAxis(ap=put[:, t:t + 1], axis=0),
                                            in_=XN[:, t, :], in_offset=None, bounds_check=E * CAP - 1,
                                            oob_is_err=False).then_inc(scattered, 16)
                for s in stored:
                    pool.wait_ge(s, 16 * E // 2)
                pool.wait_ge(scattered, 16 * NT)
                for t in range(NT):
                    pool.indirect_dma_start(out=XN[:, t, :], out_offset=None, in_=rows_out,
                                            in_offset=bass.IndirectOffsetOnAxis(ap=get[:, t:t + 1], axis=0),
                                            bounds_check=E * CAP - 1, oob_is_err=False).then_inc(gathered, 16)

            @block.tensor
            def _(pe):
                ln.pe(pe)
                pe.wait_ge(wg_loaded, 16)
                rt.pe_logits(pe, ln)
                rt.pe_counts(pe)
                hk = 0
                for e in range(E):
                    pe.wait_ge(di_loaded[e % 2], 16 * (e // 2 + 1))
                    for s in range(CB):
                        if CB * e + s >= 2:
                            pe.wait_ge(dit_ready, CB * e + s - 1)
                        for k in range(KD):
                            ins = pe.transpose(PS[s][:, k * P:(k + 1) * P], DI[:, e % 2, s, k * P:(k + 1) * P], g.ident[:, :])
                        ins.then_inc(dtp_ready, 1)
                    pe.wait_ge(w_loaded[e % WR], 32 * (e // WR + 1))
                    pe.wait_ge(dit_ready, CB * (e + 1))
                    for f in range(FC):
                        if hk >= 3:
                            pe.wait_ge(ht_ready, hk - 2)
                        for kd in range(KD):
                            ins = pe.matmul(PS[2 + hk % 3][:, 0:CAP], w1[:, e % WR, kd, f * P:(f + 1) * P], DIT[:, e % 2, kd, :],
                                            start=(kd == 0), stop=(kd == KD - 1))
                        ins.then_inc(h_ready, 1)
                        hk += 1
                    pe.wait_ge(ht_ready, FC * (e + 1))
                    for s in range(CB):
                        if e >= 1:
                            pe.wait_ge(eo_copied, CB * (e - 1) + s + 1)
                        for f in range(FC):
                            ins = pe.matmul(PS[5 + s][:, 0:D], HT[:, e % 2, f, s * P:(s + 1) * P], w2[:, e % WR, f, :],
                                            start=(f == 0), stop=(f == FC - 1))
                        ins.then_inc(eo_ready, 1)

            @block.scalar
            def _(act):
                ln.act(act)
                act.wait_ge(rt.exp_in, 1)
                act.activation(rt.EX[:, :, :], rt.L[:, :, :], ACT.Exp).then_inc(rt.exp_out, 1)
                for e in range(E):
                    for s in range(CB):
                        act.wait_ge(dtp_ready, CB * e + s + 1)
                        act.activation(DIT[:, e % 2, :, s * P:(s + 1) * P], PS[s][:, 0:D].rearrange("p (k n) -> p k n", k=KD),
                                       ACT.Copy).then_inc(dit_ready, 1)
                    for s in range(CB):
                        act.wait_ge(eo_ready, CB * e + s + 1)
                        if e >= 2 and s == 0:
                            act.wait_ge(stored[e % 2], 16 * (e // 2))
                        act.activation(EO[:, e % 2, s, :], PS[5 + s][:, 0:D], ACT.Copy).then_inc(eo_copied, 1)

            @block.vector
            def _(dve):
                ch = Chain(dve, chain)
                ln.dve(dve)
                dve.wait_ge(rt.const, 3)
                dve.wait_ge(rt.logits_ready, 1)
                lg = PS[4][:, 0:NTE].rearrange("p (t e) -> p t e", e=E)
                ch(dve.tensor_reduce(t1[:, :], lg, AX_X, ALU.max))
                dve.tensor_tensor(rt.L[:, :, :], lg, rt.wide(t1[:, :]), ALU.subtract).then_inc(rt.exp_in, 1)
                dve.wait_ge(rt.exp_in, 1)
                ch(dve.tensor_scalar(rt.A2[:, :, :], rt.L[:, :, :], 0.0, None, ALU.is_equal))
                rt.dve_first(dve, ch, rt.A2[:, :, :], rt.OH[:, :, :], low[:, :])
                dve.wait_ge(rt.exp_out, 1)
                ch(dve.tensor_reduce(t1[:, :], rt.EX[:, :, :], AX_X, ALU.add))
                ch(dve.reciprocal(gate[:, :], t1[:, :]))
                rt.dve_places(dve, ch)
                ch(dve.tensor_tensor(rt.A1[:, :, :], rt.PL[:, :, :], rt.OH[:, :, :], ALU.mult))
                ch(dve.tensor_reduce(loc[:, :], rt.A1[:, :, :], AX_X, ALU.add))
                ch(dve.tensor_scalar(keep[:, :], loc[:, :], float(CAP), None, ALU.is_lt))
                ch(dve.scalar_tensor_tensor(slot[:, :], low[:, :], float(CAP), loc[:, :], ALU.mult, ALU.add))
                ch(dve.tensor_scalar(t1[:, :], keep[:, :], -BIG, BIG + float(E * CAP), ALU.mult, ALU.add))
                ch(dve.tensor_tensor(put[:, :], slot[:, :], t1[:, :], ALU.add))
                ch(dve.tensor_scalar(get[:, :], slot[:, :], float(E * CAP), float(E * CAP - 1), ALU.add, ALU.min))
                ch(dve.tensor_tensor(gk[:, :], gate[:, :], keep[:, :], ALU.mult))
                dve.sem_inc(slots_ready, 1)
                for hk in range(E * FC):
                    e, f = hk // FC, hk % FC
                    dve.wait_ge(h_ready, hk + 1)
                    if e >= 2 and f == 0:
                        dve.wait_ge(eo_ready, CB * (e - 1))
                    dve.tensor_scalar(HT[:, e % 2, f, :], PS[2 + hk % 3][:, 0:CAP], 0.0, None, ALU.max).then_inc(ht_ready, 1)
                dve.wait_ge(gathered, 16 * NT)
                for t in range(NT):
                    ins = dve.scalar_tensor_tensor(g.X[:, t, :], XN[:, t, :], gk[:, t:t + 1], g.X[:, t, :], ALU.mult, ALU.add)


MB = 2 * T // P + E - 1


def ffn1(g, a):
    nc, PS = g.nc, g.PS
    I32 = mybir.dt.int32
    with ExitStack() as ctx:
        sb = lambda n, s, dt=F32: ctx.enter_context(nc.sbuf_tensor("f1_" + n, s, dt))
        sem = g.semaphores("f1_")
        WSZ = 2 * KD * F + FC * D
        PART = WSZ // 3
        W = sb("W", [P, 4 * WSZ], F32R)
        stage = sb("stage", [P, 3, PART])
        XN = sb("XN", [P, NT, D])
        rt = Router(g, ctx, "f1_")
        OH1, OH2, AB, MK = (sb(n, [P, NT, E]) for n in ("OH1", "OH2", "AB", "MK"))
        m1, m2, low, mult1, mult2, t1, t2 = (sb(n, [P, NT]) for n in ("m1", "m2", "low", "mult1", "mult2", "t1", "t2"))
        idx = [sb(f"idx{i}", [P, NT], U32) for i in range(2)]
        nb, start, ends = (sb(n, [P, E]) for n in ("nb", "start", "ends"))
        nbi = sb("nbi", [P, E], I32)
        blk = sb("blk", [P, MB])
        cmp = sb("cmp", [P, MB, E])
        tab = sb("tab", [P, 3, MB + 1])
        tabi = sb("tabi", [P, 3, MB + 1], I32)
        zeros = sb("zeros", [P, 3 * D])
        DI = sb("DI", [P, 3, D])
        DIT = sb("DIT", [P, 2, 2, KD, P], F32R)
        HT = sb("HT", [P, 2, 2, FC, P], F32R)
        SG, HH = (XN[:, 8 * q:8 * q + 8, :].rearrange("p t d -> p (t d)").rearrange("p (u f) -> p u f", f=F) for q in range(2))
        EO = sb("EO", [P, 2, D])
        GR = W[:, 0:2 * NT * D].bitcast(F32).rearrange("p (t q d) -> p t q d", q=2, d=D)
        rows_in = nc.dram_tensor("f1_rows_in", (MB * P, D), F32).ap()
        rows_out = nc.dram_tensor("f1_rows_out", (MB * P, D), F32).ap()

        ln = LayerNorm(g, ctx, "f1_ln", g.X, XN, g.XT, PS[0:4])
        chain, wg_loaded, w_loaded = sem("chain"), sem("wg_loaded"), [sem(f"w_loaded{i}") for i in range(3)]
        zeroed, cleared, consts = sem("zeroed"), sem("cleared"), sem("consts")
        slots_ready, scattered = sem("slots_ready"), sem("scattered")
        di_loaded = [sem(f"di_loaded{i}") for i in range(3)]
        dtp_ready, dit_ready = sem("dtp_ready"), sem("dit_ready")
        h1_ready, h3_ready, sg_ready, hh_ready = sem("h1_ready"), sem("h3_ready"), sem("sg_ready"), sem("hh_ready")
        htp_ready, ht_ready, eo_ready, eo_copied = sem("htp_ready"), sem("ht_ready"), sem("eo_ready"), sem("eo_copied")
        stored = [sem(f"stored{i}") for i in range(2)]
        gathered = [sem(f"gathered{i}") for i in range(NT // 4)]
        hi_ready, lo_ready, ditl_ready, htl_ready = sem("hi_ready"), sem("lo_ready"), sem("ditl_ready"), sem("htl_ready")
        added, room_free = sem("added"), sem("room_free")

        WPARTS = ("f1_w1", "f1_w3", "f1_w2")

        with nc.Block() as block:
            @block.sync
            def _(sp):
                sp.dma_start(rt.wg[:, :, :], a["f1_wg"]).then_inc(wg_loaded, 16)
                sp.wait_ge(zeroed, 1)
                for q in range(MB // 3):
                    sp.dma_start(rows_in[q * 3 * P:(q + 1) * 3 * P, :].rearrange("(p r) d -> p (r d)", r=3),
                                 zeros[:, :]).then_inc(cleared, 16)
                sp.wait_ge(scattered, 16 * 2 * NT)
                LAG = 4
                for k in range(MB + LAG):
                    if k < MB:
                        if k >= 3:
                            sp.wait_ge(dtp_ready, k - 2)
                        sp.dma_start(DI[:, k % 3, :], rows_in[k * P:(k + 1) * P, :]).then_inc(di_loaded[k % 3], 16)
                    if k >= LAG:
                        o = k - LAG
                        sp.wait_ge(eo_copied, o + 1)
                        sp.dma_start(rows_out[o * P:(o + 1) * P, :], EO[:, o % 2, :]).then_inc(stored[o % 2], 16)
                for n in range(2):
                    sp.wait_ge(stored[n], 16 * ((MB + 1 - n) // 2))

            @block.gpsimd
            def _(pool):
                pool.memset(zeros[:, :], 0.0).then_inc(zeroed, 1)
                rt.pool(pool)
                pool.iota(blk[:, :], pattern=[[1, MB]], base=0, channel_multiplier=0,
                          allow_small_or_imprecise_dtypes=True).then_inc(consts, 1)

                def load(p):
                    if p < 3 * E:
                        pool.dma_start(stage[:, p % 3, :], a[WPARTS[p % 3]][p // 3]).then_inc(w_loaded[p % 3], 16)

                def split(e):
                    for q in range(3):
                        p = 3 * e + q
                        hi = W[:, (e % 2) * 2 * WSZ + q * PART:(e % 2) * 2 * WSZ + (q + 1) * PART]
                        lo = W[:, (e % 2) * 2 * WSZ + WSZ + q * PART:(e % 2) * 2 * WSZ + WSZ + (q + 1) * PART]
                        pool.wait_ge(w_loaded[q], 16 * (e + 1))
                        pool.tensor_tensor(hi, stage[:, q, :], zeros[:, 0:1].to_broadcast([P, PART]), ALU.add).then_inc(hi_ready, 1)
                        pool.wait_ge(hi_ready, p + 1)
                        pool.tensor_tensor(lo, stage[:, q, :], hi.bitcast(F32), ALU.subtract).then_inc(lo_ready, 1)
                        pool.wait_ge(lo_ready, p + 1)
                        load(p + 3)
                for p in range(3):
                    load(p)
                pool.wait_ge(zeroed, 1)
                split(0)
                split(1)
                pool.wait_ge(slots_ready, 1)
                pool.wait_ge(cleared, 16 * (MB // 3))
                for t in range(NT):
                    for q in range(2):
                        pool.indirect_dma_start(out=rows_in, out_offset=bass.IndirectOffsetOnAxis(ap=idx[q][:, t:t + 1], axis=0),
                                                in_=XN[:, t, :], in_offset=None, bounds_check=MB * P - 1,
                                                oob_is_err=False).then_inc(scattered, 16)
                for e in range(2, E):
                    last = pool.value_load(tabi[0:1, 2, e - 2:e - 1], min_val=0, max_val=MB)
                    pool.wait_ge(eo_ready, last + 1)
                    pool.sem_inc(room_free, 1)
                    pool.wait_ge(room_free, e - 1)
                    split(e)
                pool.wait_ge(eo_ready, MB + 1)
                for n in range(2):
                    pool.wait_ge(stored[n], 16 * ((MB + 1 - n) // 2))
                for t in range(NT):
                    for q in range(2):
                        pool.indirect_dma_start(out=GR[:, t, q, :], out_offset=None, in_=rows_out,
                                                in_offset=bass.IndirectOffsetOnAxis(ap=idx[q][:, t:t + 1], axis=0),
                                                bounds_check=MB * P - 1, oob_is_err=False).then_inc(gathered[t // 4], 16)

            @block.tensor
            def _(pe):
                ln.pe(pe)
                pe.wait_ge(wg_loaded, 16)
                rt.pe_logits(pe, ln)
                rt.pe_counts(pe)

                def take_rows(k):
                    pe.wait_ge(di_loaded[k % 3], 16 * (k // 3 + 1))
                    if k >= 1:
                        pe.wait_ge(ditl_ready, k)
                    for kd in range(KD):
                        ins = pe.transpose(PS[6][:, kd * P:(kd + 1) * P], DI[:, k % 3, kd * P:(kd + 1) * P], g.ident[:, :])
                    ins.then_inc(dtp_ready, 1)

                def products(out, hi, lo, at, n, first, last):
                    pe.matmul(out, hi, W[:, ds(at, n)], start=first, stop=False)
                    pe.matmul(out, hi, W[:, ds(at + WSZ, n)], start=False, stop=False)
                    return pe.matmul(out, lo, W[:, ds(at, n)], start=False, stop=last)

                def up(k):
                    ex = pe.value_load(tabi[0:1, 0, k:k + 1], min_val=0, max_val=E - 1)
                    room = pe.value_load(tabi[0:1, 1, k:k + 1], min_val=0, max_val=2 * WSZ)
                    pe.wait_ge(lo_ready, ex * 3 + 2)
                    pe.wait_ge(ditl_ready, k + 1)
                    for w, ready, used in ((0, h1_ready, sg_ready), (1, h3_ready, hh_ready)):
                        if k >= 1:
                            pe.wait_ge(used, k)
                        for hf in range(2):
                            for kd in range(KD):
                                ins = products(PS[2 * w + hf][:, :], DIT[:, 0, k % 2, kd, :], DIT[:, 1, k % 2, kd, :],
                                               room + (w * KD * F + kd * F + hf * 512), 512, kd == 0, kd == KD - 1)
                        ins.then_inc(ready, 1)
                    return ex, room

                def turn(k):
                    pe.wait_ge(hh_ready, k + 1)
                    if k >= 1:
                        pe.wait_ge(htl_ready, 2 * k)
                    for hf in range(2):
                        for c in range(4):
                            f = 4 * hf + c
                            ins = pe.transpose(PS[7 if hf else 4][:, c * P:(c + 1) * P], HH[:, k % 2, f * P:(f + 1) * P], g.ident[:, :])
                        ins.then_inc(htp_ready, 1)

                def down(k, ex, room):
                    pe.wait_ge(lo_ready, ex * 3 + 3)
                    pe.wait_ge(htl_ready, 2 * k + 2)
                    if k >= 1:
                        pe.wait_ge(eo_copied, k)
                    for f in range(FC):
                        ins = products(PS[5][:, 0:D], HT[:, 0, k % 2, f, :], HT[:, 1, k % 2, f, :],
                                       room + (2 * KD * F + f * D), D, f == 0, f == FC - 1)
                    ins.then_inc(eo_ready, 1)

                pe.wait_ge(slots_ready, 1)
                pe.sem_inc(eo_ready, 1)
                take_rows(0)
                for k in range(MB + 1):
                    if k >= 1:
                        turn(k - 1)
                    if k + 1 < MB:
                        take_rows(k + 1)
                    if k < MB:
                        now = up(k)
                    if k >= 1:
                        down(k - 1, *before)
                    before = now

            @block.scalar
            def _(act):
                ln.act(act)
                for q in range(2):
                    act.wait_ge(rt.exp_in, q + 1)
                    act.activation(rt.EX[:, :, :], rt.L[:, :, :], ACT.Exp).then_inc(rt.exp_out, 1)

                def rows(k):
                    act.wait_ge(dtp_ready, k + 1)
                    act.activation(DIT[:, 0, k % 2, :, :], PS[6][:, 0:D].rearrange("p (k n) -> p k n", k=KD), ACT.Copy).then_inc(dit_ready, 1)
                rows(0)
                for k in range(MB + 1):
                    if k >= 1:
                        for hf in range(2):
                            act.wait_ge(htp_ready, 2 * (k - 1) + hf + 1)
                            act.activation(HT[:, 0, (k - 1) % 2, 4 * hf:4 * hf + 4, :], PS[7 if hf else 4][:, :].rearrange("p (c n) -> p c n", c=4),
                                           ACT.Copy).then_inc(ht_ready, 1)
                    if k + 1 < MB:
                        rows(k + 1)
                    if k < MB:
                        act.wait_ge(h1_ready, k + 1)
                        act.activation(SG[:, k % 2, :].rearrange("p (h f) -> p h f", h=2), g.ps[:, 0:2, :], ACT.Silu).then_inc(sg_ready, 1)
                    if k >= 1:
                        act.wait_ge(eo_ready, k + 1)
                        if k >= 3:
                            act.wait_ge(stored[(k - 1) % 2], 16 * ((k - 1) // 2))
                        act.activation(EO[:, (k - 1) % 2, :], PS[5][:, 0:D], ACT.Copy).then_inc(eo_copied, 1)

            @block.vector
            def _(dve):
                ch = Chain(dve, chain)
                ln.dve(dve)
                dve.wait_ge(rt.const, 3)
                dve.wait_ge(rt.logits_ready, 1)
                v3 = lambda x: x[:, :, :]
                lg = PS[4][:, 0:NTE].rearrange("p (t e) -> p t e", e=E)
                ch(dve.tensor_copy(v3(rt.PL), lg))
                ch(dve.tensor_scalar(v3(AB), v3(rt.PL), -1.0, None, ALU.mult))
                ch(dve.tensor_tensor(v3(AB), v3(AB), v3(rt.PL), ALU.max))
                ch(dve.tensor_reduce(m1[:, :], v3(rt.PL), AX_X, ALU.max))

                def weight(m, banned, out, q):
                    ch(dve.tensor_tensor(v3(rt.A2), v3(AB), rt.wide(m), ALU.max))
                    if q:
                        ch(dve.tensor_tensor(v3(rt.L), v3(rt.PL), rt.wide(m), ALU.subtract))
                        ch(dve.tensor_scalar(v3(rt.L), v3(rt.L), 0.0, None, ALU.min))
                        dve.sem_inc(rt.exp_in, 1)
                    else:
                        dve.tensor_tensor(v3(rt.L), v3(rt.PL), rt.wide(m), ALU.subtract).then_inc(rt.exp_in, 1)
                        dve.wait_ge(rt.exp_in, 1)
                    ch(dve.scalar_tensor_tensor(v3(rt.A1), v3(rt.A2), 0.02, v3(rt.L), ALU.mult, ALU.add))
                    ch(dve.tensor_scalar(v3(MK), v3(rt.A1), 0.0, None, ALU.is_ge))
                    if banned is not None:
                        ch(dve.tensor_tensor(v3(rt.A1), v3(MK), banned, ALU.mult))
                        ch(dve.tensor_tensor(v3(MK), v3(MK), v3(rt.A1), ALU.subtract))
                    dve.wait_ge(rt.exp_out, q + 1)
                    ch(dve.tensor_tensor(v3(rt.A1), v3(rt.EX), v3(MK), ALU.mult))
                    ch(dve.tensor_reduce(t1[:, :], v3(rt.A1), AX_X, ALU.add))
                    ch(dve.reciprocal(out, t1[:, :]))

                weight(m1[:, :], None, mult1[:, :], 0)
                ch(dve.tensor_tensor(v3(rt.A2), v3(rt.PL), rt.wide(m1[:, :]), ALU.is_equal))
                rt.dve_first(dve, ch, v3(rt.A2), v3(OH1), low[:, :])
                ch(dve.tensor_scalar(v3(rt.A2), v3(OH1), -3.0e38, None, ALU.mult))
                ch(dve.tensor_tensor(v3(rt.A2), v3(rt.PL), v3(rt.A2), ALU.add))
                ch(dve.tensor_reduce(m2[:, :], v3(rt.A2), AX_X, ALU.max))
                ch(dve.tensor_tensor(v3(rt.A2), v3(rt.A2), rt.wide(m2[:, :]), ALU.is_equal))
                rt.dve_first(dve, ch, v3(rt.A2), v3(OH2), low[:, :])
                weight(m2[:, :], v3(OH1), mult2[:, :], 1)
                ch(dve.tensor_tensor(v3(rt.OH), v3(OH1), v3(OH2), ALU.add))
                rt.dve_places(dve, ch)
                ch(dve.tensor_scalar(nbi[:, :], rt.CUM[:, :, NT - 1], float(P - 1), None, ALU.add))
                ch(dve.tensor_scalar(nbi[:, :], nbi[:, :], 7, None, ALU.arith_shift_right))
                ch(dve.tensor_copy(nb[:, :], nbi[:, :]))
                ch(dve.tensor_tensor_scan(ends[:, :], g.ones[:, 0:E], nb[:, :], 0.0, ALU.mult, ALU.add))
                ch(dve.tensor_tensor(start[:, :], ends[:, :], nb[:, :], ALU.subtract))
                ch(dve.tensor_scalar(start[:, :], start[:, :], float(P), None, ALU.mult))
                ch(dve.tensor_tensor(v3(rt.PL), v3(rt.PL), rt.row(start[:, :]), ALU.add))
                for q, oh in enumerate((OH1, OH2)):
                    ch(dve.tensor_tensor(v3(rt.A1), v3(rt.PL), v3(oh), ALU.mult))
                    ch(dve.tensor_reduce(t1[:, :], v3(rt.A1), AX_X, ALU.add))
                    ch(dve.tensor_copy(idx[q][:, :], t1[:, :]))
                dve.wait_ge(consts, 1)
                ch(dve.tensor_tensor(cmp[:, :, :], blk[:, :].unsqueeze(2).to_broadcast([P, MB, E]),
                                     ends[:, :].unsqueeze(1).to_broadcast([P, MB, E]), ALU.is_ge))
                ch(dve.memset(tab[:, :, :], 0.0))
                ch(dve.tensor_reduce(tab[:, 0, 0:MB], cmp[:, :, :], AX_X, ALU.add))
                ch(dve.tensor_scalar(tab[:, 0, 0:MB], tab[:, 0, 0:MB], float(E - 1), None, ALU.min))
                ch(dve.tensor_copy(tabi[:, 0, :], tab[:, 0, :]))
                ch(dve.tensor_scalar(tabi[:, 1, :], tabi[:, 0, :], 1, None, ALU.bitwise_and))
                ch(dve.tensor_copy(tab[:, 1, :], tabi[:, 1, :]))
                ch(dve.tensor_scalar(tab[:, 1, :], tab[:, 1, :], float(2 * WSZ), None, ALU.mult))
                ch(dve.tensor_copy(tab[:, 2, 0:E], ends[:, :]))
                ch(dve.tensor_copy(tabi[:, 1:3, :], tab[:, 1:3, :]))
                dve.sem_inc(slots_ready, 1)

                def rows_lo(k):
                    dve.wait_ge(dit_ready, k + 1)
                    dve.tensor_tensor(DIT[:, 1, k % 2, :, :], PS[6][:, 0:D].rearrange("p (k n) -> p k n", k=KD),
                                      DIT[:, 0, k % 2, :, :].bitcast(F32), ALU.subtract).then_inc(ditl_ready, 1)
                rows_lo(0)
                for k in range(MB + 1):
                    if k >= 1:
                        for hf in range(2):
                            dve.wait_ge(ht_ready, 2 * (k - 1) + hf + 1)
                            dve.tensor_tensor(HT[:, 1, (k - 1) % 2, 4 * hf:4 * hf + 4, :], PS[7 if hf else 4][:, :].rearrange("p (c n) -> p c n", c=4),
                                              HT[:, 0, (k - 1) % 2, 4 * hf:4 * hf + 4, :].bitcast(F32), ALU.subtract).then_inc(htl_ready, 1)
                    if k + 1 < MB:
                        rows_lo(k + 1)
                    if k < MB:
                        dve.wait_ge(sg_ready, k + 1)
                        dve.wait_ge(h3_ready, k + 1)
                        dve.tensor_tensor(HH[:, k % 2, :].rearrange("p (h f) -> p h f", h=2), SG[:, k % 2, :].rearrange("p (h f) -> p h f", h=2),
                                          g.ps[:, 2:4, :], ALU.mult).then_inc(hh_ready, 1)
                for t in range(NT):
                    if t % 4 == 0:
                        dve.wait_ge(gathered[t // 4], 16 * 8)
                    dve.scalar_tensor_tensor(g.X[:, t, :], GR[:, t, 0, :], mult1[:, t:t + 1], g.X[:, t, :], ALU.mult,
                                             ALU.add).then_inc(added, 1)
                for t in range(NT):
                    dve.wait_ge(added, t + 1)
                    dve.scalar_tensor_tensor(g.X[:, t, :], GR[:, t, 1, :], mult2[:, t:t + 1], g.X[:, t, :], ALU.mult, ALU.add)


CL = 32
NC = S // CL
PAIRS, HDW = 4, 64
ETA, DT_STEP, FLOOR = 0.1, 0.01, 0.1


def mixer1(g, a):
    nc = g.nc
    with ExitStack() as ctx:
        Hrow = ctx.enter_context(nc.sbuf_tensor("Hrow", [P, NT, D], F32))
        XN = ctx.enter_context(nc.sbuf_tensor("h_XN", [P, NT, D], F32))
        gamma = ctx.enter_context(nc.sbuf_tensor("gamma", [P, NT], F32))
        resolvent(g, a, Hrow, XN, gamma)
        g.end_stage()
        hebbian(g, a, Hrow, XN, gamma)
        g.end_stage()
        gelu_ffn(g, a, Hrow, XN)


def resolvent(g, a, Hrow, XN, gamma):
    nc, PS = g.nc, g.PS
    with ExitStack() as ctx:
        sb = lambda n, s, dt=F32: ctx.enter_context(nc.sbuf_tensor("r_" + n, s, dt))
        sem = g.semaphores("r_")
        g1, b1 = sb("g1", [P, KD]), sb("b1", [P, KD])
        w_pot, b_pot = sb("w_pot", [P, KD, 2]), sb("b_pot", [2, 1])
        w_bk = sb("w_bk", [3, D])
        POT = sb("POT", [2, T])
        CH = sb("CH", [P, 2, CL])
        Dn = sb("Dn", [P, 2, CL])
        DD = sb("DD", [P, 2, CL])
        nDi = sb("nDi", [P, CL])
        sp = sb("sp", [P, 5, CL])
        sg = sb("sg", [P, 5, NT])
        M = sb("M", [P, 3, 2, 2])
        tm, mx, rc = sb("tm", [P, 2, 2]), sb("mx", [P, 1]), sb("rc", [P, 1])
        MM = sb("MM", [P, 2, 2, 2])
        Q = sb("Q", [34, NC, 2, 2, 2])
        RM = sb("RM", [34, NC, 2, 2, 2, 2])
        W = sb("W", [34, NC + 1, 4])
        wt, wm, wr = sb("wt", [34, 4, 4]), sb("wm", [34, 1]), sb("wr", [34, 1])
        uu, un, ia, ib = sb("uu", [34, NC, 2]), sb("un", [34, NC]), sb("ia", [34, NC]), sb("ib", [34, NC])
        IA = sb("IA", [34, NC, 2])
        A0 = sb("A0", [P, 2])
        AA = sb("AA", [P, 2, CL])
        B2 = sb("B2", [64, 2, CL])
        sq, nrm, rn, GG = sb("sq", [P, 2]), sb("nrm", [P, 1]), sb("rn", [P, 1]), sb("GG", [64, 2, CL])
        s2, sn = sb("s2", [64, 2, CL]), sb("sn", [64, CL])
        GR = sb("GR", [3, T])

        ln0 = LayerNorm(g, ctx, "r_ln0", g.X, Hrow, None, None)
        ln1 = LayerNorm(g, ctx, "r_ln1", Hrow, XN, g.XT, PS[0:4], g1, b1)
        loaded, chain, act_chain = sem("loaded"), sem("chain"), sem("act_chain")
        pot_ready, pot_copied, ch_loaded = sem("pot_ready"), sem("pot_copied"), sem("ch_loaded")
        potT_ready, abs_in, abs_out = sem("potT_ready"), sem("abs_in"), sem("abs_out")
        ones_ready, mm_ready, q_loaded = sem("ones_ready"), sem("mm_ready"), sem("q_loaded")
        ia_ready, a0_loaded, aa_ready, b2_loaded = sem("ia_ready"), sem("a0_loaded"), sem("aa_ready"), sem("b2_loaded")
        gg_ready, gr_loaded, f_ready, f_used = sem("gg_ready"), sem("gr_loaded"), sem("f_ready"), sem("f_used")
        names = [(g1[:, :], "h_g1"), (b1[:, :], "h_b1"), (w_pot[:, :, :], "h_w_pot"), (b_pot[:, :], "h_b_pot"), (w_bk[:, :], "h_w_bk")]

        with nc.Block() as block:
            @block.sync
            def _(s):
                for dst, name in names:
                    s.dma_start(dst, a[name]).then_inc(loaded, 16)
                s.wait_ge(pot_copied, 4)
                for half in range(2):
                    for r in range(2):
                        s.dma_start(CH[64 * half:64 * half + 64, r, :], POT[r:r + 1, :].rearrange("a (p i) -> a p i", i=CL)).then_inc(ch_loaded, 16)
                s.wait_ge(ones_ready, 2)
                s.wait_ge(mm_ready, 1)
                for half in range(2):
                    for b in range(B):
                        lo = 64 * half + NC * b
                        s.dma_start(Q[32 * half + b:32 * half + b + 1, :, :, :, :].rearrange("a c x y z -> a c (x y z)"),
                                    MM[lo:lo + NC, :, :, :].rearrange("p x y z -> p (x y z)")).then_inc(q_loaded, 16)
                s.wait_ge(ia_ready, 1)
                for half in range(2):
                    for b in range(B):
                        lo = 64 * half + NC * b
                        s.dma_start(A0[lo:lo + NC, :], IA[32 * half + b:32 * half + b + 1, :, :]).then_inc(a0_loaded, 16)
                s.wait_ge(aa_ready, 1)
                s.dma_start(B2[:, :, :], AA[64:128, :, :]).then_inc(b2_loaded, 16)
                s.wait_ge(gg_ready, 1)
                for r in range(2):
                    s.dma_start(GR[r:r + 1, :].rearrange("a (p i) -> a p i", i=CL), GG[:, r, :]).then_inc(gr_loaded, 16)

            @block.gpsimd
            def _(pool):
                pool.memset(GR[:, :], 1.0).then_inc(ones_ready, 1)
                pool.memset(Q[:, :, :, :, :], 0.0).then_inc(ones_ready, 1)

            @block.tensor
            def _(pe):
                ln1.pe(pe)
                pe.wait_ge(loaded, 16 * len(names))
                for j in range(4):
                    pe.wait_ge(ln1.xt_ready, 4 * j + 4)
                    for kd in range(KD):
                        ins = pe.matmul(PS[4 + j][0:2, :], w_pot[:, kd, :], g.XT[:, kd, j * 512:(j + 1) * 512],
                                        start=(kd == 0), stop=(kd == KD - 1))
                    ins.then_inc(pot_ready, 1)
                pe.wait_ge(pot_copied, 4)
                pe.wait_ge(ln1.xt_ready, NT)
                for t in range(NT):
                    ins = pe.transpose(PS[0][:, 2 * t:2 * t + 2], POT[:, t * P:(t + 1) * P], g.ident[0:2, 0:2])
                ins.then_inc(potT_ready, 1)
                pe.wait_ge(gr_loaded, 32)
                for t in range(NT):
                    if t >= 2:
                        pe.wait_ge(f_used, t - 1)
                    pe.matmul(PS[1 + t % 2][:, 0:D], GR[:, t * P:(t + 1) * P], w_bk[:, :], start=True, stop=True).then_inc(f_ready, 1)

            @block.scalar
            def _(act):
                ch = Chain(act, act_chain)
                ln0.act(act)
                act.wait_ge(loaded, 16 * len(names))
                ln1.act(act)
                for j in range(4):
                    act.wait_ge(pot_ready, j + 1)
                    act.activation(POT[:, j * 512:(j + 1) * 512], PS[4 + j][0:2, :], ACT.Identity, bias=b_pot[:, 0:1]).then_inc(pot_copied, 1)
                for q, t in enumerate((sp, sg)):
                    act.wait_ge(abs_in, q + 1)
                    ch(act.activation(t[:, 1, :], t[:, 0, :], ACT.Abs))
                    ch(act.activation(t[:, 2, :], t[:, 1, :], ACT.Exp, scale=-1.0))
                    act.activation(t[:, 3, :], t[:, 2, :], ACT.Ln, bias=1.0).then_inc(abs_out, 1)

            @block.vector
            def _(dve):
                ch = Chain(dve, chain)
                ln0.dve(dve)
                dve.wait_ge(ln0.xn_ready, NT)
                ln1.dve(dve)

                def softplus(t, q, out):
                    dve.sem_inc(abs_in, 1)
                    dve.wait_ge(abs_out, q + 1)
                    ch(dve.tensor_scalar(t[:, 4, :], t[:, 2, :], 1.0, None, ALU.add))
                    ch(dve.scalar_tensor_tensor(t[:, 4, :], t[:, 4, :], 1.0, t[:, 2, :], ALU.subtract, ALU.subtract))
                    ch(dve.tensor_tensor(t[:, 4, :], t[:, 3, :], t[:, 4, :], ALU.subtract))
                    ch(dve.scalar_tensor_tensor(t[:, 4, :], t[:, 0, :], 0.0, t[:, 4, :], ALU.max, ALU.add))
                    ch(dve.tensor_scalar(out, t[:, 4, :], FLOOR, None, ALU.add))

                dve.wait_ge(ch_loaded, 64)
                ch(dve.tensor_copy(sp[:, 0, :], CH[:, 1, :]))
                softplus(sp, 0, nDi[:, :])
                ch.add(dve.tensor_scalar(Dn[:, 0, :], CH[:, 0, :], 2.0, None, ALU.add))
                ch.add(dve.tensor_scalar(Dn[:, 1, :], nDi[:, :], -1.0, None, ALU.mult))
                ch.sync()
                ch.add(dve.tensor_copy(DD[0:64, :, :], Dn[0:64, :, :]))
                ch.add(dve.tensor_copy(DD[64:128, :, :], Dn[64:128, :, ::-1]))
                ch.sync()
                ch(dve.tensor_scalar(nDi[:, :], DD[:, 1, :], -1.0, None, ALU.mult))
                ch.add(dve.memset(M[:, :, :, :], 0.0))
                ch.sync()
                ch.add(dve.memset(M[:, 0, 0, 0:1], 1.0))
                ch.add(dve.memset(M[:, 2, 0, 1:2], 1.0))
                ch.sync()

                def rescale(x):
                    ch(dve.tensor_reduce(mx[:, :], x, AX_X, ALU.max, apply_absolute_value=True))
                    ch(dve.reciprocal(rc[:, :], mx[:, :]))
                    ch(dve.tensor_scalar(x, x, rc[:, 0:1], None, ALU.mult))
                for k in range(CL):
                    cur, new, old = M[:, k % 3, :, :], M[:, (k + 1) % 3, :, :], M[:, (k + 2) % 3, :, :]
                    ch(dve.scalar_tensor_tensor(tm[:, :, :], cur, DD[:, 0, k:k + 1], old, ALU.mult, ALU.subtract))
                    ch.add(dve.scalar_tensor_tensor(new[:, 0, :], cur[:, 1, :], nDi[:, k:k + 1], tm[:, 0, :], ALU.mult, ALU.add))
                    ch.add(dve.scalar_tensor_tensor(new[:, 1, :], cur[:, 0, :], DD[:, 1, k:k + 1], tm[:, 1, :], ALU.mult, ALU.add))
                    ch.sync()
                    if k % 8 == 7:
                        rescale(M[:, :, :, :].rearrange("p k c s -> p (k c s)"))
                dve.tensor_copy(MM[:, 0, :, :], M[:, CL % 3, :, :])
                dve.tensor_copy(MM[:, 1, :, :], M[:, (CL + 2) % 3, :, :]).then_inc(mm_ready, 1)
                dve.wait_ge(potT_ready, 1)
                ch(dve.tensor_copy(sg[:, 0, :], PS[0][:, 1:2 * NT:2]))
                softplus(sg, 1, gamma[:, :])
                dve.wait_ge(q_loaded, 64)
                dve.wait_ge(ones_ready, 2)
                for lo, hi, rev in ((0, 32, False), (32, 34, True)):
                    src = Q[lo:hi, ::-1] if rev else Q[lo:hi, :]
                    for rr, cc, comp, sign in ((0, 0, 0, 1.0), (0, 1, 1, -1.0), (1, 0, 1, 1.0), (1, 1, 0, 1.0)):
                        for x in range(2):
                            ch.add(dve.tensor_scalar(RM[lo:hi, :, x, rr, :, cc], src[:, :, x, comp, :], sign, None, ALU.mult))
                ch.add(dve.memset(W[:, :, :], 0.0))
                ch.sync()
                ch(dve.memset(W[:, 0, 0:1], 1.0))
                for j in range(NC):
                    ch(dve.tensor_tensor(wt[:, :, :], RM[:, j, :, :, :, :].rearrange("p x r s c -> p (x r) (s c)"),
                                         W[:, j, :].unsqueeze(1).to_broadcast([34, 4, 4]), ALU.mult))
                    ch(dve.tensor_reduce(W[:, j + 1, :], wt[:, :, :], AX_X, ALU.add))
                    if j % 4 == 3:
                        w = W[:, j + 1, :]
                        ch(dve.tensor_reduce(wm[:, :], w, AX_X, ALU.max, apply_absolute_value=True))
                        ch(dve.tensor_scalar(wm[:, :], wm[:, :], 1e-30, None, ALU.max))
                        ch(dve.reciprocal(wr[:, :], wm[:, :]))
                        ch(dve.tensor_scalar(w, w, wr[:, 0:1], None, ALU.mult))
                u, v = W[:, 0:NC, 0:2], W[:, 0:NC, 2:4]
                ch.add(dve.tensor_tensor(uu[:, :, :], u, u, ALU.mult))
                ch.sync()
                ch(dve.tensor_tensor(un[:, :], uu[:, :, 0], uu[:, :, 1], ALU.add))
                ch(dve.tensor_scalar(un[:, :], un[:, :], 1e-37, None, ALU.max))
                ch(dve.reciprocal(un[:, :], un[:, :]))
                for comp, p0, p1, op in ((0, (0, 0), (1, 1), ALU.add), (1, (1, 0), (0, 1), ALU.subtract)):
                    ch.add(dve.tensor_tensor(ia[:, :], v[:, :, p0[0]], u[:, :, p0[1]], ALU.mult))
                    ch.add(dve.tensor_tensor(ib[:, :], v[:, :, p1[0]], u[:, :, p1[1]], ALU.mult))
                    ch.sync()
                    ch(dve.tensor_tensor(ia[:, :], ia[:, :], ib[:, :], op))
                    ch.add(dve.tensor_tensor(IA[0:32, :, comp], ia[0:32, :], un[0:32, :], ALU.mult))
                    ch.add(dve.tensor_tensor(IA[32:34, ::-1, comp], ia[32:34, :], un[32:34, :], ALU.mult))
                    ch.sync()
                dve.sem_inc(ia_ready, 1)
                dve.wait_ge(a0_loaded, 64)
                ch(dve.tensor_tensor(AA[:, :, 0], DD[:, :, 0], A0[:, :], ALU.subtract))
                for k in range(1, CL):
                    ch(dve.tensor_tensor(sq[:, :], AA[:, :, k - 1], AA[:, :, k - 1], ALU.mult))
                    ch(dve.tensor_reduce(nrm[:, :], sq[:, :], AX_X, ALU.add))
                    ch(dve.reciprocal(rn[:, :], nrm[:, :]))
                    ch.add(dve.scalar_tensor_tensor(AA[:, 1, k:k + 1], AA[:, 1, k - 1:k], rn[:, 0:1], DD[:, 1, k:k + 1], ALU.mult, ALU.add))
                    ch(dve.tensor_tensor(sq[:, 0:1], AA[:, 0, k - 1:k], rn[:, 0:1], ALU.mult))
                    ch(dve.tensor_tensor(AA[:, 0, k:k + 1], DD[:, 0, k:k + 1], sq[:, 0:1], ALU.subtract))
                dve.sem_inc(aa_ready, 1)
                dve.wait_ge(b2_loaded, 16)
                ch(dve.tensor_tensor(s2[:, :, :], AA[0:64, :, :], B2[:, :, ::-1], ALU.add))
                ch(dve.tensor_tensor(s2[:, :, :], s2[:, :, :], Dn[0:64, :, :], ALU.subtract))
                ch(dve.tensor_tensor(GG[:, :, :], s2[:, :, :], s2[:, :, :], ALU.mult))
                ch(dve.tensor_tensor(sn[:, :], GG[:, 0, :], GG[:, 1, :], ALU.add))
                ch(dve.reciprocal(sn[:, :], sn[:, :]))
                ch.add(dve.tensor_tensor(GG[:, 0, :], s2[:, 0, :], sn[:, :], ALU.mult))
                ch.add(dve.scalar_tensor_tensor(GG[:, 1, :], s2[:, 1, :], -1.0, sn[:, :], ALU.mult, ALU.mult))
                ch.sync()
                dve.sem_inc(gg_ready, 1)
                for t in range(NT):
                    dve.wait_ge(f_ready, t + 1)
                    dve.tensor_tensor(Hrow[:, t, :], Hrow[:, t, :], PS[1 + t % 2][:, 0:D], ALU.add).then_inc(f_used, 1)


def hebbian(g, a, Hrow, XN, gamma):
    nc, PS, ps = g.nc, g.PS, g.ps
    NP = PAIRS
    with ExitStack() as ctx:
        sb = lambda n, s, dt=F32: ctx.enter_context(nc.sbuf_tensor("h_" + n, s, dt))
        sem = g.semaphores("h_")
        g2, b2 = sb("g2", [P, KD]), sb("b2", [P, KD])
        w_qkv, w_out = sb("w_qkv", [P, KD, 3 * NP * P]), sb("w_out", [P, NP, D])
        b_qk, b_v, b_out = sb("b_qk", [P, 2 * NP]), sb("b_v", [P, NP * P]), sb("b_out", [P, D])
        blockd = sb("blockd", [P, P])
        Lc, Lt = sb("Lc", [P, NT]), sb("Lt", [P, NT])
        EB = sb("EB", [P, NT, P])
        DM = sb("DM", [P, NT, P])
        ks, dec = sb("ks", [P, NT]), sb("dec", [P, NT])
        QK = sb("QK", [P, 2, 2 * NP, 512])
        VV = sb("VV", [P, 2, NP * P])
        VP = sb("VP", [P, 2, 2 * NP, P])
        KS = sb("KS", [P, 2, NP * P])
        QS = sb("QS", [P, 2, NP, P])
        PTm = sb("PTm", [P, 2, 2 * NP, P])
        HB = sb("HB", [P, 2, NP, P])
        WS = sb("WS", [P, NP, P])
        KVm = sb("KVm", [P, NP, P])
        ln = LayerNorm(g, ctx, "h_ln", Hrow, XN, g.XT, PS[0:4], g2, b2)
        loaded, chain, act_chain, consts = sem("loaded"), sem("chain"), sem("act_chain"), sem("consts")
        lc_ready, lc_copied, lb_ready, lb_used, dm_in, dm_out, eb_ready = (
            sem(n) for n in ("lc_ready", "lc_copied", "lb_ready", "lb_used", "dm_in", "dm_out", "eb_ready"))
        bo_added, ws_clear = sem("bo_added"), sem("ws_clear")
        qk_ready, qk_used, v_ready, vv_ready, vp_ready = (sem(n) for n in ("qk_ready", "qk_used", "v_ready", "vv_ready", "vp_ready"))
        kt_ready, ks_ready, s_ready, pt_ready, qs_ready = (sem(n) for n in ("kt_ready", "ks_ready", "s_ready", "pt_ready", "qs_ready"))
        o_ready, hb_ready, kv_ready, ws_ready, y_ready, y_used = (
            sem(n) for n in ("o_ready", "hb_ready", "kv_ready", "ws_ready", "y_ready", "y_used"))
        names = [(g2[:, :], "h_g2"), (b2[:, :], "h_b2"), (w_qkv[:, :, :], "h_w_qkv"), (w_out[:, :, :], "h_w_out"),
                 (b_qk[:, :], "h_b_qk"), (b_v[:, :], "h_b_v"), (b_out[:, :], "h_b_out")]
        ALL = 16 * len(names)
        GT = 4

        with nc.Block() as block:
            @block.sync
            def _(s):
                for dst, name in names:
                    src = a[name]
                    if src.shape[0] == 1:
                        src = src.to_broadcast([P, src.shape[1]])
                    s.dma_start(dst, src).then_inc(loaded, 16)

            @block.gpsimd
            def _(pool):
                pool.memset(blockd[:, :], 0.0).then_inc(consts, 1)
                pool.memset(VP[:, :, :, :], 0.0).then_inc(consts, 1)
                pool.wait_ge(consts, 2)
                pool.memset(blockd[0:HDW, 0:HDW], 1.0).then_inc(consts, 1)
                pool.wait_ge(consts, 3)
                pool.memset(blockd[HDW:P, HDW:P], 1.0).then_inc(consts, 1)
                pool.wait_ge(consts, 4)
                pool.wait_ge(loaded, ALL)
                for t in range(NT):
                    pool.wait_ge(ln.xn_ready, t + 1)
                    pool.tensor_tensor(Hrow[:, t, :], Hrow[:, t, :], b_out[:, :], ALU.add).then_inc(bo_added, 1)
                for t in range(NT):
                    r = t % 2
                    pool.wait_ge(vv_ready, t + 1)
                    if t >= 2:
                        pool.wait_ge(o_ready, t - 1)
                    v = VV[:, r, :].rearrange("p (q h e) -> p q h e", h=2, e=HDW)
                    vp = VP[:, r, :, :].rearrange("p (q h) e -> p q h e", h=2)
                    pool.tensor_copy(vp[:, :, 0, 0:HDW], v[:, :, 0, :]).then_inc(vp_ready, 1)
                    pool.tensor_copy(vp[:, :, 1, HDW:P], v[:, :, 1, :]).then_inc(vp_ready, 1)
                    pool.wait_ge(qk_used, 8 * (t // GT + 1))
                    pool.wait_ge(eb_ready, 4)
                    tt = t % GT
                    pool.tensor_tensor(QS[:, r, :, :], QK[:, (t // GT) % 2, 0:NP, tt * P:(tt + 1) * P],
                                       EB[:, t:t + 1, :].to_broadcast([P, NP, P]), ALU.mult).then_inc(qs_ready, 1)

            @block.tensor
            def _(pe):
                ln.pe(pe)
                pe.matmul(PS[4][:, 0:NT], g.upper[:, :], gamma[:, :], start=True, stop=True).then_inc(lc_ready, 1)
                pe.matmul(PS[5][:, 0:NT], g.ones[:, :], gamma[:, :], start=True, stop=True).then_inc(lc_ready, 1)
                for j in range(4):
                    if j >= 2:
                        pe.wait_ge(lb_used, j - 1)
                    for c in range(4):
                        t = 4 * j + c
                        ins = pe.matmul(PS[6 + j % 2][:, c * P:(c + 1) * P], gamma[:, t:t + 1].to_broadcast([P, P]), g.upper[:, :],
                                        start=True, stop=True)
                    ins.then_inc(lb_ready, 1)
                pe.wait_ge(loaded, ALL)

                def group(j):
                    pe.wait_ge(ln.xt_ready, GT * (j + 1) if j else NT)
                    for f in range(2 * NP):
                        n = 8 * j + f
                        if n >= 2:
                            pe.wait_ge(qk_used, n - 1)
                        for kd in range(KD):
                            ins = pe.matmul(PS[n % 2][:, :], w_qkv[:, kd, f * P:(f + 1) * P], g.XT[:, kd, j * 512:(j + 1) * 512],
                                            start=(kd == 0), stop=(kd == KD - 1))
                        ins.then_inc(qk_ready, 1)

                def tile_in(t):
                    r, tt = (t // GT) % 2, t % GT
                    if t >= 1:
                        pe.wait_ge(vv_ready, t)
                    for kd in range(KD):
                        ins = pe.matmul(PS[2][:, :], g.XT[:, kd, t * P:(t + 1) * P], w_qkv[:, kd, 2 * NP * P:3 * NP * P],
                                        start=(kd == 0), stop=(kd == KD - 1))
                    ins.then_inc(v_ready, 1)
                    pe.wait_ge(qk_used, 8 * (t // GT + 1))
                    if t >= 1:
                        pe.wait_ge(ks_ready, t)
                    if t >= 2:
                        pe.wait_ge(y_used, t - 1)
                    for q in range(NP):
                        ins = pe.transpose(PS[3][:, q * P:(q + 1) * P], QK[:, r, NP + q, tt * P:(tt + 1) * P], g.ident[:, :])
                    ins.then_inc(kt_ready, 1)
                    if t >= 1:
                        pe.wait_ge(pt_ready, t)
                    else:
                        pe.wait_ge(lc_copied, 2)
                    for h in range(2 * NP):
                        q, lo = h // 2, HDW * (h % 2)
                        ins = pe.matmul(PS[4 + h % 2][:, q * P:(q + 1) * P], QK[lo:lo + HDW, r, NP + q, tt * P:(tt + 1) * P],
                                        QK[lo:lo + HDW, r, q, tt * P:(tt + 1) * P], start=True, stop=True)
                    ins.then_inc(s_ready, 1)

                def tile_out(t):
                    r = t % 2
                    pe.wait_ge(pt_ready, t + 1)
                    pe.wait_ge(vp_ready, 2 * (t + 1))
                    pe.wait_ge(qs_ready, t + 1)
                    if t >= 1:
                        pe.wait_ge(hb_ready, t)
                        pe.wait_ge(ws_ready, t)
                    else:
                        pe.wait_ge(lb_used, 4)
                        pe.wait_ge(consts, 4)
                        pe.wait_ge(ws_clear, 1)
                    for q in range(NP):
                        out = PS[6][:, q * P:(q + 1) * P]
                        for h in range(2):
                            pe.matmul(out, VP[:, r, 2 * q + h, :], PTm[:, r, h * NP + q, :], start=(h == 0), stop=False)
                        ins = pe.matmul(out, WS[:, q, :], QS[:, r, q, :], start=False, stop=True)
                    ins.then_inc(o_ready, 1)
                    pe.wait_ge(ks_ready, t + 1)
                    for q in range(NP):
                        ins = pe.matmul(PS[7][:, q * P:(q + 1) * P], KS[:, r, q * P:(q + 1) * P], VV[:, r, q * P:(q + 1) * P],
                                        start=True, stop=True)
                    ins.then_inc(kv_ready, 1)
                    pe.wait_ge(hb_ready, t + 1)
                    pe.wait_ge(ks_ready, min(t + 2, NT))
                    if t == NT - 1:
                        pe.wait_ge(y_used, t)
                    for q in range(NP):
                        ins = pe.matmul(PS[3][:, 0:D], HB[:, r, q, :], w_out[:, q, :], start=(q == 0), stop=(q == NP - 1))
                    ins.then_inc(y_ready, 1)
                for t in range(NT + 1):
                    if t < NT and t % GT == 0:
                        group(t // GT)
                    if t < NT:
                        tile_in(t)
                    if t >= 1:
                        tile_out(t - 1)

            @block.scalar
            def _(act):
                ch = Chain(act, act_chain)
                act.wait_ge(loaded, ALL)
                ln.act(act)
                for q, (dst, bank) in enumerate(((Lc, 4), (Lt, 5))):
                    act.wait_ge(lc_ready, q + 1)
                    act.activation(dst[:, :], PS[bank][:, 0:NT], ACT.Copy).then_inc(lc_copied, 1)
                for j in range(4):
                    act.wait_ge(lb_ready, j + 1)
                    act.activation(EB[:, 4 * j:4 * j + 4, :], PS[6 + j % 2][:, :].rearrange("p (t n) -> p t n", n=P), ACT.Exp,
                                   scale=-DT_STEP).then_inc(eb_ready, 1)
                act.wait_ge(dm_in, 1)
                act.activation(DM[:, :, :], DM[:, :, :], ACT.Exp, scale=-DT_STEP)
                act.activation(ks[:, :], ks[:, :], ACT.Exp, scale=-DT_STEP)
                act.activation(dec[:, :], Lt[:, :], ACT.Exp, scale=-DT_STEP).then_inc(dm_out, 1)
                for t in range(NT + 1):
                    if t < NT and t % GT == 0:
                        for f in range(2 * NP):
                            n = 8 * (t // GT) + f
                            act.wait_ge(qk_ready, n + 1)
                            act.activation(QK[:, (t // GT) % 2, f, :], PS[n % 2][:, :], ACT.Identity, bias=b_qk[:, f:f + 1]).then_inc(qk_used, 1)
                    if t < NT:
                        act.wait_ge(kt_ready, t + 1)
                        if t == 0:
                            act.wait_ge(dm_out, 2)
                        if t >= 2:
                            act.wait_ge(kv_ready, t - 1)
                        act.activation(KS[:, t % 2, :], PS[3][:, :], ACT.Copy, scale=ks[:, t:t + 1]).then_inc(ks_ready, 1)
                    if t >= 1:
                        act.wait_ge(o_ready, t)
                        if t >= 3:
                            act.wait_ge(y_ready, t - 2)
                        act.activation(HB[:, (t - 1) % 2, :, :], PS[6][:, :].rearrange("p (q n) -> p q n", n=P), ACT.Copy).then_inc(hb_ready, 1)

            @block.vector
            def _(dve):
                ch = Chain(dve, chain)
                ln.dve(dve)
                dve.wait_ge(lc_copied, 2)
                for j in range(4):
                    dve.wait_ge(eb_ready, j + 1)
                    for c in range(4):
                        t = 4 * j + c
                        ins = dve.tensor_scalar(DM[:, t, :], PS[6 + j % 2][:, c * P:(c + 1) * P], Lc[:, t:t + 1], 0.0,
                                                ALU.subtract, ALU.max)
                    ins.then_inc(lb_used, 1)
                dve.tensor_tensor(ks[:, :], Lt[:, :], Lc[:, :], ALU.subtract).then_inc(dm_in, 1)
                dve.wait_ge(dm_out, 1)
                ch.add(dve.tensor_scalar(ks[:, :], ks[:, :], ETA, None, ALU.mult))
                ch.add(dve.tensor_scalar(DM[:, :, :], DM[:, :, :], ETA, None, ALU.mult))
                ch.sync()
                ch(dve.tensor_tensor(DM[:, :, :], DM[:, :, :], g.upper[:, :].unsqueeze(1).to_broadcast([P, NT, P]), ALU.mult))
                dve.sem_inc(dm_out, 1)
                dve.memset(WS[:, :, :], 0.0).then_inc(ws_clear, 1)
                dve.wait_ge(consts, 4)
                dve.wait_ge(ws_clear, 1)
                dve.wait_ge(loaded, ALL)

                def tile_in(t):
                    r = t % 2
                    dve.wait_ge(v_ready, t + 1)
                    if t >= 2:
                        dve.wait_ge(kv_ready, t - 1)
                        dve.wait_ge(vp_ready, 2 * (t - 1))
                    dve.tensor_tensor(VV[:, r, :], PS[2][:, :], b_v[:, :], ALU.add).then_inc(vv_ready, 1)
                    dve.wait_ge(s_ready, t + 1)
                    if t >= 2:
                        dve.wait_ge(o_ready, t - 1)
                    dve.tensor_tensor(PTm[:, r, :, :], ps[:, 4:6, :].rearrange("p b (h n) -> p (b h) n", n=P),
                                      DM[:, t:t + 1, :].to_broadcast([P, 2 * NP, P]), ALU.mult).then_inc(pt_ready, 1)

                def tile_out(t):
                    dve.wait_ge(kv_ready, t + 1)
                    dve.wait_ge(o_ready, t + 1)
                    if t % TB == TB - 1:
                        dve.memset(WS[:, :, :], 0.0).then_inc(ws_ready, 1)
                    else:
                        ch(dve.tensor_tensor(KVm[:, :, :], PS[7][:, :].rearrange("p (q n) -> p q n", n=P),
                                             blockd[:, :].unsqueeze(1).to_broadcast([P, NP, P]), ALU.mult))
                        dve.scalar_tensor_tensor(WS[:, :, :], WS[:, :, :], dec[:, t:t + 1], KVm[:, :, :], ALU.mult, ALU.add).then_inc(ws_ready, 1)
                    dve.wait_ge(ws_ready, t + 1)
                    dve.wait_ge(y_ready, t + 1)
                    dve.tensor_tensor(Hrow[:, t, :], Hrow[:, t, :], PS[3][:, 0:D], ALU.add).then_inc(y_used, 1)

                dve.wait_ge(bo_added, NT)
                for t in range(NT + 1):
                    if t < NT:
                        tile_in(t)
                    if t >= 1:
                        tile_out(t - 1)


def gelu_ffn(g, a, Hrow, XN):
    nc, PS = g.nc, g.PS
    with ExitStack() as ctx:
        sb = lambda n, s, dt=F32: ctx.enter_context(nc.sbuf_tensor("g_" + n, s, dt))
        sem = g.semaphores("g_")
        g3, b3 = sb("g3", [P, KD]), sb("b3", [P, KD])
        w1, w2 = sb("w1", [P, KD, F]), sb("w2", [P, FC, D])
        bf1, bf2 = sb("bf1", [P, FC]), sb("bf2", [P, D])
        GH = sb("GH", [P, 2, FC, 512])
        ln = LayerNorm(g, ctx, "g_ln", Hrow, XN, g.XT, PS[0:4], g3, b3)
        loaded, sums = sem("loaded"), sem("sums")
        h_ready, h_used, y_ready, y_used = sem("h_ready"), sem("h_used"), sem("y_ready"), sem("y_used")
        names = [(g3[:, :], "h_g3"), (b3[:, :], "h_b3"), (w1[:, :, :], "h_w_ff1"), (w2[:, :, :], "h_w_ff2"),
                 (bf1[:, :], "h_b_ff1"), (bf2[:, :], "h_b_ff2")]
        ALL = 16 * len(names)
        with nc.Block() as block:
            @block.sync
            def _(s):
                for dst, name in names:
                    src = a[name]
                    if src.shape[0] == 1:
                        src = src.to_broadcast([P, src.shape[1]])
                    s.dma_start(dst, src).then_inc(loaded, 16)

            @block.gpsimd
            def _(pool):
                pool.wait_ge(loaded, ALL)
                for t in range(NT):
                    pool.tensor_tensor(g.X[:, t, :], g.X[:, t, :], bf2[:, :], ALU.add).then_inc(sums, 1)
                for t in range(NT):
                    pool.wait_ge(sums, NT + t)
                    pool.tensor_tensor(g.X[:, t, :], g.X[:, t, :], Hrow[:, t, :], ALU.add).then_inc(sums, 1)

            @block.tensor
            def _(pe):
                ln.pe(pe)
                pe.wait_ge(loaded, ALL)

                def up(j):
                    pe.wait_ge(ln.xt_ready, 4 * (j + 1) if j else NT)
                    for f in range(FC):
                        n = FC * j + f
                        if n >= 4:
                            pe.wait_ge(h_used, n - 3)
                        for kd in range(KD):
                            ins = pe.matmul(PS[n % 4][:, :], w1[:, kd, f * P:(f + 1) * P], g.XT[:, kd, j * 512:(j + 1) * 512],
                                            start=(kd == 0), stop=(kd == KD - 1))
                        ins.then_inc(h_ready, 1)

                def down(j):
                    pe.wait_ge(h_used, FC * (j + 1))
                    for c in range(4):
                        t = 4 * j + c
                        if t >= 4:
                            pe.wait_ge(y_used, t - 3)
                        for f in range(FC):
                            ins = pe.matmul(PS[4 + t % 4][:, 0:D], GH[:, j % 2, f, c * P:(c + 1) * P], w2[:, f, :],
                                            start=(f == 0), stop=(f == FC - 1))
                        ins.then_inc(y_ready, 1)
                up(0)
                for j in range(4):
                    if j + 1 < 4:
                        up(j + 1)
                    down(j)

            @block.scalar
            def _(act):
                act.wait_ge(loaded, ALL)
                ln.act(act)
                for n in range(4 * FC):
                    j, f = n // FC, n % FC
                    act.wait_ge(h_ready, n + 1)
                    if j >= 2:
                        act.wait_ge(y_ready, 4 * (j - 1))
                    act.activation(GH[:, j % 2, f, :], PS[n % 4][:, :], ACT.Gelu_apprx_tanh, bias=bf1[:, f:f + 1]).then_inc(h_used, 1)

            @block.vector
            def _(dve):
                ln.dve(dve)
                dve.wait_ge(sums, 2 * NT)
                for t in range(NT):
                    dve.wait_ge(y_ready, t + 1)
                    dve.tensor_tensor(g.X[:, t, :], g.X[:, t, :], PS[4 + t % 4][:, 0:D], ALU.add).then_inc(y_used, 1)


STAGES = [mamba, xattn0, ffn0, mixer1, xattn1, ffn1]


def build(nc, a, out, which=range(6)):
    g = G(nc)
    with ExitStack() as ctx:
        setup(g, ctx, a)
        g.end_stage()
        for stage in [STAGES[w] for w in which]:
            stage(g, a)
            g.end_stage()
        with nc.semaphore("stored") as stored, nc.Block() as block:
            @block.sync
            def _(sp):
                sp.dma_start(out, g.X[:, :, :]).then_inc(stored, 16)
                sp.wait_ge(stored, 16)


def lay_out(i):
    import numpy as np
    c = np.ascontiguousarray
    def rows(w):
        return c(w.reshape(-1, P, w.shape[1]).transpose(1, 0, 2))
    def cols(v):
        return c(v.reshape(-1, P).T)
    xp = i["L0_attn_x_proj_w"]
    bc = xp[R:]
    d = {
        "x": c(i["x"].reshape(NT, P, D).transpose(1, 0, 2)),
        "m_w_in": rows(i["L0_attn_in_proj_w"].T),
        "m_w_x": rows(np.concatenate([bc, bc, bc, xp[:R]]).T),
        "m_w_dt": c(i["L0_attn_dt_proj_w"].T),
        "m_w_out": rows(i["L0_attn_out_proj_w"].T),
        "m_conv_w": c(i["L0_attn_conv_w"].reshape(CI, P, DC).transpose(1, 0, 2)),
        "m_conv_b": cols(i["L0_attn_conv_b"]),
        "m_dt_b": cols(i["L0_attn_dt_proj_b"]),
        "m_skip": cols(i["L0_attn_D"]),
        "m_A_log": rows(i["L0_attn_A_log"]),
    }
    ctxT = i["ctx_1024"].reshape(B * SK, KD, P).transpose(2, 1, 0)
    d["ctxT"] = c(ctxT)
    d["dist"] = c(i["fside_BxSxS2_0"].reshape(NT, P, SK).transpose(1, 0, 2))
    d["scaling"] = c(i["L0_xattn_distance_scaling"].reshape(1, 1))
    for pre, lay, t in (("a0_", "L0_xattn_", True), ("a1_", "L1_xattn_", False)):
        for n in "qkvo":
            w = i[lay + "W" + n]
            d[pre + "w" + n] = rows(w.T if t else w)
        d[pre + "bq"], d[pre + "bk"] = cols(i[lay + "bq"]), cols(i[lay + "bk"])
        d[pre + "bv"], d[pre + "bo"] = c(i[lay + "bv"][None]), c(i[lay + "bo"][None])
    def experts(w):
        return c(w.reshape(E, -1, P, w.shape[2]).transpose(0, 2, 1, 3))
    d["f0_wg"] = rows(i["L0_ffn_wg"])
    d["f0_w1"], d["f0_w2"] = experts(i["L0_ffn_w1"]), experts(i["L0_ffn_w2"])
    d["f1_wg"] = rows(i["L1_ffn_gate_w"].T)
    for n in ("w1", "w2", "w3"):
        w = experts(i["L1_ffn_" + n].transpose(0, 2, 1))
        d["f1_" + n] = w.reshape(E, P, -1)
    lay = "L1_attn_"
    for n in "123":
        d["h_g" + n], d["h_b" + n] = cols(i[lay + f"ln{n}_g"]), cols(i[lay + f"ln{n}_b"])
    d["h_w_pot"], d["h_b_pot"] = rows(i[lay + "w_pot"]), c(i[lay + "b_pot"][:, None])
    d["h_w_bk"] = np.concatenate([i[lay + "w_bk"], i[lay + "b_bk"][None]])
    d["h_w_qkv"], d["h_w_out"] = rows(i[lay + "w_qkv"]), rows(i[lay + "w_out"])
    bq = i[lay + "b_qkv"]
    d["h_b_qk"], d["h_b_v"] = cols(bq[:1024]), c(bq[1024:][None])
    d["h_b_out"] = c(i[lay + "b_out"][None])
    d["h_w_ff1"], d["h_w_ff2"] = rows(i[lay + "w_ff1"]), rows(i[lay + "w_ff2"])
    d["h_b_ff1"], d["h_b_ff2"] = cols(i[lay + "b_ff1"]), c(i[lay + "b_ff2"][None])
    return d


def make(nc, d, which=range(6)):
    a = {n: nc.dram_tensor("in_" + n, v.shape, mybir.dt.from_np(v.dtype), kind="ExternalInput").ap() for n, v in d.items()}
    out = nc.dram_tensor("out_rows", (P, NT, D), F32, kind="ExternalOutput").ap()
    build(nc, a, out, which)


def kernel(**inputs):
    import numpy as np
    import concourse.bacc as bacc
    from concourse.bass_utils import run_bass_kernel_spmd

    d = lay_out({n: np.asarray(v) for n, v in inputs.items()})
    nc = bacc.Bacc("TRN2", target_bir_lowering=False, num_devices=1)
    make(nc, d)
    r = run_bass_kernel_spmd(nc, [{"in_" + n: v for n, v in d.items()}], core_ids=[0])
    rows = r.results[0]["out_rows"]
    return np.ascontiguousarray(rows.transpose(1, 0, 2)).reshape(B, S, D)
```

```python
from contextlib import ExitStack

import concourse.bass as bass
from concourse import mybir
from concourse.bass import ds

ALU = mybir.AluOpType
ACT = mybir.ActivationFunctionType
F32 = mybir.dt.float32
BF16 = mybir.dt.bfloat16
F32R = mybir.dt.float32r
U32 = mybir.dt.uint32
AX_X = mybir.AxisListType.X

P = 128
B, S, D = 2, 1024, 256
T = B * S
NT = T // P
TB = S // P
KD = D // P
EPS = 1e-5


class Chain:

    def __init__(self, eng, sem):
        self.eng, self.sem, self.n, self.base, self.k = eng, sem, 0, None, 0

    def add(self, ins):
        ins.then_inc(self.sem, 1)
        if self.base is None:
            self.n += 1
        else:
            self.k += 1

    def sync(self):
        if self.base is None:
            self.eng.wait_ge(self.sem, self.n)
        else:
            self.eng.wait_ge(self.sem, self.base + self.k)

    def __call__(self, ins):
        self.add(ins)
        self.sync()

    def enter(self, i, per):
        self.base, self.k, self.per = i * per + self.n, 0, per

    def leave(self, trips):
        assert self.k == self.per, (self.k, self.per)
        self.base, self.n = None, self.n + trips * self.per


class LayerNorm:

    def __init__(self, g, ctx, name, src, dst, dstT, banks, gain=None, bias=None, split=False, stats=None, arrived=None):
        nc = g.nc
        self.g, self.src, self.dst, self.dstT, self.banks = g, src, dst, dstT, banks
        self.gain, self.bias, self.split = gain, bias, split
        sem = g.semaphores(name + "_")
        self.chain, self.var_ready, self.std_ready = sem("chain"), sem("var_ready"), sem("std_ready")
        self.xn_ready, self.tp_ready, self.xt_ready = sem("xn_ready"), sem("tp_ready"), sem("xt_ready")
        self.hi_ready, self.lo_ready = sem("hi_ready"), sem("lo_ready")
        if split:
            self.hi, self.lo = (ctx.enter_context(nc.sbuf_tensor(f"{name}_{n}", [P, KD, T], F32R)) for n in ("hi", "lo"))
        sb = lambda n, s: ctx.enter_context(nc.sbuf_tensor(f"{name}_{n}", s, F32))
        self.arrived = arrived
        self.given = stats is not None
        self.stats = stats if self.given else sb("stats", [P, NT, 6])
        self.mv = sb("mv", [P, NT, 2])
        self.std = sb("std", [P, NT])
        self.rstd = sb("rstd", [P, NT])

    def dve(self, dve):
        ch = Chain(dve, self.chain)
        if not self.given:
            for t in range(NT):
                if self.arrived and t % 4 == 0:
                    dve.wait_ge(self.arrived[t // 4], 16)
                ch.add(dve.bn_stats(self.stats[:, t, :], self.src[:, t, :]))
        for t in range(NT):
            if not self.given:
                dve.wait_ge(self.chain, t + 1)
            ins = dve.bn_aggr(self.mv[:, t, :], self.stats[:, t, :])
        ins.then_inc(self.var_ready, 1)
        dve.wait_ge(self.std_ready, 1)
        ch(dve.reciprocal(self.rstd[:, :], self.std[:, :]))
        for t in range(NT):
            dve.tensor_scalar(self.dst[:, t, :], self.src[:, t, :], self.mv[:, t, 0:1], self.rstd[:, t:t + 1],
                              ALU.subtract, ALU.mult).then_inc(self.xn_ready, 1)
        if self.split:
            for t in range(NT):
                dve.wait_ge(self.hi_ready, t + 1)
                n = slice(t * P, (t + 1) * P)
                dve.tensor_tensor(self.lo[:, :, n], self.dstT[:, :, n], self.hi[:, :, n].bitcast(F32), ALU.subtract).then_inc(self.lo_ready, 1)

    def act(self, act):
        self.act_std(act)
        self.act_transposed(act)

    def act_std(self, act):
        act.wait_ge(self.var_ready, 1)
        act.activation(self.std[:, :], self.mv[:, :, 1], ACT.Sqrt, bias=self.g.eps[:, 0:1]).then_inc(self.std_ready, 1)

    def act_transposed(self, act):
        if self.dstT is None:
            return
        for t in range(NT):
            act.wait_ge(self.tp_ready, t + 1)
            bank = self.banks[t % len(self.banks)]
            if self.gain is None:
                act.activation(self.dstT[:, :, t * P:(t + 1) * P],
                               bank[:, 0:D].rearrange("p (k n) -> p k n", k=KD), ACT.Copy).then_inc(self.xt_ready, 1)
            else:
                for k in range(KD):
                    ins = act.activation(self.dstT[:, k, t * P:(t + 1) * P], bank[:, k * P:(k + 1) * P], ACT.Identity,
                                         bias=self.bias[:, k:k + 1], scale=self.gain[:, k:k + 1])
                ins.then_inc(self.xt_ready, 1)
            if self.split:
                act.wait_ge(self.xt_ready, t + 1)
                n = slice(t * P, (t + 1) * P)
                act.activation(self.hi[:, :, n], self.dstT[:, :, n], ACT.Copy).then_inc(self.hi_ready, 1)

    def pe(self, pe):
        for t in range(NT):
            pe.wait_ge(self.xn_ready, t + 1)
            if t >= len(self.banks):
                pe.wait_ge(self.xt_ready, t + 1 - len(self.banks))
            bank = self.banks[t % len(self.banks)]
            for k in range(KD):
                ins = pe.transpose(bank[:, k * P:(k + 1) * P], self.dst[:, t, k * P:(k + 1) * P], self.g.ident[:, :])
            ins.then_inc(self.tp_ready, 1)


def products(pe, out, ah, al, bh, bl, first, last):
    pe.matmul(out, ah, bh, start=first, stop=False)
    pe.matmul(out, ah, bl, start=False, stop=False)
    return pe.matmul(out, al, bh, start=False, stop=last)


class G:

    def __init__(self, nc):
        self.nc, self.made = nc, []
        self.x_stats = None

    def semaphores(self, prefix):
        def make_one(name):
            self.made.append(self.nc.alloc_semaphore(name=prefix + name))
            return self.made[-1]
        return make_one

    def keep_stats(self, dve, stats, rows, updated, t):
        if t:
            dve.wait_ge(updated, t)
            dve.bn_stats(stats[:, t - 1, :], rows[:, t - 1, :])

    def end_stage(self):
        self.nc.clear_and_free_semaphores(self.made)
        self.nc.all_engine_barrier()
        self.made = []


def setup(g, ctx, a):
    nc = g.nc
    sb = lambda n, s, dt=F32: ctx.enter_context(nc.sbuf_tensor(n, s, dt))
    g.X = sb("X", [P, NT, D])
    g.XT = sb("XT", [P, KD, T])
    g.ident = sb("ident", [P, P])
    g.upper = sb("upper", [P, P])
    g.ones = sb("ones", [P, P])
    g.stats = sb("x_stats", [P, NT, 6])
    g.eps = sb("eps", [P, 2])
    g.ps = ctx.enter_context(nc.psum_tensor("ps", [P, 8, 512], F32))
    g.PS = [g.ps[:, i, :] for i in range(8)]
    const_chain = g.semaphores("s_")("const_chain")
    g.x_loaded = [nc.alloc_semaphore(name=f"x_loaded{j}") for j in range(NT // 4)]
    with nc.Block() as block:
        @block.sync
        def _(sp):
            for j in range(NT // 4):
                sp.dma_start(g.X[:, 4 * j:4 * j + 4, :], a["x"][:, 4 * j:4 * j + 4, :]).then_inc(g.x_loaded[j], 16)

        @block.gpsimd
        def _(pool):
            ch = Chain(pool, const_chain)
            ch.add(pool.memset(g.ident[:, :], 0.0))
            ch.add(pool.memset(g.ones[:, :], 1.0))
            ch.add(pool.memset(g.eps[:, 0:1], EPS))
            ch.add(pool.memset(g.eps[:, 1:2], 1e-9))
            ch.sync()
            ch.add(pool.affine_select(out=g.ident[:, :], in_=g.ident[:, :], compare_op=ALU.not_equal, fill=1.0,
                                      base=0, pattern=[[-1, P]], channel_multiplier=1))
            ch(pool.affine_select(out=g.upper[:, :], in_=g.ones[:, :], compare_op=ALU.is_ge, fill=0.0,
                                  base=0, pattern=[[1, P]], channel_multiplier=-1))


DI, NS, DC, R = 512, 16, 4, 16
CI = DI // P
HB = S // 512
RING = 3


def mamba(g, a):
    nc = g.nc
    PS = g.PS
    with ExitStack() as ctx:
        sb = lambda n, s, dt=F32: ctx.enter_context(nc.sbuf_tensor(n, s, dt))
        sem = g.semaphores("m_")
        w_in = sb("w_in", [P, KD, 2 * DI])
        w_x = sb("w_x", [P, CI, 3 * 2 * NS + R])
        w_dt = sb("w_dt", [P, DI])
        w_out = sb("m_w_out", [P, CI, D])
        conv_w, conv_b = sb("conv_w", [P, CI, DC]), sb("conv_b", [P, CI])
        dt_b, skip = sb("dt_b", [P, CI]), sb("skip", [P, CI])
        nA = sb("nA", [P, CI, NS])
        sel = sb("sel", [P, 2 * NS, P], BF16)
        XC = sb("XC", [P, CI, DC - 1 + S])
        Z = sb("Z", [P, CI, S])
        XS = sb("XS", [P, CI, S])
        DT = sb("DT", [P, CI, S])
        DTX = XC
        GY = sb("GY", [P, CI, S])
        XN = GY[:, :, :].rearrange("p c (t d) -> p (c t) d", d=D)
        dA = sb("dA", [P, RING, S])
        U = sb("U", [P, RING, S])
        H = sb("H", [P, RING, S])
        HC = sb("HC", [P, RING, S])
        BC = sb("BC", [P, 2, 2, S])
        XP = dA[:, 0, :]
        R1, R2 = dA[:, 1, :], dA[:, 2, :]
        parts = sb("parts", [P, S], BF16)
        part_f = sb("part_f", [P, 2, 512], BF16)
        CV = lambda h, c: DT[:, c, h * 512:(h + 1) * 512]
        EA = lambda k: XC[:, k % CI, k // CI * 512:(k // CI + 1) * 512]
        LN = lambda k: [U, H, HC][k // 3][:, k % 3, 0:512]
        W1 = lambda k: [U, H, HC][k // 3][:, k % 3, 512:1024]

        loaded, cc = sem("loaded"), sem("const_chain")
        ln = LayerNorm(g, ctx, "m_ln", g.X, XN, g.XT, PS[0:4], arrived=g.x_loaded)
        chain, act_chain = sem("chain"), sem("act_chain")
        in_ready, in_used = sem("in_ready"), sem("in_used")
        conv_ready, xs_ready = sem("conv_ready"), sem("xs_ready")
        xp_ready, xp_used, parts_ready = sem("xp_ready"), sem("xp_used"), sem("parts_ready")
        dtp_ready, dtp_used, abs_used, log_ready = sem("dtp_ready"), sem("dtp_used"), sem("abs_used"), sem("log_ready")
        exp_ready, padded, corr_ready, dt_ready = sem("exp_ready"), sem("padded"), sem("corr_ready"), sem("dt_ready")
        dtx_ready = sem("dtx_ready")
        bc_ready, bc_copied = sem("bc_ready"), sem("bc_copied")
        da_ready, u_ready, h_ready, hc_ready, hc_used = (sem("da_ready"), sem("u_ready"), sem("h_ready"),
                                                         sem("hc_ready"), sem("hc_used"))
        y_used, gy_ready = sem("y_used"), sem("gy_ready")
        o_ready, o_used = sem("o_ready"), sem("o_used")

        names = [(w_in[:, :, :], "w_in"), (w_x[:, :, :], "w_x"), (w_dt[96:96 + R, :], "w_dt"), (w_out[:, :, :], "w_out"),
                 (conv_w[:, :, :], "conv_w"), (conv_b[:, :], "conv_b"), (dt_b[:, :], "dt_b"), (skip[:, :], "skip"),
                 (nA[:, :, :], "A_log")]
        ALL = 16 * len(names)
        CPB = 2
        ITS = NS * CPB
        NBLK = CI // CPB

        with nc.Block() as block:
            @block.sync
            def _(sp):
                for dst, name in names:
                    sp.dma_start(dst, a["m_" + name]).then_inc(loaded, 16)

            @block.gpsimd
            def _(pool):
                ch = Chain(pool, cc)
                ch.add(pool.memset(sel[0:96, :, :], 0.0))
                ch.sync()
                for q in range(3):
                    ch(pool.affine_select(out=sel[0:96, :, :], in_=sel[0:96, :, :], compare_op=ALU.not_equal, fill=1.0,
                                          base=-32 * q, pattern=[[-1, 2 * NS], [0, P]], channel_multiplier=1))

                def times_x(b, k):
                    c, s = k % CI, slice(k // CI * 512, (k // CI + 1) * 512)
                    pool.wait_ge(dt_ready, b * 8 + k + 1)
                    pool.tensor_tensor(DTX[:, c, s], DT[:, c, s], XS[:, c, s], ALU.mult).then_inc(dtx_ready, 1)

                for b in range(B):
                    if b:
                        pool.wait_ge(u_ready, b * (NBLK * ITS))
                    pool.memset(XC[:, :, 0:DC - 1], 0.0).then_inc(padded, 1)
                    for h in range(HB):
                        pool.wait_ge(xp_used, b * 2 + h + 1)
                        s = slice(h * 512, (h + 1) * 512)
                        ch(pool.tensor_copy(part_f[0:96, 0, :], XP[0:96, s]))
                        ch(pool.tensor_tensor(R1[0:96, s], XP[0:96, s], part_f[0:96, 0, :], ALU.subtract))
                        ch(pool.tensor_copy(part_f[0:96, 1, :], R1[0:96, s]))
                        ch(pool.tensor_tensor(R2[0:96, s], R1[0:96, s], part_f[0:96, 1, :], ALU.subtract))
                        if b and h == 0:
                            pool.wait_ge(bc_ready, b * (NBLK * NS * 4))
                        ch(pool.tensor_copy(parts[0:32, s], part_f[0:32, 0, :]))
                        ch(pool.tensor_copy(parts[32:64, s], part_f[32:64, 1, :]))
                        ch(pool.tensor_copy(parts[64:96, s], R2[64:96, s]))
                    pool.sem_inc(parts_ready, 1)
                    one = g.ones[:, 0:1].to_broadcast([P, 512])
                    for k in range(1, CI * HB, 2):
                        pool.wait_ge(exp_ready, b * 8 + k + 1)
                        ch(pool.tensor_tensor(W1(k), EA(k), one, ALU.add))
                        ch(pool.tensor_tensor(W1(k), W1(k), one, ALU.subtract))
                        pool.tensor_tensor(W1(k), W1(k), EA(k), ALU.subtract).then_inc(corr_ready, 1)
                        if k >= 3:
                            times_x(b, k - 3)
                            times_x(b, k - 2)
                    times_x(b, CI * HB - 2)
                    times_x(b, CI * HB - 1)
                    for blk in range(NBLK):
                        for it in range(ITS):
                            n, c = it // CPB, CPB * blk + it % CPB
                            step = blk * ITS + it
                            if it == 0:
                                pool.wait_ge(dtx_ready, (b + 1) * CI * HB)
                            if it % CPB == 0:
                                pool.wait_ge(bc_copied, b * (NBLK * NS * 4) + 4 * (blk * NS + n) + 2)
                            if step >= RING:
                                pool.wait_ge(h_ready, b * (NBLK * ITS) + step - RING + 1)
                            pool.tensor_tensor(U[:, step % RING, :], DTX[:, c, 0:S], BC[:, 0, n % 2, :],
                                               ALU.mult).then_inc(u_ready, 1)

            @block.tensor
            def _(pe):
                pe.wait_ge(cc, 4)
                ln.pe(pe)
                pe.wait_ge(loaded, ALL)

                def project_in(b, k):
                    f, h = k // HB, k % HB
                    if k in range(4, 8) or k >= 12:
                        pe.wait_ge(in_used, b * 16 + k - 3)
                    for kd in range(KD):
                        ins = pe.matmul(PS[k % 4 + (4 if k < 8 else 0)][:, :], w_in[:, kd, f * P:(f + 1) * P],
                                        g.XT[:, kd, b * S + h * 512:b * S + (h + 1) * 512], start=(kd == 0), stop=(kd == KD - 1))
                    ins.then_inc(in_ready, 1)

                def project_out(b, t):
                    if t == 0:
                        pe.wait_ge(gy_ready, (b + 1) * CI * HB)
                    if t >= 4:
                        pe.wait_ge(o_used, b * TB + t - 3)
                    for c in range(CI):
                        ins = pe.matmul(PS[t % 4][:, 0:D], GY[:, c, t * P:(t + 1) * P], w_out[:, c, :],
                                        start=(c == 0), stop=(c == CI - 1))
                    ins.then_inc(o_ready, 1)

                def rows_of(b, h):
                    pe.wait_ge(in_used, b * 16 + 8)
                    for c in range(CI):
                        pe.wait_ge(xs_ready, b * 8 + 4 * h + c + 1)
                        ins = pe.matmul(PS[4 + h][0:112, :], w_x[:, c, :], XS[:, c, h * 512:(h + 1) * 512],
                                        start=(c == 0), stop=(c == CI - 1))
                    ins.then_inc(xp_ready, 1)

                for b in range(B):
                    if b == 0:
                        pe.wait_ge(ln.xt_ready, NT)
                        for k in range(8):
                            project_in(b, k)
                    rows_of(b, 0)
                    if b:
                        for t in range(TB // 2):
                            project_out(b - 1, t)
                    else:
                        project_in(b, 8)
                        project_in(b, 9)
                    rows_of(b, 1)
                    for k in range(CI * HB):
                        h, c = k // CI, k % CI
                        if c == 0:
                            pe.wait_ge(xp_used, b * 2 + h + 1)
                        if k >= 2:
                            pe.wait_ge(dtp_used, b * 8 + k - 1)
                            pe.wait_ge(abs_used, b * 8 + k - 1)
                        pe.matmul(PS[6 + k % 2][:, :], w_dt[96:96 + R, c * P:(c + 1) * P],
                                  XP[96:96 + R, h * 512:(h + 1) * 512], start=True, stop=True).then_inc(dtp_ready, 1)
                    if b:
                        for t in range(TB // 2, TB):
                            project_out(b - 1, t)
                        pe.wait_ge(o_used, b * TB)
                    for k in range(8 if b else 10, 16):
                        project_in(b, k)
                    def broadcast(blk, n):
                        m = blk * NS + n
                        for w in range(2):
                            for h in range(HB):
                                q = 4 * m + 2 * w + h
                                if m == 0 and w == 0 and h == 0:
                                    pe.wait_ge(parts_ready, b + 1)
                                    pe.wait_ge(xp_used, (b + 1) * 2)
                                    pe.wait_ge(dtp_used, (b + 1) * 8)
                                    pe.wait_ge(abs_used, (b + 1) * 8)
                                if m >= 1:
                                    pe.wait_ge(bc_copied, b * (NBLK * NS * 4) + q - 3)
                                pe.matmul(PS[4 + 2 * w + h][:, :], sel[0:96, NS * w + n, :],
                                          parts[0:96, h * 512:(h + 1) * 512], start=True, stop=True).then_inc(bc_ready, 1)

                    for blk in range(NBLK):
                        if blk == 0:
                            broadcast(0, 0)
                            broadcast(0, 1)
                        for it in range(ITS):
                            n, c = it // CPB, it % CPB
                            step = blk * ITS + it
                            if c == CPB - 1 and blk * NS + n + 2 < NBLK * NS:
                                broadcast((blk * NS + n + 2) // NS, (n + 2) % NS)
                            if it < CPB:
                                if blk == 0:
                                    pe.wait_ge(in_used, (b + 1) * 16)
                                else:
                                    pe.wait_ge(y_used, b * (NBLK * 4) + 4 * (blk - 1) + 2 * (c + 1))
                            pe.wait_ge(hc_ready, b * (NBLK * ITS) + step + 1)
                            for h in range(HB):
                                ins = pe.matmul(PS[2 * c + h][:, :], g.ident[:, :], HC[:, step % RING, h * 512:(h + 1) * 512],
                                                start=(n == 0), stop=(n == NS - 1))
                            ins.then_inc(hc_used, 1)
                    if b + 1 < B:
                        pe.wait_ge(bc_copied, (b + 1) * (NBLK * NS * 4))
                        for k in range(8):
                            project_in(b + 1, k)
                for t in range(TB):
                    project_out(B - 1, t)

            @block.scalar
            def _(act):
                act.wait_ge(loaded, ALL)
                ch = Chain(act, act_chain)
                ln.act(act)
                ch(act.activation(nA[:, :, :], nA[:, :, :], ACT.Exp))
                ch(act.mul(nA[:, :, :], nA[:, :, :], -1.0))
                for b in range(B):
                    def silu_z(k):
                        if b and k == 8:
                            act.wait_ge(gy_ready, b * 8)
                        act.wait_ge(in_ready, b * 16 + k + 1)
                        f, h = (k - 8) // HB, k % HB
                        act.activation(Z[:, f, h * 512:(h + 1) * 512], PS[k % 4][:, :], ACT.Silu).then_inc(in_used, 1)

                    if b:
                        act.wait_ge(dtx_ready, b * 8)
                        act.wait_ge(u_ready, b * (NBLK * ITS))
                    for k in range(8):
                        f, h = k // HB, k % HB
                        act.wait_ge(in_ready, b * 16 + k + 1)
                        act.activation(XC[:, f, DC - 1 + h * 512:DC - 1 + (h + 1) * 512], PS[4 + k % 4][:, :], ACT.Copy).then_inc(in_used, 1)
                    if b:
                        act.wait_ge(gy_ready, b * 8)
                    for h in range(HB):
                        for c in range(CI):
                            act.wait_ge(conv_ready, b * 8 + 4 * h + c + 1)
                            act.activation(XS[:, c, h * 512:(h + 1) * 512], CV(h, c), ACT.Silu).then_inc(xs_ready, 1)
                        act.wait_ge(xp_ready, b * 2 + h + 1)
                        act.activation(XP[0:112, h * 512:(h + 1) * 512], PS[4 + h][0:112, :], ACT.Copy).then_inc(xp_used, 1)
                        if h == 0 and b == 0:
                            silu_z(8)
                            silu_z(9)
                    for k in range(CI * HB):
                        act.wait_ge(dtp_ready, b * 8 + k + 1)
                        act.activation(EA(k), PS[6 + k % 2][:, :], ACT.Abs, bias=dt_b[:, k % CI:k % CI + 1]).then_inc(abs_used, 1)
                    for k in range(CI * HB):
                        act.wait_ge(abs_used, b * 8 + k + 1)
                        act.activation(EA(k), EA(k), ACT.Exp, scale=-1.0).then_inc(exp_ready, 1)
                    for k in range(CI * HB):
                        act.wait_ge(exp_ready, b * 8 + k + 1)
                        act.activation(LN(k), EA(k), ACT.Ln, bias=1.0).then_inc(log_ready, 1)
                    for k in range(8 if b else 10, 16):
                        silu_z(k)
                    def copy_rows(row, w):
                        if row >= 2:
                            act.wait_ge(hc_ready if w else u_ready, b * (NBLK * ITS) + CPB * (row - 1))
                        for h in range(HB):
                            act.wait_ge(bc_ready, b * (NBLK * NS * 4) + 4 * row + 2 * w + h + 1)
                            act.activation(BC[:, w, row % 2, h * 512:(h + 1) * 512], PS[4 + 2 * w + h][:, :],
                                           ACT.Copy).then_inc(bc_copied, 1)

                    for step in range(NBLK * ITS):
                        row, c = step // CPB, CPB * (step // ITS) + step % CPB
                        n = row % NS
                        if step % CPB == 0:
                            copy_rows(row, 0)
                        if step == 0:
                            act.wait_ge(dtx_ready, (b + 1) * 8)
                        if step >= RING:
                            act.wait_ge(h_ready, b * (NBLK * ITS) + step - RING + 1)
                        act.activation(dA[:, step % RING, :], DT[:, c, :], ACT.Exp,
                                       scale=nA[:, c, n:n + 1]).then_inc(da_ready, 1)
                        if step % CPB == 0:
                            copy_rows(row, 1)

            @block.vector
            def _(dve):
                ln.dve(dve)
                dve.wait_ge(loaded, ALL)
                dve.wait_ge(ln.tp_ready, NT)
                ch = Chain(dve, chain)

                def add_rows(b, t):
                    dve.wait_ge(o_ready, b * TB + t + 1)
                    row = g.X[:, b * TB + t, :]
                    dve.tensor_tensor(row, row, PS[t % 4][:, 0:D], ALU.add).then_inc(o_used, 1)

                for b in range(B):
                    dve.wait_ge(padded, b + 1)
                    if b:
                        dve.wait_ge(da_ready, b * (NBLK * ITS))
                    for k in range(HB * CI):
                        h, c = k // CI, k % CI
                        o = CV(h, c)
                        dve.wait_ge(in_used, b * 16 + 2 * c + h + 1)
                        ch(dve.tensor_scalar(o, XC[:, c, h * 512:h * 512 + 512], conv_w[:, c, 0:1], conv_b[:, c:c + 1],
                                             ALU.mult, ALU.add))
                        for j in range(1, DC):
                            ins = dve.scalar_tensor_tensor(o, XC[:, c, h * 512 + j:h * 512 + j + 512],
                                                           conv_w[:, c, j:j + 1], o, ALU.mult, ALU.add)
                            if j < DC - 1:
                                ch(ins)
                        ins.then_inc(conv_ready, 1)
                    if b:
                        for t in range(TB // 2):
                            add_rows(b - 1, t)
                    for k in range(CI * HB):
                        c, s = k % CI, slice(k // CI * 512, (k // CI + 1) * 512)
                        dve.wait_ge(abs_used, b * 8 + k + 1)
                        dve.tensor_scalar(DT[:, c, s], PS[6 + k % 2][:, :], dt_b[:, c:c + 1], 0.0, ALU.add,
                                          ALU.max).then_inc(dtp_used, 1)
                    if b:
                        for t in range(TB // 2, TB):
                            add_rows(b - 1, t)
                    dve.wait_ge(in_used, b * 16 + 8)
                    for k in range(CI * HB):
                        c, s = k % CI, slice(k // CI * 512, (k // CI + 1) * 512)
                        dve.wait_ge(exp_ready, b * 8 + k + 1)
                        if k % 2:
                            dve.wait_ge(corr_ready, b * 4 + k // 2 + 1)
                        else:
                            ch(dve.tensor_scalar(W1(k), EA(k), 1.0, None, ALU.add))
                            ch(dve.scalar_tensor_tensor(W1(k), W1(k), 1.0, EA(k), ALU.subtract, ALU.subtract))
                        ch(dve.tensor_tensor(DT[:, c, s], DT[:, c, s], W1(k), ALU.subtract))
                        dve.wait_ge(log_ready, b * 8 + k + 1)
                        dve.tensor_tensor(DT[:, c, s], DT[:, c, s], LN(k), ALU.add).then_inc(dt_ready, 1)
                    for blk in range(NBLK):
                        for it in range(ITS):
                            n, c = it // CPB, it % CPB
                            step = blk * ITS + it
                            r = step % RING
                            dve.wait_ge(da_ready, b * (NBLK * ITS) + step + 1)
                            dve.wait_ge(u_ready, b * (NBLK * ITS) + step + 1)
                            dve.tensor_tensor_scan(H[:, r, :], dA[:, r, :], U[:, r, :], 0.0, ALU.mult,
                                                   ALU.add).then_inc(h_ready, 1)
                            dve.wait_ge(h_ready, b * (NBLK * ITS) + step + 1)
                            if c == 0:
                                dve.wait_ge(bc_copied, b * (NBLK * NS * 4) + 4 * (blk * NS + n) + 4)
                            if step >= RING:
                                dve.wait_ge(hc_used, b * (NBLK * ITS) + step - RING + 1)
                            dve.tensor_tensor(HC[:, r, :], H[:, r, :], BC[:, 1, n % 2, :], ALU.mult).then_inc(hc_ready, 1)
                        dve.wait_ge(hc_used, b * (NBLK * ITS) + (blk + 1) * ITS)
                        for c in range(CPB):
                            for h in range(HB):
                                cc_, s = CPB * blk + c, slice(h * 512, (h + 1) * 512)
                                dve.scalar_tensor_tensor(GY[:, cc_, s], XS[:, cc_, s], skip[:, cc_:cc_ + 1],
                                                         PS[2 * c + h][:, :], ALU.mult, ALU.add).then_inc(y_used, 1)
                        for c in range(CPB):
                            cc_ = CPB * blk + c
                            dve.wait_ge(y_used, b * 8 + 4 * blk + 2 * c + 2)
                            dve.tensor_tensor(GY[:, cc_, :], GY[:, cc_, :], Z[:, cc_, :], ALU.mult).then_inc(gy_ready, HB)
                for t in range(TB):
                    add_rows(B - 1, t)

NH, HD, SK = 16, 16, 77
HALF = NH // 2
HW = HALF * SK
NCH = -(-HW // P)
LASTW = HW - (NCH - 1) * P
NEWTON = 24
LATE = 3
TURN = NT // 2 - 2
OUT = 384


def attention(g, a, pre, sparse):
    nc = g.nc
    ps, PS = g.ps, g.PS
    with ExitStack() as ctx:
        sb = lambda n, s, dt=F32: ctx.enter_context(nc.sbuf_tensor(pre + n, s, dt))
        sem = g.semaphores(pre)
        wq, wk, wv, wo = (sb(n, [P, KD, D]) for n in ("wq", "wk", "wv", "wo"))
        bq, bk = sb("bq", [P, KD]), sb("bk", [P, KD])
        bv, bo = sb("bv", [P, D]), sb("bo", [P, D])
        ctxT = sb("ctxT", [P, KD, B * SK])
        KT = sb("KT", [P, KD, B * SK])
        hmask = sb("hmask", [P, HALF])
        KBD = sb("KBD", [P, 2, B, HALF, SK])
        VS = sb("VS", [P, B, D])
        VBD = sb("VBD", [P, B, 2, NCH, P])
        QT = sb("QT", [P, KD, T])
        PN = sb("PN", [P, 2, NH, SK])
        PT = sb("PT", [P, 2, 2, NCH, P])
        OT = sb("OT", [P, 2, D])
        zeros = sb("zeros", [P, NCH * P])
        if sparse:
            SC = sb("SC", [P, NT, NH, SK])
            Z8 = sb("Z8", [P, NT * NH, 8])
            reset = sb("reset", [P, NT * NH, 8])
            W8, CS = (QT[:, k, :].rearrange("p (r e) -> p r e", e=8) for k in range(2))
            T8 = g.XT[:, 0, :].rearrange("p (r e) -> p r e", e=8)
            rank = sb("rank", [P, 8])
            cnt, rcnt, th = sb("cnt", [P, NT * NH]), sb("rcnt", [P, NT * NH]), sb("th", [P, NT * NH])
            top = sb("top", [P, 2])
            topw, topi = sb("topw", [1, 1]), sb("topi", [1, 1], mybir.dt.int32)
            nt_d, nt_g = (g.XT[:, k, 0:NH * SK].rearrange("p (h s) -> p h s", h=NH) for k in (1, 0))
            nt_f, nt_c = sb("nt_f", [P, NH]), sb("nt_c", [P, NH])
            XN = SC[:, 0:4, :, :].rearrange("p a h s -> p (a h s)")[:, 0:NT * D].rearrange("p (t d) -> p t d", d=D)
        else:
            LB = sb("LB", [P, NT, SK])
            scaling = sb("scaling", [P, 2])
            SC = sb("SC", [P, 2, NH, SK])
            mx, sm, rs = sb("mx", [P, 2, NH]), sb("sm", [P, 2, NH]), sb("rs", [P, 2, NH])
            xn_room = sb("xn", [P, NT, D])
            XN = xn_room[:, :, :]
        VD = nc.dram_tensor(pre + "values", (B, 2, NCH * P * P), F32).ap()

        loaded, hm, vz = sem("loaded"), sem("hm"), sem("vz")
        ln = LayerNorm(g, ctx, pre + "ln", g.X, XN, g.XT, PS[0:4], stats=g.x_stats)
        bo_added = sem("bo_added")
        k_ready, kt_ready, kbd_ready = sem("k_ready"), sem("kt_ready"), sem("kbd_ready")
        v_ready, vs_ready, v_stored, vbd_ready = sem("v_ready"), sem("vs_ready"), sem("v_stored"), sem("vbd_ready")
        q_ready, q_used, bq_scaled = sem("q_ready"), sem("q_used"), sem("bq_scaled")
        sc_ready, sc_used, sc_copied = sem("sc_ready"), sem("sc_used"), sem("sc_copied")
        chain, act_chain = sem("chain"), sem("act_chain")
        sub_ready, e_ready, rs_ready, pn_ready = sem("sub_ready"), sem("e_ready"), sem("rs_ready"), sem("pn_ready")
        tpa_ready, pta_ready, ot_ready, otc_ready, o_ready, x_ready = (
            sem("tpa_ready"), sem("pta_ready"), sem("ot_ready"), sem("otc_ready"), sem("o_ready"), sem("x_ready"))
        top_ready, topt_ready, lb_ready = sem("top_ready"), sem("topt_ready"), sem("lb_ready")

        names = [(wq[:, :, :], pre + "wq"), (wk[:, :, :], pre + "wk"), (wv[:, :, :], pre + "wv"), (wo[:, :, :], pre + "wo"),
                 (bq[:, :], pre + "bq"), (bk[:, :], pre + "bk"), (ctxT[:, :, :], "ctxT"),
                 (bv[:, :], pre + "bv"), (bo[:, :], pre + "bo")]
        if not sparse:
            names += [(LB[:, :, :], "dist"), (scaling[:, 0:1], "scaling")]
        ALL = 16 * len(names)

        def score_bank(i):
            return 4 * (i % 2) if sparse and i >= T // 512 else 0

        def score_view(bank0):
            return ps[:, bank0:bank0 + 4, 0:HW // 2]

        with nc.Block() as block:
            @block.sync
            def _(sp):
                for dst, name in names:
                    src = a[name]
                    if dst.shape[0] == P and src.shape[0] == 1:
                        src = src.to_broadcast([P, src.shape[1]])
                    sp.dma_start(dst, src).then_inc(loaded, 16)
                sp.wait_ge(hm, 1)
                for b in range(B):
                    for h in range(2):
                        sp.dma_start(VD[b, h].rearrange("(q w) -> q w", w=NCH * P), zeros[:, :]).then_inc(vz, 16)
                sp.wait_ge(vz, 16 * 2 * B)
                sp.wait_ge(vs_ready, B)
                step = SK * P + HD
                for b in range(B):
                    for h in range(2):
                        dst = VD[b, h, 0:HALF * step].rearrange("(h x) -> h x", x=step)[:, 0:SK * P]
                        dst = dst.rearrange("h (s c) -> s h c", c=P)[:, :, 0:HD]
                        sp.dma_start(dst, VS[0:SK, b, h * P:(h + 1) * P].rearrange("s (h d) -> s h d", d=HD)).then_inc(v_stored, 16)
                sp.wait_ge(v_stored, 16 * 2 * B)
                for b in range(B):
                    for h in range(2):
                        sp.dma_start(VBD[:, b, h, :, :], VD[b, h].rearrange("(m p c) -> p m c", p=P, c=P)).then_inc(vbd_ready, 16)

            @block.gpsimd
            def _(pool):
                pool.memset(zeros[:, :], 0.0).then_inc(hm, 1)
                pool.memset(hmask[:, :], 1.0).then_inc(hm, 1)
                pool.wait_ge(hm, 2)
                pool.affine_select(out=hmask[:, :], in_=hmask[:, :], compare_op=ALU.is_ge, fill=0.0,
                                   base=0, pattern=[[-HD, HALF]], channel_multiplier=1).then_inc(hm, 1)
                pool.wait_ge(hm, 3)
                pool.affine_select(out=hmask[:, :], in_=hmask[:, :], compare_op=ALU.is_ge, fill=0.0,
                                   base=HD - 1, pattern=[[HD, HALF]], channel_multiplier=-1).then_inc(hm, 1)
                if sparse:
                    pool.memset(reset[:, :, :], 1.0).then_inc(hm, 1)
                    pool.iota(rank[:, :], pattern=[[1, 8]], base=1, channel_multiplier=0,
                              allow_small_or_imprecise_dtypes=True).then_inc(hm, 1)
                    pool.wait_ge(hm, 6)
                    pool.memset(reset[:, :, 0:1], 0.0).then_inc(hm, 1)
                pool.wait_ge(loaded, ALL)
                with pool.Fori(0, NT) as i:
                    pool.wait_ge(ln.xn_ready, i + 1)
                    row = g.X[:, ds(i, 1), :].rearrange("p a d -> p (a d)")
                    pool.tensor_tensor(row, row, bo[:, :], ALU.add).then_inc(bo_added, 1)
                if not sparse:
                    with pool.Fori(0, NT // 2) as j:
                        for u in range(2):
                            pool.wait_ge(rs_ready, 2 * j + u + 1)
                            pool.tensor_tensor(PN[:, u, :, :], PN[:, u, :, :],
                                               rs[:, u, :].unsqueeze(2).to_broadcast([P, NH, SK]),
                                               ALU.mult).then_inc(pn_ready, 1)

            @block.tensor
            def _(pe):
                pe.wait_ge(loaded, ALL)
                for k in range(KD):
                    for kd in range(KD):
                        ins = pe.matmul(PS[4 + k][:, 0:B * SK], wk[:, kd, k * P:(k + 1) * P], ctxT[:, kd, :],
                                        start=(kd == 0), stop=(kd == KD - 1))
                    ins.then_inc(k_ready, 1)
                for b in range(B):
                    for kd in range(KD):
                        ins = pe.matmul(PS[6 + b][0:SK, 0:D], ctxT[:, kd, b * SK:(b + 1) * SK], wv[:, kd, :],
                                        start=(kd == 0), stop=(kd == KD - 1))
                    ins.then_inc(v_ready, 1)
                ln.pe(pe)

                def queries(j):
                    if j == 0:
                        pe.wait_ge(kt_ready, KD)
                    pe.wait_ge(ln.xt_ready, 4 * (j + 1))
                    for f in range(KD):
                        k = KD * j + f
                        if k >= 2:
                            pe.wait_ge(q_used, k - 1)
                        for kd in range(KD):
                            ins = pe.matmul(PS[4 + k % 2][:, :], wq[:, kd, f * P:(f + 1) * P], g.XT[:, kd, j * 512:(j + 1) * 512],
                                            start=(kd == 0), stop=(kd == KD - 1))
                        ins.then_inc(q_ready, 1)

                def scores(i):
                    for q in range(4):
                        half, hh = q // 2, q % 2
                        ins = pe.matmul(PS[q + score_bank(i)][:, 0:HW // 2], QT[:, half, i * P:(i + 1) * P],
                                        KBD[:, half, i // TB, 4 * hh:4 * hh + 4, :].rearrange("p h s -> p (h s)"),
                                        start=True, stop=True)
                    return ins

                def project(i):
                    pe.wait_ge(otc_ready, i + 1)
                    for c in range(2):
                        for h in range(2):
                            ins = pe.matmul(PS[2 + c][:, OUT:OUT + P], OT[:, i % 2, h * P:(h + 1) * P], wo[:, h, c * P:(c + 1) * P],
                                            start=(h == 0), stop=(h == 1))
                    return ins

                def round_(n):
                    if n >= 1:
                        pe.wait_ge(sc_used, n)
                    if n < NT:
                        ins = scores(n)
                    if n >= 4:
                        ins = project(n - 4)
                    ins.then_inc(sc_ready, 1)

                def transpose_weights(i):
                    pe.wait_ge(pn_ready, i + 1)
                    weights = PN[:, i % 2, :, :].rearrange("p h s -> p (h s)")
                    for h in range(2):
                        if i >= 1:
                            pe.wait_ge(pta_ready, 3 * (i - 1) + h + 1)
                        for m in range(NCH - 1):
                            ins = pe.transpose(PS[4 + h][:, m * P:(m + 1) * P], weights[:, h * HW + m * P:h * HW + (m + 1) * P],
                                               g.ident[:, :])
                        ins.then_inc(tpa_ready, 1)
                    if i >= 1:
                        pe.wait_ge(pta_ready, 3 * i)
                    for h in range(2):
                        ins = pe.transpose(PS[6][0:LASTW, h * P:(h + 1) * P], weights[:, (h + 1) * HW - LASTW:(h + 1) * HW],
                                           g.ident[:, :])
                    ins.then_inc(tpa_ready, 1)

                def weigh_values(i):
                    if i == 0:
                        pe.wait_ge(vbd_ready, 16 * 2 * B)
                    if i >= 1:
                        pe.wait_ge(otc_ready, i)
                    pe.wait_ge(pta_ready, 3 * (i + 1))
                    for h in range(2):
                        for m in range(NCH):
                            w = P if m < NCH - 1 else LASTW
                            ins = pe.matmul(PS[7][:, h * P:(h + 1) * P], VBD[0:w, i // TB, h, m, :], PT[0:w, i % 2, h, m, :],
                                            start=(m == 0), stop=(m == NCH - 1))
                    ins.then_inc(ot_ready, 1)

                for j in range(T // 512):
                    queries(j)
                    if j == 0:
                        pe.wait_ge(kbd_ready, 2 * B)
                        pe.wait_ge(vs_ready, B)
                        pe.wait_ge(ln.xt_ready, NT)
                        pe.wait_ge(q_used, KD)
                    if sparse:
                        if j >= 1:
                            pe.wait_ge(sc_copied, j)
                        scores(j).then_inc(sc_ready, 1)
                    elif j < 2:
                        round_(j)
                pe.wait_ge(q_used, KD * (T // 512))
                if sparse:
                    for i in range(T // 512, NT):
                        if score_bank(i) == score_bank(i - 1):
                            pe.wait_ge(sc_copied, i)
                        else:
                            pe.wait_ge(sc_copied, i - 1)
                        scores(i).then_inc(sc_ready, 1)
                    pe.wait_ge(sc_copied, NT)

                def turn_top(half):
                    pe.wait_ge(top_ready, half + 1)
                    pe.transpose(PS[0][0:2, 0:P], top[:, :], g.ident[:, :]).then_inc(topt_ready, 1)

                for i in range(NT + 2):
                    if sparse and i == 0:
                        turn_top(0)
                    if not sparse:
                        round_(i + 2)
                    elif i >= 2:
                        if i >= 3:
                            pe.wait_ge(x_ready, i - 2)
                        project(i - 2).then_inc(o_ready, 1)
                        if i == TURN:
                            turn_top(1)
                    if 1 <= i <= NT:
                        weigh_values(i - 1)
                    if i < NT:
                        transpose_weights(i)

            @block.scalar
            def _(act):
                ln.act_std(act)
                act.wait_ge(loaded, ALL)
                ch = Chain(act, act_chain)
                if not sparse:
                    ch.add(act.activation(LB[:, :, :], LB[:, :, :], ACT.Ln, bias=g.eps[:, 1:2]))
                    ch.add(act.activation(scaling[:, 1:2], scaling[:, 0:1], ACT.Abs))
                    ch.sync()
                    ch(act.mul(scaling[:, 1:2], scaling[:, 1:2], -1.0))
                    act.activation(LB[:, :, :], LB[:, :, :], ACT.Copy, scale=scaling[:, 1:2]).then_inc(lb_ready, 1)
                act.activation(bq[:, :], bq[:, :], ACT.Copy, scale=HD ** -0.5).then_inc(bq_scaled, 1)
                for k in range(KD):
                    act.wait_ge(k_ready, k + 1)
                    act.activation(KT[:, k, :], PS[4 + k][:, 0:B * SK], ACT.Identity, bias=bk[:, k:k + 1]).then_inc(kt_ready, 1)
                ln.act_transposed(act)
                act.wait_ge(bq_scaled, 1)

                def copy_scores(i):
                    act.wait_ge(sc_ready, i + 1)
                    act.activation(SC[:, i, :, :].rearrange("p (q h) s -> p q (h s)", q=4), score_view(score_bank(i)),
                                   ACT.Copy).then_inc(sc_copied, 1)

                for j in range(T // 512):
                    for f in range(KD):
                        act.wait_ge(q_ready, KD * j + f + 1)
                        act.activation(QT[:, f, j * 512:(j + 1) * 512], PS[4 + (KD * j + f) % 2][:, :], ACT.Identity,
                                       bias=bq[:, f:f + 1], scale=HD ** -0.5).then_inc(q_used, 1)
                    if sparse:
                        copy_scores(j)
                if sparse:
                    for i in range(T // 512, NT):
                        copy_scores(i)

                def out_steps(i, u):
                    fn = ACT.Relu if sparse else ACT.Copy
                    for h in range(2):
                        act.wait_ge(tpa_ready, 3 * i + h + 1)
                        act.activation(PT[:, u, h, 0:NCH - 1, :], PS[4 + h][:, :].rearrange("p (m n) -> p m n", n=P),
                                       fn).then_inc(pta_ready, 1)
                    act.wait_ge(tpa_ready, 3 * i + 3)
                    act.activation(PT[0:LASTW, u, :, NCH - 1, :], PS[6][0:LASTW, 0:2 * P].rearrange("p (h n) -> p h n", h=2),
                                   fn).then_inc(pta_ready, 1)

                def exponentials(i, u):
                    act.wait_ge(sub_ready, i + 1)
                    act.activation(PN[:, u, :, :], SC[:, u, :, :], ACT.Exp).then_inc(e_ready, 1)

                def outputs(i, u):
                    act.wait_ge(ot_ready, i + 1)
                    act.activation(OT[:, u, :], PS[7][:, 0:D], ACT.Copy).then_inc(otc_ready, 1)

                if not sparse:
                    exponentials(0, 0)
                    exponentials(1, 1)
                out_steps(0, 0)
                with act.Fori(0, NT // 2 - 1) as j:
                    for u in range(2):
                        i = 2 * j + u
                        if not sparse:
                            exponentials(i + 2, u)
                        outputs(i, u)
                        out_steps(i + 1, 1 - u)
                outputs(NT - 2, 0)
                out_steps(NT - 1, 1)
                outputs(NT - 1, 1)

            @block.vector
            def _(dve):
                ch = Chain(dve, chain)
                ln.dve(dve)
                dve.wait_ge(loaded, ALL)
                dve.wait_ge(hm, 4)
                for b in range(B):
                    dve.wait_ge(v_ready, b + 1)
                    dve.tensor_tensor(VS[0:SK, b, :], PS[6 + b][0:SK, 0:D], bv[0:SK, :], ALU.add).then_inc(vs_ready, 1)
                for h in range(2):
                    for b in range(B):
                        dve.wait_ge(kt_ready, h + 1)
                        dve.tensor_tensor(KBD[:, h, b, :, :], KT[:, h, b * SK:(b + 1) * SK].unsqueeze(1).to_broadcast([P, HALF, SK]),
                                          hmask[:, :].unsqueeze(2).to_broadcast([P, HALF, SK]), ALU.mult).then_inc(kbd_ready, 1)
                if sparse:
                    flat = lambda x: x.rearrange("p r e -> p (r e)")

                    def largest(i):
                        dve.wait_ge(sc_copied, i + 1)
                        for h in range(NH):
                            ins = dve.max(Z8[:, i * NH + h, :], SC[:, i, h, :])
                        ins.then_inc(sc_used, 1)

                    def thresholds(half):
                        n = NT * NH // 2
                        R = slice(half * n, (half + 1) * n)
                        z8, w8, cs, t8 = Z8[:, R, :], W8[:, R, :], CS[:, R, :], T8[:, R, :]
                        dve.wait_ge(sc_used, NT // 2 * (half + 1))
                        dve.wait_ge(hm, 7)
                        ch(dve.tensor_tensor(w8, z8, z8[:, :, 0:1].to_broadcast([P, n, 8]), ALU.subtract))
                        ch.add(dve.tensor_tensor_scan(flat(cs), flat(reset[:, R, :]), flat(w8), 0.0, ALU.mult, ALU.add))
                        ch.add(dve.tensor_tensor(t8, w8, rank[:, :].unsqueeze(1).to_broadcast([P, n, 8]), ALU.mult))
                        ch.sync()
                        ch(dve.scalar_tensor_tensor(flat(t8), flat(t8), 1.0, flat(cs), ALU.add, ALU.subtract))
                        ch(dve.tensor_scalar(flat(t8), flat(t8), 0.0, None, ALU.is_gt))
                        ch.add(dve.tensor_reduce(cnt[:, R], t8, AX_X, ALU.add))
                        ch.add(dve.tensor_tensor(w8, w8, t8, ALU.mult))
                        ch.sync()
                        ch.add(dve.tensor_reduce(th[:, R], w8, AX_X, ALU.add))
                        ch.add(dve.reciprocal(rcnt[:, R], cnt[:, R]))
                        ch.add(dve.memset(top[:, :], 0.0))
                        ch.sync()
                        dve.tensor_reduce(top[:, 0:1], cnt[:, R], AX_X, ALU.max).then_inc(top_ready, 1)
                        ch(dve.scalar_tensor_tensor(th[:, R], th[:, R], -1.0, rcnt[:, R], ALU.add, ALU.mult))
                        ch(dve.tensor_tensor(th[:, R], th[:, R], z8[:, :, 0], ALU.add))

                    def wide_supports(half):
                        dve.wait_ge(topt_ready, half + 1)
                        ch(dve.tensor_reduce(topw[0:1, :], PS[0][0:1, 0:P], AX_X, ALU.max))
                        ch(dve.tensor_copy(topi[0:1, 0:1], topw[0:1, :]))
                        widest = dve.value_load(topi[0:1, 0:1], min_val=0, max_val=8)
                        with dve.If(widest >= 8):
                            with dve.Fori(0, NEWTON) as it:
                                with dve.Fori(half * NT // 2, (half + 1) * NT // 2) as i:
                                    thv = th[:, ds(i * NH, NH)]
                                    dve.tensor_tensor(nt_d, SC[:, ds(i, 1), :, :].rearrange("p a h s -> p (a h) s"),
                                                      thv.unsqueeze(2).to_broadcast([P, NH, SK]), ALU.subtract)
                                    dve.drain()
                                    dve.tensor_scalar(nt_g, nt_d, 0.0, None, ALU.is_gt)
                                    dve.tensor_scalar(nt_d, nt_d, 0.0, None, ALU.max)
                                    dve.drain()
                                    dve.tensor_reduce(nt_c[:, :], nt_g, AX_X, ALU.add)
                                    dve.tensor_reduce(nt_f[:, :], nt_d, AX_X, ALU.add)
                                    dve.drain()
                                    dve.reciprocal(nt_c[:, :], nt_c[:, :])
                                    dve.drain()
                                    dve.scalar_tensor_tensor(nt_f[:, :], nt_f[:, :], -1.0, nt_c[:, :], ALU.add, ALU.mult)
                                    dve.drain()
                                    dve.tensor_tensor(thv, thv, nt_f[:, :], ALU.add)
                                    dve.drain()

                    for i in range(NT // 2):
                        largest(i)
                    thresholds(0)
                    for i in range(NT // 2, NT - LATE):
                        largest(i)
                    wide_supports(0)

                def add_out(i):
                    row = g.X[:, ds(i, 1), :].rearrange("p a (c n) -> p (a c) n", n=P)
                    return dve.tensor_tensor(row, row, ps[:, 2:4, OUT:OUT + P], ALU.add)

                dve.wait_ge(bo_added, NT)
                if sparse:
                    def weights(i):
                        dve.tensor_tensor(PN[:, i % 2, :, :], SC[:, i, :, :],
                                          th[:, i * NH:(i + 1) * NH].unsqueeze(2).to_broadcast([P, NH, SK]), ALU.subtract).then_inc(pn_ready, 1)
                    weights(0)
                    weights(1)
                    for i in range(NT):
                        if i == TURN:
                            wide_supports(1)
                        if i + 2 < NT:
                            dve.wait_ge(tpa_ready, 3 * i + 3)
                            weights(i + 2)
                        if i < LATE:
                            largest(NT - LATE + i)
                        if i == LATE:
                            thresholds(1)
                        dve.wait_ge(o_ready, i + 1)
                        add_out(i).then_inc(x_ready, 1)
                        g.keep_stats(dve, g.stats, g.X, x_ready, i)
                    g.keep_stats(dve, g.stats, g.X, x_ready, NT)
                else:
                    dve.wait_ge(lb_ready, 1)

                    def round_(n, u, scores=True, output=True):
                        dve.wait_ge(sc_ready, n + 1)
                        if scores:
                            for q in range(4):
                                ins = dve.tensor_tensor(SC[:, u, 4 * q:4 * q + 4, :], PS[q][:, 0:HW // 2].rearrange("p (h s) -> p h s", s=SK),
                                                        LB[:, ds(n, 1), :].to_broadcast([P, 4, SK]), ALU.add)
                        if output:
                            ins = add_out(n - 4)
                        ins.then_inc(sc_used, 1)
                        if scores:
                            dve.wait_ge(sc_used, n + 1)
                            ch(dve.tensor_reduce(mx[:, u, :], SC[:, u, :, :], AX_X, ALU.max))
                            dve.tensor_tensor(SC[:, u, :, :], SC[:, u, :, :], mx[:, u, :].unsqueeze(2).to_broadcast([P, NH, SK]),
                                              ALU.subtract).then_inc(sub_ready, 1)

                    def sums(i, u):
                        dve.wait_ge(e_ready, i + 1)
                        ch(dve.tensor_reduce(sm[:, u, :], PN[:, u, :, :], AX_X, ALU.add))
                        dve.reciprocal(rs[:, u, :], sm[:, u, :]).then_inc(rs_ready, 1)

                    round_(0, 0, output=False)
                    round_(1, 1, output=False)
                    for i in range(2):
                        sums(i, i)
                        round_(i + 2, i, output=False)
                    with dve.Fori(0, NT // 2 - 2) as j:
                        ch.enter(j, 4)
                        for u in range(2):
                            sums(2 * j + u + 2, u)
                            round_(2 * j + u + 4, u)
                    ch.leave(NT // 2 - 2)
                    for i in range(2):
                        sums(NT - 2 + i, i)
                        round_(NT + i, i, scores=False)
                    round_(NT + 2, 0, scores=False)
                    round_(NT + 3, 1, scores=False)


    g.x_stats = g.stats if sparse else None


def xattn0(g, a):
    attention(g, a, "a0_", False)


def xattn1(g, a):
    attention(g, a, "a1_", True)


E = 8
F = 1024
FC = F // P
CAP = T // E
CB = CAP // P
NTE = NT * E
BIG = float(1 << 20)


class Router:

    def __init__(self, g, ctx, pre):
        nc = g.nc
        self.g = g
        sb = lambda n, s, dt=F32: ctx.enter_context(nc.sbuf_tensor(pre + "r_" + n, s, dt))
        sem = g.semaphores(pre + "r_")
        self.sb = sb
        self.wg = sb("wg", [P, KD, E])
        self.L, self.EX, self.A1, self.A2 = (sb(n, [P, NT, E]) for n in ("L", "EX", "A1", "A2"))
        self.TOT, self.CUM, self.first = (sb(n, [P, E, NT]) for n in ("TOT", "CUM", "first"))
        self.OH = sb("OH", [P, NT, E])
        self.PL = sb("PL", [P, NT, E])
        self.e8 = sb("e8", [P, E])
        self.logits_ready, self.exp_in, self.exp_out = sem("logits_ready"), sem("exp_in"), sem("exp_out")
        self.oh_ready, self.count_ready, self.const = sem("oh_ready"), sem("count_ready"), sem("const")

    def pool(self, pool):
        pool.iota(self.e8[:, :], pattern=[[1, E]], base=-E, channel_multiplier=0,
                  allow_small_or_imprecise_dtypes=True).then_inc(self.const, 1)
        pool.memset(self.first[:, :, :], 1.0).then_inc(self.const, 1)
        pool.wait_ge(self.const, 2)
        pool.memset(self.first[:, :, 0:1], 0.0).then_inc(self.const, 1)

    def pe_logits(self, pe, ln):
        for t in range(NT):
            pe.wait_ge(ln.xt_ready, t + 1)
            for kd in range(KD):
                ins = pe.matmul(self.g.PS[4][:, t * E:(t + 1) * E], self.g.XT[:, kd, t * P:(t + 1) * P], self.wg[:, kd, :],
                                start=(kd == 0), stop=(kd == KD - 1))
        ins.then_inc(self.logits_ready, 1)

    def pe_counts(self, pe):
        pe.wait_ge(self.oh_ready, 1)
        oh = self.OH[:, :, :].rearrange("p t e -> p (t e)")
        pe.matmul(self.g.PS[5][:, 0:NTE], self.g.upper[:, :], oh, start=True, stop=True)
        pe.matmul(self.g.PS[6][:, 0:NTE], self.g.ones[:, :], oh, start=True, stop=True).then_inc(self.count_ready, 1)

    def wide(self, x):
        return x.unsqueeze(2).to_broadcast([P, NT, E])

    def row(self, x):
        return x.unsqueeze(1).to_broadcast([P, NT, E])

    def dve_first(self, dve, ch, best, onehot, low):
        ch(dve.tensor_tensor(self.A1[:, :, :], best, self.row(self.e8[:, :]), ALU.mult))
        ch(dve.tensor_reduce(low, self.A1[:, :, :], AX_X, ALU.min))
        ch(dve.tensor_tensor(onehot, self.row(self.e8[:, :]), self.wide(low), ALU.is_equal))

    def dve_places(self, dve, ch):
        dve.sem_inc(self.oh_ready, 1)
        dve.wait_ge(self.count_ready, 1)
        dve.wait_ge(self.const, 3)
        flat = lambda x: x[:, :, :].rearrange("p e t -> p (e t)")
        ch(dve.tensor_copy(self.TOT[:, :, :], self.g.PS[6][:, 0:NTE].rearrange("p (t e) -> p e t", e=E)))
        ch(dve.tensor_tensor_scan(flat(self.CUM), flat(self.first), flat(self.TOT), 0.0, ALU.mult, ALU.add))
        ch(dve.tensor_tensor(self.TOT[:, :, :], self.CUM[:, :, :], self.TOT[:, :, :], ALU.subtract))
        ch(dve.tensor_tensor(self.PL[:, :, :], self.g.PS[5][:, 0:NTE].rearrange("p (t e) -> p t e", e=E),
                             self.TOT[:, :, :].rearrange("p e t -> p t e"), ALU.add))
        ch(dve.tensor_scalar(self.PL[:, :, :], self.PL[:, :, :], 1.0, None, ALU.subtract))


def ffn0(g, a):
    nc, PS = g.nc, g.PS
    with ExitStack() as ctx:
        sb = lambda n, s, dt=F32: ctx.enter_context(nc.sbuf_tensor("f0_" + n, s, dt))
        sem = g.semaphores("f0_")
        WR = 2
        w1, w2 = sb("w1", [P, WR, KD, F]), sb("w2", [P, WR, FC, D])
        XN = sb("XN", [P, NT, D])
        rt = Router(g, ctx, "f0_")
        gate, low, loc, slot, keep, gk, t1 = (sb(n, [P, NT]) for n in ("gate", "low", "loc", "slot", "keep", "gk", "t1"))
        put, get = sb("put", [P, NT], U32), sb("get", [P, NT], U32)
        zeros = sb("zeros", [P, 2 * D])
        DI = sb("DI", [P, 2, CB, D])
        DIT = sb("DIT", [P, 2, 2, KD, CAP], F32R)
        h1, h2 = sb("h1", [P, 2, KD, F], F32R), sb("h2", [P, 2, FC, D], F32R)
        l1, l2 = sb("l1", [P, 2, KD, F], F32R), sb("l2", [P, 2, FC, D], F32R)
        HT = sb("HT", [P, 2, 2, FC, CAP], F32R)
        EO = sb("EO", [P, 2, CB, D])
        rows_in = nc.dram_tensor("f0_rows_in", (E * CAP, D), F32).ap()
        rows_out = nc.dram_tensor("f0_rows_out", (E * CAP, D), F32).ap()

        ln = LayerNorm(g, ctx, "f0_ln", g.X, XN, g.XT, PS[0:4], stats=g.x_stats)
        chain, wg_loaded = sem("chain"), sem("wg_loaded")
        w_loaded = [sem(f"w_loaded{i}") for i in range(WR)]
        zeroed, cleared = sem("zeroed"), sem("cleared")
        slots_ready, scattered = sem("slots_ready"), sem("scattered")
        di_loaded = [sem(f"di_loaded{i}") for i in range(2)]
        dtp_ready, dit_ready = sem("dtp_ready"), sem("dit_ready")
        h_ready, ht_ready, eo_ready, eo_copied = sem("h_ready"), sem("ht_ready"), sem("eo_ready"), sem("eo_copied")
        stored = [sem(f"stored{i}") for i in range(2)]
        gathered = [sem(f"gathered{i}") for i in range(NT // 4)]
        wh_ready, wl_ready, ditl_ready, hth_ready = sem("wh_ready"), sem("wl_ready"), sem("ditl_ready"), sem("hth_ready")
        added = sem("added")

        with nc.Block() as block:
            @block.sync
            def _(sp):
                sp.dma_start(rt.wg[:, :, :], a["f0_wg"]).then_inc(wg_loaded, 16)

                def load_weights(e):
                    if e >= WR:
                        sp.wait_ge(wl_ready, 2 * (e - WR + 1))
                    sp.dma_start(w1[:, e % WR, :, :], a["f0_w1"][e]).then_inc(w_loaded[e % WR], 16)
                    sp.dma_start(w2[:, e % WR, :, :], a["f0_w2"][e]).then_inc(w_loaded[e % WR], 16)
                sp.wait_ge(zeroed, 1)
                for q in range(E * CAP * D // (P * 2 * D)):
                    sp.dma_start(rows_in[q * 2 * P:(q + 1) * 2 * P, :].rearrange("(p r) d -> p (r d)", r=2),
                                 zeros[:, :]).then_inc(cleared, 16)
                for e in range(WR):
                    load_weights(e)
                sp.wait_ge(scattered, 16 * NT)
                for e in range(E):
                    if e >= 2:
                        sp.wait_ge(dtp_ready, CB * (e - 1))
                    sp.dma_start(DI[:, e % 2, :, :], rows_in[e * CAP:(e + 1) * CAP, :].rearrange("(s p) d -> p s d", p=P)).then_inc(
                        di_loaded[e % 2], 16)
                    if e >= 1:
                        if e - 1 + WR < E:
                            load_weights(e - 1 + WR)
                        sp.wait_ge(eo_copied, CB * e)
                        sp.dma_start(rows_out[(e - 1) * CAP:e * CAP, :].rearrange("(s p) d -> p s d", p=P),
                                     EO[:, (e - 1) % 2, :, :]).then_inc(stored[(e - 1) % 2], 16)
                sp.wait_ge(eo_copied, CB * E)
                sp.dma_start(rows_out[(E - 1) * CAP:E * CAP, :].rearrange("(s p) d -> p s d", p=P),
                             EO[:, (E - 1) % 2, :, :]).then_inc(stored[(E - 1) % 2], 16)
                for s in stored:
                    sp.wait_ge(s, 16 * E // 2)

            @block.gpsimd
            def _(pool):
                pool.memset(zeros[:, :], 0.0).then_inc(zeroed, 1)
                rt.pool(pool)

                def low_weights(e):
                    for q, (w, h, l) in enumerate(((w1, h1, l1), (w2, h2, l2))):
                        pool.wait_ge(wh_ready, 2 * e + q + 1)
                        pool.tensor_tensor(l[:, e % 2, :, :], w[:, e % WR, :, :], h[:, e % 2, :, :].bitcast(F32),
                                           ALU.subtract).then_inc(wl_ready, 1)
                        pool.wait_ge(wl_ready, 2 * e + q + 1)
                low_weights(0)
                pool.wait_ge(slots_ready, 1)
                pool.wait_ge(cleared, 16 * (E * CAP // (2 * P)))
                for t in range(NT):
                    pool.indirect_dma_start(out=rows_in, out_offset=bass.IndirectOffsetOnAxis(ap=put[:, t:t + 1], axis=0),
                                            in_=XN[:, t, :], in_offset=None, bounds_check=E * CAP - 1,
                                            oob_is_err=False).then_inc(scattered, 16)
                for e in range(1, E):
                    low_weights(e)
                for s in stored:
                    pool.wait_ge(s, 16 * E // 2)
                pool.wait_ge(scattered, 16 * NT)
                for t in range(NT):
                    pool.indirect_dma_start(out=XN[:, t, :], out_offset=None, in_=rows_out,
                                            in_offset=bass.IndirectOffsetOnAxis(ap=get[:, t:t + 1], axis=0),
                                            bounds_check=E * CAP - 1, oob_is_err=False).then_inc(gathered[t // 4], 16)

            @block.tensor
            def _(pe):
                ln.pe(pe)
                pe.wait_ge(wg_loaded, 16)
                rt.pe_logits(pe, ln)
                rt.pe_counts(pe)
                hk = 0
                for e in range(E):
                    pe.wait_ge(di_loaded[e % 2], 16 * (e // 2 + 1))
                    for s in range(CB):
                        if CB * e + s >= 2:
                            pe.wait_ge(ditl_ready, CB * e + s - 1)
                        for k in range(KD):
                            ins = pe.transpose(PS[s][:, k * P:(k + 1) * P], DI[:, e % 2, s, k * P:(k + 1) * P], g.ident[:, :])
                        ins.then_inc(dtp_ready, 1)
                    pe.wait_ge(wl_ready, 2 * e + 1)
                    pe.wait_ge(ditl_ready, CB * (e + 1))
                    for f in range(FC):
                        if hk >= 3:
                            pe.wait_ge(ht_ready, hk - 2)
                        for kd in range(KD):
                            ins = products(pe, PS[2 + hk % 3][:, 0:CAP], h1[:, e % 2, kd, f * P:(f + 1) * P],
                                           l1[:, e % 2, kd, f * P:(f + 1) * P],
                                           DIT[:, 0, e % 2, kd, :], DIT[:, 1, e % 2, kd, :], kd == 0, kd == KD - 1)
                        ins.then_inc(h_ready, 1)
                        hk += 1
                    pe.wait_ge(wl_ready, 2 * e + 2)
                    pe.wait_ge(ht_ready, FC * (e + 1))
                    for s in range(CB):
                        if e >= 1:
                            pe.wait_ge(eo_copied, CB * (e - 1) + s + 1)
                        for f in range(FC):
                            ins = products(pe, PS[5 + s][:, 0:D], HT[:, 0, e % 2, f, s * P:(s + 1) * P], HT[:, 1, e % 2, f, s * P:(s + 1) * P],
                                           h2[:, e % 2, f, :], l2[:, e % 2, f, :], f == 0, f == FC - 1)
                        ins.then_inc(eo_ready, 1)

            @block.scalar
            def _(act):

                def high_weights(e):
                    act.wait_ge(w_loaded[e % WR], 32 * (e // WR + 1))
                    act.activation(h1[:, e % 2, :, :], w1[:, e % WR, :, :], ACT.Copy).then_inc(wh_ready, 1)
                    act.activation(h2[:, e % 2, :, :], w2[:, e % WR, :, :], ACT.Copy).then_inc(wh_ready, 1)
                ln.act(act)
                high_weights(0)
                act.wait_ge(rt.exp_in, 1)
                act.activation(rt.EX[:, :, :], rt.L[:, :, :], ACT.Exp).then_inc(rt.exp_out, 1)
                for e in range(E):
                    for s in range(CB):
                        act.wait_ge(dtp_ready, CB * e + s + 1)
                        act.activation(DIT[:, 0, e % 2, :, s * P:(s + 1) * P], PS[s][:, 0:D].rearrange("p (k n) -> p k n", k=KD),
                                       ACT.Copy).then_inc(dit_ready, 1)
                    for f in range(FC):
                        act.wait_ge(h_ready, FC * e + f + 1)
                        act.activation(HT[:, 0, e % 2, f, :], PS[2 + (FC * e + f) % 3][:, 0:CAP], ACT.Relu).then_inc(hth_ready, 1)
                    if e + 1 < E:
                        high_weights(e + 1)
                    for s in range(CB):
                        act.wait_ge(eo_ready, CB * e + s + 1)
                        if e >= 2 and s == 0:
                            act.wait_ge(stored[e % 2], 16 * (e // 2))
                        act.activation(EO[:, e % 2, s, :], PS[5 + s][:, 0:D], ACT.Copy).then_inc(eo_copied, 1)

            @block.vector
            def _(dve):
                ch = Chain(dve, chain)
                ln.dve(dve)
                dve.wait_ge(rt.const, 3)
                dve.wait_ge(rt.logits_ready, 1)
                lg = PS[4][:, 0:NTE].rearrange("p (t e) -> p t e", e=E)
                ch(dve.tensor_reduce(t1[:, :], lg, AX_X, ALU.max))
                dve.tensor_tensor(rt.L[:, :, :], lg, rt.wide(t1[:, :]), ALU.subtract).then_inc(rt.exp_in, 1)
                dve.wait_ge(rt.exp_in, 1)
                ch(dve.tensor_scalar(rt.A2[:, :, :], rt.L[:, :, :], 0.0, None, ALU.is_equal))
                rt.dve_first(dve, ch, rt.A2[:, :, :], rt.OH[:, :, :], low[:, :])
                dve.wait_ge(rt.exp_out, 1)
                ch(dve.tensor_reduce(t1[:, :], rt.EX[:, :, :], AX_X, ALU.add))
                ch(dve.reciprocal(gate[:, :], t1[:, :]))
                rt.dve_places(dve, ch)
                ch(dve.tensor_tensor(rt.A1[:, :, :], rt.PL[:, :, :], rt.OH[:, :, :], ALU.mult))
                ch(dve.tensor_reduce(loc[:, :], rt.A1[:, :, :], AX_X, ALU.add))
                ch(dve.tensor_scalar(keep[:, :], loc[:, :], float(CAP), None, ALU.is_lt))
                ch(dve.scalar_tensor_tensor(slot[:, :], low[:, :], float(CAP), loc[:, :], ALU.mult, ALU.add))
                ch(dve.tensor_scalar(t1[:, :], keep[:, :], -BIG, BIG + float(E * CAP), ALU.mult, ALU.add))
                ch(dve.tensor_tensor(put[:, :], slot[:, :], t1[:, :], ALU.add))
                ch(dve.tensor_scalar(get[:, :], slot[:, :], float(E * CAP), float(E * CAP - 1), ALU.add, ALU.min))
                ch(dve.tensor_tensor(gk[:, :], gate[:, :], keep[:, :], ALU.mult))
                dve.sem_inc(slots_ready, 1)
                for e in range(E):
                    for s in range(CB):
                        dve.wait_ge(dit_ready, CB * e + s + 1)
                        rows = slice(s * P, (s + 1) * P)
                        dve.tensor_tensor(DIT[:, 1, e % 2, :, rows], PS[s][:, 0:D].rearrange("p (k n) -> p k n", k=KD),
                                          DIT[:, 0, e % 2, :, rows].bitcast(F32), ALU.subtract).then_inc(ditl_ready, 1)
                    for f in range(FC):
                        dve.wait_ge(hth_ready, FC * e + f + 1)
                        dve.scalar_tensor_tensor(HT[:, 1, e % 2, f, :], PS[2 + (FC * e + f) % 3][:, 0:CAP], 0.0,
                                                 HT[:, 0, e % 2, f, :].bitcast(F32), ALU.max, ALU.subtract).then_inc(ht_ready, 1)
                for t in range(NT):
                    if t % 4 == 0:
                        dve.wait_ge(gathered[t // 4], 16 * 4)
                    dve.scalar_tensor_tensor(g.X[:, t, :], XN[:, t, :], gk[:, t:t + 1], g.X[:, t, :], ALU.mult, ALU.add).then_inc(added, 1)
                    g.keep_stats(dve, g.stats, g.X, added, t)
                g.keep_stats(dve, g.stats, g.X, added, NT)
    g.x_stats = g.stats


MB = 2 * T // P + E - 1


def ffn1(g, a):
    nc, PS = g.nc, g.PS
    I32 = mybir.dt.int32
    with ExitStack() as ctx:
        sb = lambda n, s, dt=F32: ctx.enter_context(nc.sbuf_tensor("f1_" + n, s, dt))
        sem = g.semaphores("f1_")
        WSZ = 2 * KD * F + FC * D
        PART = WSZ // 3
        W = sb("W", [P, 4 * WSZ], F32R)
        stage = sb("stage", [P, 3, PART])
        XN = sb("XN", [P, NT, D])
        rt = Router(g, ctx, "f1_")
        OH1, OH2, AB, MK = (sb(n, [P, NT, E]) for n in ("OH1", "OH2", "AB", "MK"))
        m1, m2, low, mult1, mult2, t1 = (sb(n, [P, NT]) for n in ("m1", "m2", "low", "mult1", "mult2", "t1"))
        idx = [sb(f"idx{i}", [P, NT], U32) for i in range(2)]
        nb, start, ends = (sb(n, [P, E]) for n in ("nb", "start", "ends"))
        nbi = sb("nbi", [P, E], I32)
        blk = sb("blk", [P, MB])
        cmp = sb("cmp", [P, MB, E])
        tab = sb("tab", [P, 3, MB + 1])
        tabi = sb("tabi", [P, 3, MB + 1], I32)
        zeros = sb("zeros", [P, 3 * D])
        DI = sb("DI", [P, 3, D])
        DIT = sb("DIT", [P, 2, 2, KD, P], F32R)
        HT = sb("HT", [P, 2, 2, FC, P], F32R)
        SG, HH = (XN[:, 8 * q:8 * q + 8, :].rearrange("p t d -> p (t d)").rearrange("p (u f) -> p u f", f=F) for q in range(2))
        EO = sb("EO", [P, 2, D])
        GR = W[:, 0:2 * NT * D].bitcast(F32).rearrange("p (t q d) -> p t q d", q=2, d=D)
        rows_in = nc.dram_tensor("f1_rows_in", (MB * P, D), F32).ap()
        rows_out = nc.dram_tensor("f1_rows_out", (MB * P, D), F32).ap()

        ln = LayerNorm(g, ctx, "f1_ln", g.X, XN, g.XT, PS[0:4], stats=g.x_stats)
        chain, wg_loaded, w_loaded = sem("chain"), sem("wg_loaded"), [sem(f"w_loaded{i}") for i in range(3)]
        zeroed, cleared, consts = sem("zeroed"), sem("cleared"), sem("consts")
        slots_ready, scattered = sem("slots_ready"), sem("scattered")
        di_loaded = [sem(f"di_loaded{i}") for i in range(3)]
        dtp_ready, dit_ready = sem("dtp_ready"), sem("dit_ready")
        h1_ready, h3_ready, sg_ready, hh_ready = sem("h1_ready"), sem("h3_ready"), sem("sg_ready"), sem("hh_ready")
        htp_ready, ht_ready, eo_ready, eo_copied = sem("htp_ready"), sem("ht_ready"), sem("eo_ready"), sem("eo_copied")
        stored = [sem(f"stored{i}") for i in range(2)]
        gathered = [sem(f"gathered{i}") for i in range(NT // 4)]
        hi_ready, lo_ready, ditl_ready, htl_ready = sem("hi_ready"), sem("lo_ready"), sem("ditl_ready"), sem("htl_ready")
        added, room_free, out_stored = sem("added"), sem("room_free"), sem("out_stored")

        WPARTS = ("f1_w1", "f1_w3", "f1_w2")

        with nc.Block() as block:
            @block.sync
            def _(sp):
                sp.dma_start(rt.wg[:, :, :], a["f1_wg"]).then_inc(wg_loaded, 16)
                sp.wait_ge(zeroed, 1)
                for q in range(MB // 3):
                    sp.dma_start(rows_in[q * 3 * P:(q + 1) * 3 * P, :].rearrange("(p r) d -> p (r d)", r=3),
                                 zeros[:, :]).then_inc(cleared, 16)
                sp.wait_ge(scattered, 16 * 2 * NT)
                LAG = 4
                for k in range(MB + LAG):
                    if k < MB:
                        if k >= 3:
                            sp.wait_ge(dtp_ready, k - 2)
                        sp.dma_start(DI[:, k % 3, :], rows_in[k * P:(k + 1) * P, :]).then_inc(di_loaded[k % 3], 16)
                    if k >= LAG:
                        o = k - LAG
                        sp.wait_ge(eo_copied, o + 1)
                        sp.dma_start(rows_out[o * P:(o + 1) * P, :], EO[:, o % 2, :]).then_inc(stored[o % 2], 16)
                for n in range(2):
                    sp.wait_ge(stored[n], 16 * ((MB + 1 - n) // 2))
                for j in range(NT // 4):
                    sp.wait_ge(added, 8 * (j + 1))
                    sp.dma_start(g.out[:, 4 * j:4 * j + 4, :], g.X[:, 4 * j:4 * j + 4, :]).then_inc(out_stored, 16)
                sp.wait_ge(out_stored, 16 * (NT // 4))

            @block.gpsimd
            def _(pool):
                pool.memset(zeros[:, :], 0.0).then_inc(zeroed, 1)
                rt.pool(pool)
                pool.iota(blk[:, :], pattern=[[1, MB]], base=0, channel_multiplier=0,
                          allow_small_or_imprecise_dtypes=True).then_inc(consts, 1)

                def load(p):
                    if p < 3 * E:
                        pool.dma_start(stage[:, p % 3, :], a[WPARTS[p % 3]][p // 3]).then_inc(w_loaded[p % 3], 16)

                def split(e):
                    for q in range(3):
                        p = 3 * e + q
                        hi = W[:, (e % 2) * 2 * WSZ + q * PART:(e % 2) * 2 * WSZ + (q + 1) * PART]
                        lo = W[:, (e % 2) * 2 * WSZ + WSZ + q * PART:(e % 2) * 2 * WSZ + WSZ + (q + 1) * PART]
                        pool.wait_ge(w_loaded[q], 16 * (e + 1))
                        pool.tensor_tensor(hi, stage[:, q, :], zeros[:, 0:1].to_broadcast([P, PART]), ALU.add).then_inc(hi_ready, 1)
                        pool.wait_ge(hi_ready, p + 1)
                        pool.tensor_tensor(lo, stage[:, q, :], hi.bitcast(F32), ALU.subtract).then_inc(lo_ready, 1)
                        pool.wait_ge(lo_ready, p + 1)
                        load(p + 3)
                for p in range(3):
                    load(p)
                pool.wait_ge(zeroed, 1)
                split(0)
                pool.wait_ge(slots_ready, 1)
                pool.wait_ge(cleared, 16 * (MB // 3))
                for t in range(NT):
                    for q in range(2):
                        pool.indirect_dma_start(out=rows_in, out_offset=bass.IndirectOffsetOnAxis(ap=idx[q][:, t:t + 1], axis=0),
                                                in_=XN[:, t, :], in_offset=None, bounds_check=MB * P - 1,
                                                oob_is_err=False).then_inc(scattered, 16)
                split(1)
                for e in range(2, E):
                    last = pool.value_load(tabi[0:1, 2, e - 2:e - 1], min_val=0, max_val=MB)
                    pool.wait_ge(eo_ready, last + 1)
                    pool.sem_inc(room_free, 1)
                    pool.wait_ge(room_free, e - 1)
                    split(e)
                pool.wait_ge(eo_ready, MB + 1)
                for n in range(2):
                    pool.wait_ge(stored[n], 16 * ((MB + 1 - n) // 2))
                for t in range(NT):
                    for q in range(2):
                        pool.indirect_dma_start(out=GR[:, t, q, :], out_offset=None, in_=rows_out,
                                                in_offset=bass.IndirectOffsetOnAxis(ap=idx[q][:, t:t + 1], axis=0),
                                                bounds_check=MB * P - 1, oob_is_err=False).then_inc(gathered[t // 4], 16)

            @block.tensor
            def _(pe):
                ln.pe(pe)
                pe.wait_ge(wg_loaded, 16)
                rt.pe_logits(pe, ln)
                rt.pe_counts(pe)

                def take_rows(k):
                    pe.wait_ge(di_loaded[k % 3], 16 * (k // 3 + 1))
                    if k >= 1:
                        pe.wait_ge(ditl_ready, k)
                    for kd in range(KD):
                        ins = pe.transpose(PS[6][:, kd * P:(kd + 1) * P], DI[:, k % 3, kd * P:(kd + 1) * P], g.ident[:, :])
                    ins.then_inc(dtp_ready, 1)

                def up(k):
                    ex = pe.value_load(tabi[0:1, 0, k:k + 1], min_val=0, max_val=E - 1)
                    room = pe.value_load(tabi[0:1, 1, k:k + 1], min_val=0, max_val=2 * WSZ)
                    pe.wait_ge(lo_ready, ex * 3 + 2)
                    pe.wait_ge(ditl_ready, k + 1)
                    for w, ready, used in ((0, h1_ready, sg_ready), (1, h3_ready, hh_ready)):
                        if k >= 1:
                            pe.wait_ge(used, k)
                        for hf in range(2):
                            for kd in range(KD):
                                at = room + (w * KD * F + kd * F + hf * 512)
                                ins = products(pe, PS[2 * w + hf][:, :], DIT[:, 0, k % 2, kd, :], DIT[:, 1, k % 2, kd, :],
                                               W[:, ds(at, 512)], W[:, ds(at + WSZ, 512)], kd == 0, kd == KD - 1)
                        ins.then_inc(ready, 1)
                    return ex, room

                def turn(k):
                    pe.wait_ge(hh_ready, k + 1)
                    if k >= 1:
                        pe.wait_ge(htl_ready, 2 * k)
                    for hf in range(2):
                        for c in range(4):
                            f = 4 * hf + c
                            ins = pe.transpose(PS[7 if hf else 4][:, c * P:(c + 1) * P], HH[:, k % 2, f * P:(f + 1) * P], g.ident[:, :])
                        ins.then_inc(htp_ready, 1)

                def down(k, ex, room):
                    pe.wait_ge(lo_ready, ex * 3 + 3)
                    pe.wait_ge(htl_ready, 2 * k + 2)
                    if k >= 1:
                        pe.wait_ge(eo_copied, k)
                    for f in range(FC):
                        at = room + (2 * KD * F + f * D)
                        ins = products(pe, PS[5][:, 0:D], HT[:, 0, k % 2, f, :], HT[:, 1, k % 2, f, :],
                                       W[:, ds(at, D)], W[:, ds(at + WSZ, D)], f == 0, f == FC - 1)
                    ins.then_inc(eo_ready, 1)

                pe.wait_ge(slots_ready, 1)
                pe.sem_inc(eo_ready, 1)
                take_rows(0)
                for k in range(MB + 1):
                    if k >= 1:
                        turn(k - 1)
                    if k + 1 < MB:
                        take_rows(k + 1)
                    if k < MB:
                        now = up(k)
                    if k >= 1:
                        down(k - 1, *before)
                    before = now

            @block.scalar
            def _(act):
                ln.act(act)
                for q in range(2):
                    act.wait_ge(rt.exp_in, q + 1)
                    act.activation(rt.EX[:, :, :], rt.L[:, :, :], ACT.Exp).then_inc(rt.exp_out, 1)

                def rows(k):
                    act.wait_ge(dtp_ready, k + 1)
                    act.activation(DIT[:, 0, k % 2, :, :], PS[6][:, 0:D].rearrange("p (k n) -> p k n", k=KD), ACT.Copy).then_inc(dit_ready, 1)
                rows(0)
                for k in range(MB + 1):
                    if k >= 1:
                        for hf in range(2):
                            act.wait_ge(htp_ready, 2 * (k - 1) + hf + 1)
                            act.activation(HT[:, 0, (k - 1) % 2, 4 * hf:4 * hf + 4, :], PS[7 if hf else 4][:, :].rearrange("p (c n) -> p c n", c=4),
                                           ACT.Copy).then_inc(ht_ready, 1)
                    if k + 1 < MB:
                        rows(k + 1)
                    if k < MB:
                        act.wait_ge(h1_ready, k + 1)
                        act.activation(SG[:, k % 2, :].rearrange("p (h f) -> p h f", h=2), g.ps[:, 0:2, :], ACT.Silu).then_inc(sg_ready, 1)
                    if k >= 1:
                        act.wait_ge(eo_ready, k + 1)
                        if k >= 3:
                            act.wait_ge(stored[(k - 1) % 2], 16 * ((k - 1) // 2))
                        act.activation(EO[:, (k - 1) % 2, :], PS[5][:, 0:D], ACT.Copy).then_inc(eo_copied, 1)

            @block.vector
            def _(dve):
                ch = Chain(dve, chain)
                ln.dve(dve)
                dve.wait_ge(rt.const, 3)
                dve.wait_ge(rt.logits_ready, 1)
                v3 = lambda x: x[:, :, :]
                lg = PS[4][:, 0:NTE].rearrange("p (t e) -> p t e", e=E)
                ch(dve.tensor_copy(v3(rt.PL), lg))
                ch(dve.tensor_scalar(v3(AB), v3(rt.PL), -1.0, None, ALU.mult))
                ch(dve.tensor_tensor(v3(AB), v3(AB), v3(rt.PL), ALU.max))
                ch(dve.tensor_reduce(m1[:, :], v3(rt.PL), AX_X, ALU.max))

                def weight(m, banned, out, q):
                    ch(dve.tensor_tensor(v3(rt.A2), v3(AB), rt.wide(m), ALU.max))
                    if q:
                        ch(dve.tensor_tensor(v3(rt.L), v3(rt.PL), rt.wide(m), ALU.subtract))
                        ch(dve.tensor_scalar(v3(rt.L), v3(rt.L), 0.0, None, ALU.min))
                        dve.sem_inc(rt.exp_in, 1)
                    else:
                        dve.tensor_tensor(v3(rt.L), v3(rt.PL), rt.wide(m), ALU.subtract).then_inc(rt.exp_in, 1)
                        dve.wait_ge(rt.exp_in, 1)
                    ch(dve.scalar_tensor_tensor(v3(rt.A1), v3(rt.A2), 0.02, v3(rt.L), ALU.mult, ALU.add))
                    ch(dve.tensor_scalar(v3(MK), v3(rt.A1), 0.0, None, ALU.is_ge))
                    if banned is not None:
                        ch(dve.tensor_tensor(v3(rt.A1), v3(MK), banned, ALU.mult))
                        ch(dve.tensor_tensor(v3(MK), v3(MK), v3(rt.A1), ALU.subtract))
                    dve.wait_ge(rt.exp_out, q + 1)
                    ch(dve.tensor_tensor(v3(rt.A1), v3(rt.EX), v3(MK), ALU.mult))
                    ch(dve.tensor_reduce(t1[:, :], v3(rt.A1), AX_X, ALU.add))
                    ch(dve.reciprocal(out, t1[:, :]))

                weight(m1[:, :], None, mult1[:, :], 0)
                ch(dve.tensor_tensor(v3(rt.A2), v3(rt.PL), rt.wide(m1[:, :]), ALU.is_equal))
                rt.dve_first(dve, ch, v3(rt.A2), v3(OH1), low[:, :])
                ch(dve.tensor_scalar(v3(rt.A2), v3(OH1), -3.0e38, None, ALU.mult))
                ch(dve.tensor_tensor(v3(rt.A2), v3(rt.PL), v3(rt.A2), ALU.add))
                ch(dve.tensor_reduce(m2[:, :], v3(rt.A2), AX_X, ALU.max))
                ch(dve.tensor_tensor(v3(rt.A2), v3(rt.A2), rt.wide(m2[:, :]), ALU.is_equal))
                rt.dve_first(dve, ch, v3(rt.A2), v3(OH2), low[:, :])
                weight(m2[:, :], v3(OH1), mult2[:, :], 1)
                ch(dve.tensor_tensor(v3(rt.OH), v3(OH1), v3(OH2), ALU.add))
                rt.dve_places(dve, ch)
                ch(dve.tensor_scalar(nbi[:, :], rt.CUM[:, :, NT - 1], float(P - 1), None, ALU.add))
                ch(dve.tensor_scalar(nbi[:, :], nbi[:, :], 7, None, ALU.arith_shift_right))
                ch(dve.tensor_copy(nb[:, :], nbi[:, :]))
                ch(dve.tensor_tensor_scan(ends[:, :], g.ones[:, 0:E], nb[:, :], 0.0, ALU.mult, ALU.add))
                ch(dve.tensor_tensor(start[:, :], ends[:, :], nb[:, :], ALU.subtract))
                ch(dve.tensor_scalar(start[:, :], start[:, :], float(P), None, ALU.mult))
                ch(dve.tensor_tensor(v3(rt.PL), v3(rt.PL), rt.row(start[:, :]), ALU.add))
                for q, oh in enumerate((OH1, OH2)):
                    ch(dve.tensor_tensor(v3(rt.A1), v3(rt.PL), v3(oh), ALU.mult))
                    ch(dve.tensor_reduce(t1[:, :], v3(rt.A1), AX_X, ALU.add))
                    ch(dve.tensor_copy(idx[q][:, :], t1[:, :]))
                dve.wait_ge(consts, 1)
                ch(dve.tensor_tensor(cmp[:, :, :], blk[:, :].unsqueeze(2).to_broadcast([P, MB, E]),
                                     ends[:, :].unsqueeze(1).to_broadcast([P, MB, E]), ALU.is_ge))
                ch(dve.memset(tab[:, :, :], 0.0))
                ch(dve.tensor_reduce(tab[:, 0, 0:MB], cmp[:, :, :], AX_X, ALU.add))
                ch(dve.tensor_scalar(tab[:, 0, 0:MB], tab[:, 0, 0:MB], float(E - 1), None, ALU.min))
                ch(dve.tensor_copy(tabi[:, 0, :], tab[:, 0, :]))
                ch(dve.tensor_scalar(tabi[:, 1, :], tabi[:, 0, :], 1, None, ALU.bitwise_and))
                ch(dve.tensor_copy(tab[:, 1, :], tabi[:, 1, :]))
                ch(dve.tensor_scalar(tab[:, 1, :], tab[:, 1, :], float(2 * WSZ), None, ALU.mult))
                ch(dve.tensor_copy(tab[:, 2, 0:E], ends[:, :]))
                ch(dve.tensor_copy(tabi[:, 1:3, :], tab[:, 1:3, :]))
                dve.sem_inc(slots_ready, 1)

                def rows_lo(k):
                    dve.wait_ge(dit_ready, k + 1)
                    dve.tensor_tensor(DIT[:, 1, k % 2, :, :], PS[6][:, 0:D].rearrange("p (k n) -> p k n", k=KD),
                                      DIT[:, 0, k % 2, :, :].bitcast(F32), ALU.subtract).then_inc(ditl_ready, 1)
                rows_lo(0)
                for k in range(MB + 1):
                    if k >= 1:
                        for hf in range(2):
                            dve.wait_ge(ht_ready, 2 * (k - 1) + hf + 1)
                            dve.tensor_tensor(HT[:, 1, (k - 1) % 2, 4 * hf:4 * hf + 4, :], PS[7 if hf else 4][:, :].rearrange("p (c n) -> p c n", c=4),
                                              HT[:, 0, (k - 1) % 2, 4 * hf:4 * hf + 4, :].bitcast(F32), ALU.subtract).then_inc(htl_ready, 1)
                    if k + 1 < MB:
                        rows_lo(k + 1)
                    if k < MB:
                        dve.wait_ge(sg_ready, k + 1)
                        dve.wait_ge(h3_ready, k + 1)
                        dve.tensor_tensor(HH[:, k % 2, :].rearrange("p (h f) -> p h f", h=2), SG[:, k % 2, :].rearrange("p (h f) -> p h f", h=2),
                                          g.ps[:, 2:4, :], ALU.mult).then_inc(hh_ready, 1)
                for j in range(NT // 4):
                    dve.wait_ge(gathered[j], 16 * 8)
                    for q, m in enumerate((mult1, mult2)):
                        for t in range(4 * j, 4 * j + 4):
                            if q:
                                dve.wait_ge(added, 8 * j + t % 4 + 1)
                            dve.scalar_tensor_tensor(g.X[:, t, :], GR[:, t, q, :], m[:, t:t + 1], g.X[:, t, :], ALU.mult,
                                                     ALU.add).then_inc(added, 1)


CL = 32
NC = S // CL
PAIRS, HDW = 4, 64
ETA, DT_STEP, FLOOR = 0.1, 0.01, 0.1


def mixer1(g, a):
    nc = g.nc
    with ExitStack() as ctx:
        Hrow = ctx.enter_context(nc.sbuf_tensor("Hrow", [P, NT, D], F32))
        XN = ctx.enter_context(nc.sbuf_tensor("h_XN", [P, NT, D], F32))
        gamma = ctx.enter_context(nc.sbuf_tensor("gamma", [P, NT], F32))
        h_stats = ctx.enter_context(nc.sbuf_tensor("h_stats", [P, NT, 6], F32))
        resolvent(g, a, Hrow, XN, gamma)
        g.end_stage()
        hebbian(g, a, Hrow, XN, gamma, h_stats)
        g.end_stage()
        gelu_ffn(g, a, Hrow, XN, h_stats)
        g.x_stats = g.stats


def resolvent(g, a, Hrow, XN, gamma):
    nc, PS = g.nc, g.PS
    with ExitStack() as ctx:
        sb = lambda n, s, dt=F32: ctx.enter_context(nc.sbuf_tensor("r_" + n, s, dt))
        sem = g.semaphores("r_")
        g1, b1 = sb("g1", [P, KD]), sb("b1", [P, KD])
        w_pot, b_pot = sb("w_pot", [P, KD, 2]), sb("b_pot", [2, 1])
        w_bk = sb("w_bk", [3, D])
        POT = sb("POT", [2, T])
        CH = sb("CH", [P, 2, CL])
        Dn = sb("Dn", [P, 2, CL])
        DD = sb("DD", [P, 2, CL])
        nDi = sb("nDi", [P, CL])
        sp = sb("sp", [P, 5, CL])
        sg = sb("sg", [P, 5, NT])
        GS, NG = 8, CL // 8
        CT = sb("CT", [P, NG, GS + 2, 2, 2])
        tm, mx, rc = sb("tm", [P, 2, 2]), sb("mx", [P, 1]), sb("rc", [P, 1])
        MM = sb("MM", [P, 2, 2, 2])
        Q = sb("Q", [34, NC, 2, 2, 2])
        RM = sb("RM", [34, NC, 2, 2, 2, 2])
        W = sb("W", [34, NC + 1, 4])
        wt, wm, wr = sb("wt", [34, 4, 4]), sb("wm", [34, 1]), sb("wr", [34, 1])
        uu, un, ia, ib = sb("uu", [34, NC, 2]), sb("un", [34, NC]), sb("ia", [34, NC]), sb("ib", [34, NC])
        IA = sb("IA", [34, NC, 2])
        A0 = sb("A0", [P, 2])
        AA = sb("AA", [P, 2, CL])
        B2 = sb("B2", [64, 2, CL])
        nA0 = sb("nA0", [P, 1])
        UK = sb("UK", [P, 2, NG, GS + 2])
        sq, cp, rn, GG = sb("sq", [P, 2, NG, GS]), sb("cp", [P, 2, NG, GS]), sb("rn", [P, NG, GS]), sb("GG", [64, 2, CL])
        s2, sn = sb("s2", [64, 2, CL]), sb("sn", [64, CL])
        GR = sb("GR", [3, T])

        ln0 = LayerNorm(g, ctx, "r_ln0", g.X, Hrow, None, None, stats=g.x_stats)
        ln1 = LayerNorm(g, ctx, "r_ln1", Hrow, XN, g.XT, PS[0:4], g1, b1)
        loaded, chain, act_chain = sem("loaded"), sem("chain"), sem("act_chain")
        pot_ready, pot_copied, ch_loaded = sem("pot_ready"), sem("pot_copied"), sem("ch_loaded")
        potT_ready, abs_in, abs_out = sem("potT_ready"), sem("abs_in"), sem("abs_out")
        ones_ready, mm_ready, q_loaded = sem("ones_ready"), sem("mm_ready"), sem("q_loaded")
        ia_ready, a0_loaded, aa_ready, b2_loaded = sem("ia_ready"), sem("a0_loaded"), sem("aa_ready"), sem("b2_loaded")
        gg_ready, gr_loaded, f_ready, f_used = sem("gg_ready"), sem("gr_loaded"), sem("f_ready"), sem("f_used")
        names = [(g1[:, :], "h_g1"), (b1[:, :], "h_b1"), (w_pot[:, :, :], "h_w_pot"), (b_pot[:, :], "h_b_pot"), (w_bk[:, :], "h_w_bk")]

        with nc.Block() as block:
            @block.sync
            def _(s):
                for dst, name in names:
                    s.dma_start(dst, a[name]).then_inc(loaded, 16)
                s.wait_ge(pot_copied, 4)
                for half in range(2):
                    for r in range(2):
                        s.dma_start(CH[64 * half:64 * half + 64, r, :], POT[r:r + 1, :].rearrange("a (p i) -> a p i", i=CL)).then_inc(ch_loaded, 16)
                s.wait_ge(ones_ready, 2)
                s.wait_ge(mm_ready, 1)
                for half in range(2):
                    for b in range(B):
                        lo = 64 * half + NC * b
                        s.dma_start(Q[32 * half + b:32 * half + b + 1, :, :, :, :].rearrange("a c x y z -> a c (x y z)"),
                                    MM[lo:lo + NC, :, :, :].rearrange("p x y z -> p (x y z)")).then_inc(q_loaded, 16)
                s.wait_ge(ia_ready, 1)
                for half in range(2):
                    for b in range(B):
                        lo = 64 * half + NC * b
                        s.dma_start(A0[lo:lo + NC, :], IA[32 * half + b:32 * half + b + 1, :, :]).then_inc(a0_loaded, 16)
                s.wait_ge(aa_ready, 1)
                s.dma_start(B2[:, :, :], AA[64:128, :, :]).then_inc(b2_loaded, 16)
                s.wait_ge(gg_ready, 1)
                for r in range(2):
                    s.dma_start(GR[r:r + 1, :].rearrange("a (p i) -> a p i", i=CL), GG[:, r, :]).then_inc(gr_loaded, 16)

            @block.gpsimd
            def _(pool):
                pool.memset(GR[:, :], 1.0).then_inc(ones_ready, 1)
                pool.memset(Q[:, :, :, :, :], 0.0).then_inc(ones_ready, 1)

            @block.tensor
            def _(pe):
                ln1.pe(pe)
                pe.wait_ge(loaded, 16 * len(names))
                for j in range(4):
                    pe.wait_ge(ln1.xt_ready, 4 * j + 4)
                    for kd in range(KD):
                        ins = pe.matmul(PS[4 + j][0:2, :], w_pot[:, kd, :], g.XT[:, kd, j * 512:(j + 1) * 512],
                                        start=(kd == 0), stop=(kd == KD - 1))
                    ins.then_inc(pot_ready, 1)
                pe.wait_ge(pot_copied, 4)
                pe.wait_ge(ln1.xt_ready, NT)
                for t in range(NT):
                    ins = pe.transpose(PS[0][:, 2 * t:2 * t + 2], POT[:, t * P:(t + 1) * P], g.ident[0:2, 0:2])
                ins.then_inc(potT_ready, 1)
                pe.wait_ge(gr_loaded, 32)
                for t in range(NT):
                    if t >= 2:
                        pe.wait_ge(f_used, t - 1)
                    pe.matmul(PS[1 + t % 2][:, 0:D], GR[:, t * P:(t + 1) * P], w_bk[:, :], start=True, stop=True).then_inc(f_ready, 1)

            @block.scalar
            def _(act):
                ch = Chain(act, act_chain)
                ln0.act(act)
                act.wait_ge(loaded, 16 * len(names))
                ln1.act(act)
                for j in range(4):
                    act.wait_ge(pot_ready, j + 1)
                    act.activation(POT[:, j * 512:(j + 1) * 512], PS[4 + j][0:2, :], ACT.Identity, bias=b_pot[:, 0:1]).then_inc(pot_copied, 1)
                for q, t in enumerate((sp, sg)):
                    act.wait_ge(abs_in, q + 1)
                    ch(act.activation(t[:, 1, :], t[:, 0, :], ACT.Abs))
                    ch(act.activation(t[:, 2, :], t[:, 1, :], ACT.Exp, scale=-1.0))
                    act.activation(t[:, 3, :], t[:, 2, :], ACT.Ln, bias=1.0).then_inc(abs_out, 1)

            @block.vector
            def _(dve):
                ch = Chain(dve, chain)
                ln0.dve(dve)
                dve.wait_ge(ln0.xn_ready, NT)
                ln1.dve(dve)

                def softplus(t, q, out):
                    dve.sem_inc(abs_in, 1)
                    dve.wait_ge(abs_out, q + 1)
                    ch(dve.tensor_scalar(t[:, 4, :], t[:, 2, :], 1.0, None, ALU.add))
                    ch(dve.scalar_tensor_tensor(t[:, 4, :], t[:, 4, :], 1.0, t[:, 2, :], ALU.subtract, ALU.subtract))
                    ch(dve.tensor_tensor(t[:, 4, :], t[:, 3, :], t[:, 4, :], ALU.subtract))
                    ch(dve.scalar_tensor_tensor(t[:, 4, :], t[:, 0, :], 0.0, t[:, 4, :], ALU.max, ALU.add))
                    ch(dve.tensor_scalar(out, t[:, 4, :], FLOOR, None, ALU.add))

                dve.wait_ge(ch_loaded, 64)
                ch(dve.tensor_copy(sp[:, 0, :], CH[:, 1, :]))
                softplus(sp, 0, nDi[:, :])
                ch.add(dve.tensor_scalar(Dn[:, 0, :], CH[:, 0, :], 2.0, None, ALU.add))
                ch.add(dve.tensor_scalar(Dn[:, 1, :], nDi[:, :], -1.0, None, ALU.mult))
                ch.sync()
                ch.add(dve.tensor_copy(DD[0:64, :, :], Dn[0:64, :, :]))
                ch.add(dve.tensor_copy(DD[64:128, :, :], Dn[64:128, :, ::-1]))
                ch.sync()
                ch(dve.tensor_scalar(nDi[:, :], DD[:, 1, :], -1.0, None, ALU.mult))
                ch(dve.memset(CT[:, :, :, :, :], 0.0))
                ch.add(dve.memset(CT[:, 0, 1, 0, 0:1], 1.0))
                ch.add(dve.memset(CT[:, 0, 0, 0, 1:2], 1.0))
                ch.sync()
                for k in range(CL):
                    j, q = k // GS, k % GS
                    old, cur, new = (CT[:, j, q + e, :, :] for e in range(3))
                    ch(dve.scalar_tensor_tensor(tm[:, :, :], cur, DD[:, 0, k:k + 1], old, ALU.mult, ALU.subtract))
                    ch.add(dve.scalar_tensor_tensor(new[:, 0, :], cur[:, 1, :], nDi[:, k:k + 1], tm[:, 0, :], ALU.mult, ALU.add))
                    ch.add(dve.scalar_tensor_tensor(new[:, 1, :], cur[:, 0, :], DD[:, 1, k:k + 1], tm[:, 1, :], ALU.mult, ALU.add))
                    ch.sync()
                    if q == GS - 1:
                        two = CT[:, j, GS:GS + 2, :, :]
                        ch(dve.tensor_reduce(mx[:, :], two.rearrange("p e c s -> p (e c s)"), AX_X, ALU.max, apply_absolute_value=True))
                        ch(dve.reciprocal(rc[:, :], mx[:, :]))
                        if j + 1 < NG:
                            ch(dve.tensor_scalar(CT[:, j + 1, 0:2, :, :], two, rc[:, 0:1], None, ALU.mult))
                ch.add(dve.tensor_scalar(MM[:, 0, :, :], CT[:, NG - 1, GS + 1, :, :], rc[:, 0:1], None, ALU.mult))
                ch.add(dve.tensor_scalar(MM[:, 1, :, :], CT[:, NG - 1, GS, :, :], rc[:, 0:1], None, ALU.mult))
                ch.sync()
                dve.sem_inc(mm_ready, 1)
                dve.wait_ge(potT_ready, 1)
                ch(dve.tensor_copy(sg[:, 0, :], PS[0][:, 1:2 * NT:2]))
                softplus(sg, 1, gamma[:, :])
                dve.wait_ge(q_loaded, 64)
                dve.wait_ge(ones_ready, 2)
                for lo, hi, rev in ((0, 32, False), (32, 34, True)):
                    src = Q[lo:hi, ::-1] if rev else Q[lo:hi, :]
                    for rr, cc, comp, sign in ((0, 0, 0, 1.0), (0, 1, 1, -1.0), (1, 0, 1, 1.0), (1, 1, 0, 1.0)):
                        for x in range(2):
                            ch.add(dve.tensor_scalar(RM[lo:hi, :, x, rr, :, cc], src[:, :, x, comp, :], sign, None, ALU.mult))
                ch.add(dve.memset(W[:, :, :], 0.0))
                ch.sync()
                ch(dve.memset(W[:, 0, 0:1], 1.0))
                for j in range(NC):
                    ch(dve.tensor_tensor(wt[:, :, :], RM[:, j, :, :, :, :].rearrange("p x r s c -> p (x r) (s c)"),
                                         W[:, j, :].unsqueeze(1).to_broadcast([34, 4, 4]), ALU.mult))
                    ch(dve.tensor_reduce(W[:, j + 1, :], wt[:, :, :], AX_X, ALU.add))
                    if j % 4 == 3:
                        w = W[:, j + 1, :]
                        ch(dve.tensor_reduce(wm[:, :], w, AX_X, ALU.max, apply_absolute_value=True))
                        ch(dve.tensor_scalar(wm[:, :], wm[:, :], 1e-30, None, ALU.max))
                        ch(dve.reciprocal(wr[:, :], wm[:, :]))
                        ch(dve.tensor_scalar(w, w, wr[:, 0:1], None, ALU.mult))
                u, v = W[:, 0:NC, 0:2], W[:, 0:NC, 2:4]
                ch.add(dve.tensor_tensor(uu[:, :, :], u, u, ALU.mult))
                ch.sync()
                ch(dve.tensor_tensor(un[:, :], uu[:, :, 0], uu[:, :, 1], ALU.add))
                ch(dve.tensor_scalar(un[:, :], un[:, :], 1e-37, None, ALU.max))
                ch(dve.reciprocal(un[:, :], un[:, :]))
                for comp, p0, p1, op in ((0, (0, 0), (1, 1), ALU.add), (1, (1, 0), (0, 1), ALU.subtract)):
                    ch.add(dve.tensor_tensor(ia[:, :], v[:, :, p0[0]], u[:, :, p0[1]], ALU.mult))
                    ch.add(dve.tensor_tensor(ib[:, :], v[:, :, p1[0]], u[:, :, p1[1]], ALU.mult))
                    ch.sync()
                    ch(dve.tensor_tensor(ia[:, :], ia[:, :], ib[:, :], op))
                    ch.add(dve.tensor_tensor(IA[0:32, :, comp], ia[0:32, :], un[0:32, :], ALU.mult))
                    ch.add(dve.tensor_tensor(IA[32:34, ::-1, comp], ia[32:34, :], un[32:34, :], ALU.mult))
                    ch.sync()
                dve.sem_inc(ia_ready, 1)
                dve.wait_ge(a0_loaded, 64)
                ch.add(dve.tensor_scalar(nA0[:, :], A0[:, 1:2], -1.0, None, ALU.mult))
                ct = CT[:, :, :, :, :].rearrange("p j q c s -> p c s (j q)")
                uk = UK[:, :, :, :].rearrange("p c j q -> p c (j q)")
                ch.add(dve.scalar_tensor_tensor(uk[:, 1, :], ct[:, 0, 1, :], A0[:, 1:2], ct[:, 1, 0, :], ALU.mult, ALU.add))
                ch.sync()
                ch.add(dve.scalar_tensor_tensor(uk[:, 0, :], ct[:, 1, 1, :], nA0[:, 0:1], ct[:, 0, 0, :], ALU.mult, ALU.add))
                ch.add(dve.scalar_tensor_tensor(uk[:, 1, :], ct[:, 1, 1, :], A0[:, 0:1], uk[:, 1, :], ALU.mult, ALU.add))
                ch.sync()
                ch(dve.scalar_tensor_tensor(uk[:, 0, :], ct[:, 0, 1, :], A0[:, 0:1], uk[:, 0, :], ALU.mult, ALU.add))
                last, this = UK[:, :, :, 1:GS + 1], UK[:, :, :, 2:GS + 2]
                ch.add(dve.tensor_tensor(sq[:, :, :, :], last, last, ALU.mult))
                ch.add(dve.tensor_tensor(cp[:, :, :, :], this, last, ALU.mult))
                ch.sync()
                aa = AA[:, :, :].rearrange("p c (j q) -> p c j q", q=GS)
                ch.add(dve.tensor_tensor(rn[:, :, :], sq[:, 0, :, :], sq[:, 1, :, :], ALU.add))
                ch.add(dve.tensor_tensor(aa[:, 0, :, :], cp[:, 0, :, :], cp[:, 1, :, :], ALU.add))
                ch.sync()
                ch.add(dve.reciprocal(rn[:, :, :], rn[:, :, :]))
                ch.add(dve.tensor_tensor(cp[:, 0, :, :], this[:, 1, :, :], last[:, 0, :, :], ALU.mult))
                ch.add(dve.tensor_tensor(cp[:, 1, :, :], this[:, 0, :, :], last[:, 1, :, :], ALU.mult))
                ch.sync()
                ch(dve.tensor_tensor(aa[:, 1, :, :], cp[:, 0, :, :], cp[:, 1, :, :], ALU.subtract))
                ch(dve.tensor_tensor(aa, aa, rn[:, :, :].unsqueeze(1).to_broadcast([P, 2, NG, GS]), ALU.mult))
                dve.sem_inc(aa_ready, 1)
                dve.wait_ge(b2_loaded, 16)
                ch(dve.tensor_tensor(s2[:, :, :], AA[0:64, :, :], B2[:, :, ::-1], ALU.add))
                ch(dve.tensor_tensor(s2[:, :, :], s2[:, :, :], Dn[0:64, :, :], ALU.subtract))
                ch(dve.tensor_tensor(GG[:, :, :], s2[:, :, :], s2[:, :, :], ALU.mult))
                ch(dve.tensor_tensor(sn[:, :], GG[:, 0, :], GG[:, 1, :], ALU.add))
                ch(dve.reciprocal(sn[:, :], sn[:, :]))
                ch.add(dve.tensor_tensor(GG[:, 0, :], s2[:, 0, :], sn[:, :], ALU.mult))
                ch.add(dve.scalar_tensor_tensor(GG[:, 1, :], s2[:, 1, :], -1.0, sn[:, :], ALU.mult, ALU.mult))
                ch.sync()
                dve.sem_inc(gg_ready, 1)
                for t in range(NT):
                    dve.wait_ge(f_ready, t + 1)
                    dve.tensor_tensor(Hrow[:, t, :], Hrow[:, t, :], PS[1 + t % 2][:, 0:D], ALU.add).then_inc(f_used, 1)


def hebbian(g, a, Hrow, XN, gamma, h_stats):
    nc, PS, ps = g.nc, g.PS, g.ps
    NP = PAIRS
    with ExitStack() as ctx:
        sb = lambda n, s, dt=F32: ctx.enter_context(nc.sbuf_tensor("h_" + n, s, dt))
        sem = g.semaphores("h_")
        g2, b2 = sb("g2", [P, KD]), sb("b2", [P, KD])
        h_qkv, h_out = sb("h_qkv", [P, KD, 3 * NP * P], F32R), sb("h_out", [P, NP, D], F32R)
        l_qkv, l_out = sb("l_qkv", [P, KD, 3 * NP * P], F32R), sb("l_out", [P, NP, D], F32R)
        b_qk, b_v, b_out = sb("b_qk", [P, 2 * NP]), sb("b_v", [P, NP * P]), sb("b_out", [P, D])
        blockd = sb("blockd", [P, P])
        Lc, Lt = sb("Lc", [P, NT]), sb("Lt", [P, NT])
        EB = sb("EB", [P, NT, P])
        DM = sb("DM", [P, NT, P])
        ks, dec = sb("ks", [P, NT]), sb("dec", [P, NT])
        QK = sb("QK", [P, 2, 2 * NP, 512])
        room = QK[:, :, :, :].rearrange("p s f n -> p (s f n)")
        w_qkv = room[:, 0:KD * 3 * NP * P].rearrange("p (k n) -> p k n", k=KD)
        w_out = room[:, KD * 3 * NP * P:KD * 3 * NP * P + NP * D].rearrange("p (q d) -> p q d", q=NP)
        VV, KS = (XN[:, 4 * i:4 * i + 4, :].rearrange("p t d -> p (t d)").rearrange("p (s n) -> p s n", s=2) for i in range(2))
        PTm = XN[:, 8:16, :].rearrange("p t d -> p (t d)").rearrange("p (s h n) -> p s h n", s=2, n=P)
        VP = sb("VP", [P, 2, 2 * NP, P])
        QS = sb("QS", [P, 2, NP, P])
        HB = sb("HB", [P, 2, 2, NP, P], F32R)
        WS = sb("WS", [P, NP, P])
        KVm = sb("KVm", [P, NP, P])
        ln = LayerNorm(g, ctx, "h_ln", Hrow, XN, g.XT, PS[0:4], g2, b2, split=True)
        loaded, chain, consts = sem("loaded"), sem("chain"), sem("consts")
        lc_ready, lc_copied, lb_ready, lb_used, dm_in, dm_out, eb_ready = (
            sem(n) for n in ("lc_ready", "lc_copied", "lb_ready", "lb_used", "dm_in", "dm_out", "eb_ready"))
        bo_added, ws_clear = sem("bo_added"), sem("ws_clear")
        qk_ready, qk_used, v_ready, vv_ready, vp_ready = (sem(n) for n in ("qk_ready", "qk_used", "v_ready", "vv_ready", "vp_ready"))
        kt_ready, ks_ready, s_ready, pt_ready, qs_ready = (sem(n) for n in ("kt_ready", "ks_ready", "s_ready", "pt_ready", "qs_ready"))
        o_ready, hb_ready, kv_ready, ws_ready, y_ready, y_used = (
            sem(n) for n in ("o_ready", "hb_ready", "kv_ready", "ws_ready", "y_ready", "y_used"))
        wh_ready, wl_ready, hbl_ready = sem("wh_ready"), sem("wl_ready"), sem("hbl_ready")
        names = [(g2[:, :], "h_g2"), (b2[:, :], "h_b2"), (w_qkv, "h_w_qkv"), (w_out, "h_w_out"),
                 (b_qk[:, :], "h_b_qk"), (b_v[:, :], "h_b_v"), (b_out[:, :], "h_b_out")]
        ALL = 16 * len(names)
        GT = 4

        with nc.Block() as block:
            @block.sync
            def _(s):
                for dst, name in names:
                    src = a[name]
                    if src.shape[0] == 1:
                        src = src.to_broadcast([P, src.shape[1]])
                    s.dma_start(dst, src).then_inc(loaded, 16)

            @block.gpsimd
            def _(pool):
                pool.memset(blockd[:, :], 0.0).then_inc(consts, 1)
                pool.memset(VP[:, :, :, :], 0.0).then_inc(consts, 1)
                pool.wait_ge(consts, 2)
                pool.memset(blockd[0:HDW, 0:HDW], 1.0).then_inc(consts, 1)
                pool.wait_ge(consts, 3)
                pool.memset(blockd[HDW:P, HDW:P], 1.0).then_inc(consts, 1)
                pool.wait_ge(consts, 4)
                pool.wait_ge(loaded, ALL)
                for q, (w, h, l) in enumerate(((w_qkv, h_qkv, l_qkv), (w_out, h_out, l_out))):
                    pool.wait_ge(wh_ready, q + 1)
                    pool.tensor_tensor(l[:, :, :], w, h[:, :, :].bitcast(F32), ALU.subtract).then_inc(wl_ready, 1)
                    pool.wait_ge(wl_ready, q + 1)
                for t in range(NT):
                    pool.wait_ge(ln.xn_ready, t + 1)
                    pool.tensor_tensor(Hrow[:, t, :], Hrow[:, t, :], b_out[:, :], ALU.add).then_inc(bo_added, 1)
                for t in range(NT):
                    r = t % 2
                    pool.wait_ge(vv_ready, t + 1)
                    if t >= 2:
                        pool.wait_ge(o_ready, t - 1)
                    v = VV[:, r, :].rearrange("p (q h e) -> p q h e", h=2, e=HDW)
                    vp = VP[:, r, :, :].rearrange("p (q h) e -> p q h e", h=2)
                    pool.tensor_copy(vp[:, :, 0, 0:HDW], v[:, :, 0, :]).then_inc(vp_ready, 1)
                    pool.tensor_copy(vp[:, :, 1, HDW:P], v[:, :, 1, :]).then_inc(vp_ready, 1)
                    pool.wait_ge(qk_used, 8 * (t // GT + 1))
                    pool.wait_ge(eb_ready, 4)
                    tt = t % GT
                    pool.tensor_tensor(QS[:, r, :, :], QK[:, (t // GT) % 2, 0:NP, tt * P:(tt + 1) * P],
                                       EB[:, t:t + 1, :].to_broadcast([P, NP, P]), ALU.mult).then_inc(qs_ready, 1)

            @block.tensor
            def _(pe):
                ln.pe(pe)
                pe.matmul(PS[4][:, 0:NT], g.upper[:, :], gamma[:, :], start=True, stop=True).then_inc(lc_ready, 1)
                pe.matmul(PS[5][:, 0:NT], g.ones[:, :], gamma[:, :], start=True, stop=True).then_inc(lc_ready, 1)
                for j in range(4):
                    if j >= 2:
                        pe.wait_ge(lb_used, j - 1)
                    for c in range(4):
                        t = 4 * j + c
                        ins = pe.matmul(PS[6 + j % 2][:, c * P:(c + 1) * P], gamma[:, t:t + 1].to_broadcast([P, P]), g.upper[:, :],
                                        start=True, stop=True)
                    ins.then_inc(lb_ready, 1)
                pe.wait_ge(wl_ready, 2)

                def group(j):
                    pe.wait_ge(ln.xt_ready, GT * (j + 1) if j else NT)
                    pe.wait_ge(ln.lo_ready, GT * (j + 1))
                    for f in range(2 * NP):
                        n = 8 * j + f
                        if n >= 2:
                            pe.wait_ge(qk_used, n - 1)
                        for kd in range(KD):
                            ins = products(pe, PS[n % 2][:, :], h_qkv[:, kd, f * P:(f + 1) * P], l_qkv[:, kd, f * P:(f + 1) * P],
                                           ln.hi[:, kd, j * 512:(j + 1) * 512], ln.lo[:, kd, j * 512:(j + 1) * 512],
                                           kd == 0, kd == KD - 1)
                        ins.then_inc(qk_ready, 1)

                def values(t):
                    if t >= 1:
                        pe.wait_ge(vv_ready, t)
                    for kd in range(KD):
                        ins = products(pe, PS[2][:, :], ln.hi[:, kd, t * P:(t + 1) * P], ln.lo[:, kd, t * P:(t + 1) * P],
                                       h_qkv[:, kd, 2 * NP * P:3 * NP * P], l_qkv[:, kd, 2 * NP * P:3 * NP * P],
                                       kd == 0, kd == KD - 1)
                    ins.then_inc(v_ready, 1)

                def project(t):
                    pe.wait_ge(hbl_ready, t + 1)
                    pe.wait_ge(ks_ready, min(t + 2, NT))
                    if t == NT - 1:
                        pe.wait_ge(y_used, t)
                    for q in range(NP):
                        ins = products(pe, PS[3][:, 0:D], HB[:, 0, t % 2, q, :], HB[:, 1, t % 2, q, :], h_out[:, q, :], l_out[:, q, :],
                                       q == 0, q == NP - 1)
                    ins.then_inc(y_ready, 1)

                def scores(t):
                    r, tt = (t // GT) % 2, t % GT
                    pe.wait_ge(qk_used, 8 * (t // GT + 1))
                    if t >= 1:
                        pe.wait_ge(pt_ready, t)
                    else:
                        pe.wait_ge(lc_copied, 2)
                    for h in range(2 * NP):
                        q, lo = h // 2, HDW * (h % 2)
                        ins = pe.matmul(PS[4 + h % 2][:, q * P:(q + 1) * P], QK[lo:lo + HDW, r, NP + q, tt * P:(tt + 1) * P],
                                        QK[lo:lo + HDW, r, q, tt * P:(tt + 1) * P], start=True, stop=True)
                    ins.then_inc(s_ready, 1)

                def keys(t):
                    r, tt = (t // GT) % 2, t % GT
                    if t >= 1:
                        pe.wait_ge(ks_ready, t)
                    if t >= 2:
                        pe.wait_ge(y_used, t - 1)
                    for q in range(NP):
                        ins = pe.transpose(PS[3][:, q * P:(q + 1) * P], QK[:, r, NP + q, tt * P:(tt + 1) * P], g.ident[:, :])
                    ins.then_inc(kt_ready, 1)

                def read_out(t):
                    r = t % 2
                    pe.wait_ge(pt_ready, t + 1)
                    pe.wait_ge(vp_ready, 2 * (t + 1))
                    pe.wait_ge(qs_ready, t + 1)
                    if t >= 1:
                        pe.wait_ge(hbl_ready, t)
                        pe.wait_ge(ws_ready, t)
                    else:
                        pe.wait_ge(lb_used, 4)
                        pe.wait_ge(consts, 4)
                        pe.wait_ge(ws_clear, 1)
                    for q in range(NP):
                        out = PS[6][:, q * P:(q + 1) * P]
                        for h in range(2):
                            pe.matmul(out, VP[:, r, 2 * q + h, :], PTm[:, r, h * NP + q, :], start=(h == 0), stop=False)
                        ins = pe.matmul(out, WS[:, q, :], QS[:, r, q, :], start=False, stop=True)
                    ins.then_inc(o_ready, 1)
                    pe.wait_ge(ks_ready, t + 1)
                    for q in range(NP):
                        ins = pe.matmul(PS[7][:, q * P:(q + 1) * P], KS[:, r, q * P:(q + 1) * P], VV[:, r, q * P:(q + 1) * P],
                                        start=True, stop=True)
                    ins.then_inc(kv_ready, 1)

                for t in range(NT + 2):
                    if t < NT and t % GT == 0:
                        group(t // GT)
                    if t < NT:
                        values(t)
                    if t >= 2:
                        project(t - 2)
                    if t < NT:
                        scores(t)
                        keys(t)
                    if 1 <= t <= NT:
                        read_out(t - 1)

            @block.scalar
            def _(act):
                ln.act_std(act)
                act.wait_ge(loaded, ALL)
                act.activation(h_qkv[:, :, :], w_qkv, ACT.Copy).then_inc(wh_ready, 1)
                act.activation(h_out[:, :, :], w_out, ACT.Copy).then_inc(wh_ready, 1)
                ln.act_transposed(act)
                for q, (dst, bank) in enumerate(((Lc, 4), (Lt, 5))):
                    act.wait_ge(lc_ready, q + 1)
                    act.activation(dst[:, :], PS[bank][:, 0:NT], ACT.Copy).then_inc(lc_copied, 1)
                for j in range(4):
                    act.wait_ge(lb_ready, j + 1)
                    act.activation(EB[:, 4 * j:4 * j + 4, :], PS[6 + j % 2][:, :].rearrange("p (t n) -> p t n", n=P), ACT.Exp,
                                   scale=-DT_STEP).then_inc(eb_ready, 1)
                act.wait_ge(dm_in, 1)
                act.activation(DM[:, :, :], DM[:, :, :], ACT.Exp, scale=-DT_STEP)
                act.activation(ks[:, :], ks[:, :], ACT.Exp, scale=-DT_STEP)
                act.activation(dec[:, :], Lt[:, :], ACT.Exp, scale=-DT_STEP).then_inc(dm_out, 1)
                for t in range(NT + 1):
                    if t < NT and t % GT == 0:
                        for f in range(2 * NP):
                            n = 8 * (t // GT) + f
                            act.wait_ge(qk_ready, n + 1)
                            act.activation(QK[:, (t // GT) % 2, f, :], PS[n % 2][:, :], ACT.Identity, bias=b_qk[:, f:f + 1]).then_inc(qk_used, 1)
                    if t < NT:
                        act.wait_ge(kt_ready, t + 1)
                        if t == 0:
                            act.wait_ge(dm_out, 2)
                        if t >= 2:
                            act.wait_ge(kv_ready, t - 1)
                        act.activation(KS[:, t % 2, :], PS[3][:, :], ACT.Copy, scale=ks[:, t:t + 1]).then_inc(ks_ready, 1)
                    if t >= 1:
                        act.wait_ge(o_ready, t)
                        if t >= 3:
                            act.wait_ge(y_ready, t - 2)
                        act.activation(HB[:, 0, (t - 1) % 2, :, :], PS[6][:, :].rearrange("p (q n) -> p q n", n=P), ACT.Copy).then_inc(hb_ready, 1)

            @block.vector
            def _(dve):
                ch = Chain(dve, chain)
                ln.dve(dve)
                dve.wait_ge(lc_copied, 2)
                for j in range(4):
                    dve.wait_ge(eb_ready, j + 1)
                    for c in range(4):
                        t = 4 * j + c
                        ins = dve.tensor_scalar(DM[:, t, :], PS[6 + j % 2][:, c * P:(c + 1) * P], Lc[:, t:t + 1], 0.0,
                                                ALU.subtract, ALU.max)
                    ins.then_inc(lb_used, 1)
                dve.tensor_tensor(ks[:, :], Lt[:, :], Lc[:, :], ALU.subtract).then_inc(dm_in, 1)
                dve.wait_ge(dm_out, 1)
                ch.add(dve.tensor_scalar(ks[:, :], ks[:, :], ETA, None, ALU.mult))
                ch.add(dve.tensor_scalar(DM[:, :, :], DM[:, :, :], ETA, None, ALU.mult))
                ch.sync()
                ch(dve.tensor_tensor(DM[:, :, :], DM[:, :, :], g.upper[:, :].unsqueeze(1).to_broadcast([P, NT, P]), ALU.mult))
                dve.sem_inc(dm_out, 1)
                dve.memset(WS[:, :, :], 0.0).then_inc(ws_clear, 1)
                dve.wait_ge(consts, 4)
                dve.wait_ge(ws_clear, 1)
                dve.wait_ge(loaded, ALL)

                def values(t):
                    dve.wait_ge(v_ready, t + 1)
                    if t >= 2:
                        dve.wait_ge(kv_ready, t - 1)
                        dve.wait_ge(vp_ready, 2 * (t - 1))
                    dve.tensor_tensor(VV[:, t % 2, :], PS[2][:, :], b_v[:, :], ALU.add).then_inc(vv_ready, 1)

                def masked(t):
                    dve.wait_ge(s_ready, t + 1)
                    if t >= 2:
                        dve.wait_ge(o_ready, t - 1)
                    dve.tensor_tensor(PTm[:, t % 2, :, :], ps[:, 4:6, :].rearrange("p b (h n) -> p (b h) n", n=P),
                                      DM[:, t:t + 1, :].to_broadcast([P, 2 * NP, P]), ALU.mult).then_inc(pt_ready, 1)

                def update(t):
                    dve.wait_ge(hb_ready, t + 1)
                    if t >= 2:
                        dve.wait_ge(y_ready, t - 1)
                    dve.tensor_tensor(HB[:, 1, t % 2, :, :], PS[6][:, :].rearrange("p (q n) -> p q n", n=P),
                                      HB[:, 0, t % 2, :, :].bitcast(F32), ALU.subtract).then_inc(hbl_ready, 1)
                    dve.wait_ge(kv_ready, t + 1)
                    dve.wait_ge(o_ready, t + 1)
                    if t % TB == TB - 1:
                        dve.memset(WS[:, :, :], 0.0).then_inc(ws_ready, 1)
                    else:
                        ch(dve.tensor_tensor(KVm[:, :, :], PS[7][:, :].rearrange("p (q n) -> p q n", n=P),
                                             blockd[:, :].unsqueeze(1).to_broadcast([P, NP, P]), ALU.mult))
                        dve.scalar_tensor_tensor(WS[:, :, :], WS[:, :, :], dec[:, t:t + 1], KVm[:, :, :], ALU.mult, ALU.add).then_inc(ws_ready, 1)
                    dve.wait_ge(ws_ready, t + 1)

                def add_out(t):
                    dve.wait_ge(y_ready, t + 1)
                    dve.tensor_tensor(Hrow[:, t, :], Hrow[:, t, :], PS[3][:, 0:D], ALU.add).then_inc(y_used, 1)
                    g.keep_stats(dve, h_stats, Hrow, y_used, t)

                dve.wait_ge(bo_added, NT)
                for t in range(NT + 2):
                    if t < NT:
                        values(t)
                    if t >= 2:
                        add_out(t - 2)
                    if t < NT:
                        masked(t)
                    if 1 <= t <= NT:
                        update(t - 1)
                g.keep_stats(dve, h_stats, Hrow, y_used, NT)


def gelu_ffn(g, a, Hrow, XN, h_stats):
    nc, PS = g.nc, g.PS
    with ExitStack() as ctx:
        sb = lambda n, s, dt=F32: ctx.enter_context(nc.sbuf_tensor("g_" + n, s, dt))
        sem = g.semaphores("g_")
        g3, b3 = sb("g3", [P, KD]), sb("b3", [P, KD])
        w1, w2 = sb("w1", [P, KD, F]), sb("w2", [P, FC, D])
        bf1, bf2 = sb("bf1", [P, FC]), sb("bf2", [P, D])
        h1, h2 = sb("h1", [P, KD, F], F32R), sb("h2", [P, FC, D], F32R)
        l1, l2 = sb("l1", [P, KD, F], F32R), sb("l2", [P, FC, D], F32R)
        GN = 256
        GT, NG = GN // P, T // GN
        GF = sb("GF", [P, 2, GN])
        GH, GL = sb("GH", [P, 2, FC, GN], F32R), sb("GL", [P, 2, FC, GN], F32R)
        ln = LayerNorm(g, ctx, "g_ln", Hrow, XN, g.XT, PS[0:4], g3, b3, split=True, stats=h_stats)
        loaded, sums = sem("loaded"), sem("sums")
        h_ready, y_ready, y_used = sem("h_ready"), sem("y_ready"), sem("y_used")
        wh_ready, wl_ready, gf_ready, gh_ready, gl_ready = (sem(n) for n in ("wh_ready", "wl_ready", "gf_ready", "gh_ready", "gl_ready"))
        names = [(g3[:, :], "h_g3"), (b3[:, :], "h_b3"), (w1[:, :, :], "h_w_ff1"), (w2[:, :, :], "h_w_ff2"),
                 (bf1[:, :], "h_b_ff1"), (bf2[:, :], "h_b_ff2")]
        ALL = 16 * len(names)
        with nc.Block() as block:
            @block.sync
            def _(s):
                for dst, name in names:
                    src = a[name]
                    if src.shape[0] == 1:
                        src = src.to_broadcast([P, src.shape[1]])
                    s.dma_start(dst, src).then_inc(loaded, 16)

            @block.gpsimd
            def _(pool):
                for q, (w, h, l) in enumerate(((w1, h1, l1), (w2, h2, l2))):
                    pool.wait_ge(wh_ready, q + 1)
                    pool.tensor_tensor(l[:, :, :], w[:, :, :], h[:, :, :].bitcast(F32), ALU.subtract).then_inc(wl_ready, 1)
                    pool.wait_ge(wl_ready, q + 1)
                for t in range(NT):
                    pool.tensor_tensor(g.X[:, t, :], g.X[:, t, :], bf2[:, :], ALU.add).then_inc(sums, 1)
                for t in range(NT):
                    pool.wait_ge(sums, NT + t)
                    pool.tensor_tensor(g.X[:, t, :], g.X[:, t, :], Hrow[:, t, :], ALU.add).then_inc(sums, 1)

            @block.tensor
            def _(pe):
                ln.pe(pe)

                def up(j):
                    pe.wait_ge(wl_ready, 1)
                    pe.wait_ge(ln.lo_ready, GT * (j + 1))
                    for f in range(FC):
                        n = FC * j + f
                        if n >= 4:
                            pe.wait_ge(gf_ready, n - 3)
                        for kd in range(KD):
                            cols = slice(j * GN, (j + 1) * GN)
                            ins = products(pe, PS[n % 4][:, 0:GN], h1[:, kd, f * P:(f + 1) * P], l1[:, kd, f * P:(f + 1) * P],
                                           ln.hi[:, kd, cols], ln.lo[:, kd, cols], kd == 0, kd == KD - 1)
                        ins.then_inc(h_ready, 1)

                def down(j):
                    pe.wait_ge(wl_ready, 2)
                    pe.wait_ge(gl_ready, FC * (j + 1))
                    for c in range(GT):
                        t = GT * j + c
                        if t >= 4:
                            pe.wait_ge(y_used, t - 3)
                        for f in range(FC):
                            ins = products(pe, PS[4 + t % 4][:, 0:D], GH[:, j % 2, f, c * P:(c + 1) * P], GL[:, j % 2, f, c * P:(c + 1) * P],
                                           h2[:, f, :], l2[:, f, :], f == 0, f == FC - 1)
                        ins.then_inc(y_ready, 1)
                pe.wait_ge(ln.xt_ready, NT)
                up(0)
                for j in range(NG):
                    if j + 1 < NG:
                        up(j + 1)
                    down(j)

            @block.scalar
            def _(act):
                ln.act_std(act)
                act.wait_ge(loaded, ALL)
                act.activation(h1[:, :, :], w1[:, :, :], ACT.Copy).then_inc(wh_ready, 1)
                act.activation(h2[:, :, :], w2[:, :, :], ACT.Copy).then_inc(wh_ready, 1)
                ln.act_transposed(act)
                for n in range(NG * FC):
                    j, f = n // FC, n % FC
                    act.wait_ge(h_ready, n + 1)
                    if j >= 2:
                        act.wait_ge(y_ready, GT * (j - 1))
                    if n >= 2:
                        act.wait_ge(gl_ready, n - 1)
                    act.activation(GF[:, n % 2, :], PS[n % 4][:, 0:GN], ACT.Gelu_apprx_tanh, bias=bf1[:, f:f + 1]).then_inc(gf_ready, 1)
                    act.wait_ge(gf_ready, n + 1)
                    act.activation(GH[:, j % 2, f, :], GF[:, n % 2, :], ACT.Copy).then_inc(gh_ready, 1)

            @block.vector
            def _(dve):
                ln.dve(dve)

                def low(j):
                    for n in range(FC * j, FC * (j + 1)):
                        dve.wait_ge(gh_ready, n + 1)
                        dve.tensor_tensor(GL[:, j % 2, n % FC, :], GF[:, n % 2, :], GH[:, j % 2, n % FC, :].bitcast(F32),
                                          ALU.subtract).then_inc(gl_ready, 1)
                low(0)
                for j in range(NG):
                    if j + 1 < NG:
                        low(j + 1)
                    dve.wait_ge(sums, 2 * NT)
                    for t in range(GT * j, GT * (j + 1)):
                        dve.wait_ge(y_ready, t + 1)
                        dve.tensor_tensor(g.X[:, t, :], g.X[:, t, :], PS[4 + t % 4][:, 0:D], ALU.add).then_inc(y_used, 1)
                        g.keep_stats(dve, g.stats, g.X, y_used, t)
                g.keep_stats(dve, g.stats, g.X, y_used, NT)


STAGES = [mamba, xattn0, ffn0, mixer1, xattn1, ffn1]


def build(nc, a, out, which=range(6)):
    g = G(nc)
    g.out = out
    with ExitStack() as ctx:
        setup(g, ctx, a)
        g.end_stage()
        for stage in [STAGES[w] for w in which]:
            stage(g, a)
            if stage is ffn1:
                return
            g.end_stage()
        with nc.semaphore("stored") as stored, nc.Block() as block:
            @block.sync
            def _(sp):
                sp.dma_start(out, g.X[:, :, :]).then_inc(stored, 16)
                sp.wait_ge(stored, 16)


def lay_out(i):
    import numpy as np
    c = np.ascontiguousarray
    def rows(w):
        return c(w.reshape(-1, P, w.shape[1]).transpose(1, 0, 2))
    def cols(v):
        return c(v.reshape(-1, P).T)
    xp = i["L0_attn_x_proj_w"]
    bc = xp[R:]
    d = {
        "x": c(i["x"].reshape(NT, P, D).transpose(1, 0, 2)),
        "m_w_in": rows(i["L0_attn_in_proj_w"].T),
        "m_w_x": rows(np.concatenate([bc, bc, bc, xp[:R]]).T),
        "m_w_dt": c(i["L0_attn_dt_proj_w"].T),
        "m_w_out": rows(i["L0_attn_out_proj_w"].T),
        "m_conv_w": c(i["L0_attn_conv_w"].reshape(CI, P, DC).transpose(1, 0, 2)),
        "m_conv_b": cols(i["L0_attn_conv_b"]),
        "m_dt_b": cols(i["L0_attn_dt_proj_b"]),
        "m_skip": cols(i["L0_attn_D"]),
        "m_A_log": rows(i["L0_attn_A_log"]),
    }
    ctxT = i["ctx_1024"].reshape(B * SK, KD, P).transpose(2, 1, 0)
    d["ctxT"] = c(ctxT)
    d["dist"] = c(i["fside_BxSxS2_0"].reshape(NT, P, SK).transpose(1, 0, 2))
    d["scaling"] = c(i["L0_xattn_distance_scaling"].reshape(1, 1))
    for pre, lay, t in (("a0_", "L0_xattn_", True), ("a1_", "L1_xattn_", False)):
        for n in "qkvo":
            w = i[lay + "W" + n]
            d[pre + "w" + n] = rows(w.T if t else w)
        d[pre + "bq"], d[pre + "bk"] = cols(i[lay + "bq"]), cols(i[lay + "bk"])
        d[pre + "bv"], d[pre + "bo"] = c(i[lay + "bv"][None]), c(i[lay + "bo"][None])
    def experts(w):
        return c(w.reshape(E, -1, P, w.shape[2]).transpose(0, 2, 1, 3))
    d["f0_wg"] = rows(i["L0_ffn_wg"])
    d["f0_w1"], d["f0_w2"] = experts(i["L0_ffn_w1"]), experts(i["L0_ffn_w2"])
    d["f1_wg"] = rows(i["L1_ffn_gate_w"].T)
    for n in ("w1", "w2", "w3"):
        w = experts(i["L1_ffn_" + n].transpose(0, 2, 1))
        d["f1_" + n] = w.reshape(E, P, -1)
    lay = "L1_attn_"
    for n in "123":
        d["h_g" + n], d["h_b" + n] = cols(i[lay + f"ln{n}_g"]), cols(i[lay + f"ln{n}_b"])
    d["h_w_pot"], d["h_b_pot"] = rows(i[lay + "w_pot"]), c(i[lay + "b_pot"][:, None])
    d["h_w_bk"] = np.concatenate([i[lay + "w_bk"], i[lay + "b_bk"][None]])
    d["h_w_qkv"], d["h_w_out"] = rows(i[lay + "w_qkv"]), rows(i[lay + "w_out"])
    bq = i[lay + "b_qkv"]
    d["h_b_qk"], d["h_b_v"] = cols(bq[:1024]), c(bq[1024:][None])
    d["h_b_out"] = c(i[lay + "b_out"][None])
    d["h_w_ff1"], d["h_w_ff2"] = rows(i[lay + "w_ff1"]), rows(i[lay + "w_ff2"])
    d["h_b_ff1"], d["h_b_ff2"] = cols(i[lay + "b_ff1"]), c(i[lay + "b_ff2"][None])
    return d


def make(nc, d, which=range(6)):
    a = {n: nc.dram_tensor("in_" + n, v.shape, mybir.dt.from_np(v.dtype), kind="ExternalInput").ap() for n, v in d.items()}
    out = nc.dram_tensor("out_rows", (P, NT, D), F32, kind="ExternalOutput").ap()
    build(nc, a, out, which)


def kernel(**inputs):
    import numpy as np
    import concourse.bacc as bacc
    from concourse.bass_utils import run_bass_kernel_spmd

    d = lay_out({n: np.asarray(v) for n, v in inputs.items()})
    nc = bacc.Bacc("TRN2", target_bir_lowering=False, num_devices=1)
    make(nc, d)
    r = run_bass_kernel_spmd(nc, [{"in_" + n: v for n, v in d.items()}], core_ids=[0])
    rows = r.results[0]["out_rows"]
    return np.ascontiguousarray(rows.transpose(1, 0, 2)).reshape(B, S, D)
```
